# Optimizing a Trainium2 kernel written in Bass

```python
import numpy as np
import jax
import jax.numpy as jnp

def _softmax(x, axis=-1):
    return jax.nn.softmax(x, axis=axis)

def _gelu(x):
    return jax.nn.gelu(x, approximate=True)

def _silu(x):
    return jax.nn.silu(x)

def _sigmoid(x):
    return jax.nn.sigmoid(x)

def _layernorm(x, axis=-1, eps=1e-05):
    m = jnp.mean(x, axis=axis, keepdims=True)
    v = jnp.var(x, axis=axis, keepdims=True)
    return (x - m) / jnp.sqrt(v + eps)

def _scatter_add(tgt, idx, src, axis=0):
    return tgt.at[idx].add(src)

def _segment_sum(src, seg, n):
    return jax.ops.segment_sum(src, seg, n)
kernel_name = 'mk_adj_resnorm_d2_adj_r2_3b7705'

def setup_inputs(seed: int=0):
    np.random.seed(seed)
    _w = jnp.asarray

    def _rec_inputs():
        import jax
        import jax.numpy as jnp
        _gk = jax.random.key(seed)
        x = -0.0002928 + 1 * jax.random.normal(jax.random.fold_in(_gk, 1), (4096, 256), jnp.float32)
        _a = jax.random.bernoulli(jax.random.fold_in(_gk, 2), 0.000488281, (4096, 4096))
        _a = jnp.logical_or(_a, jnp.swapaxes(_a, -1, -2))
        _a = jnp.logical_or(_a, jnp.eye(4096, dtype=bool))
        adj = _a.astype(jnp.int32)
        return (x, adj)
    x, adj = _rec_inputs()

    def _L0_gnn_setup():
        import jax, jax.numpy as jnp
        import numpy as np
        N, D_IN, D_OUT = (4096, 256, 256)
        key = jax.random.key(seed)
        ks = jax.random.split(key, 8)
        scale_in = 1.0 / np.sqrt(D_IN)
        scale_cat = 1.0 / np.sqrt(2 * D_OUT)
        return {'x': jax.random.normal(ks[0], (N, D_IN), dtype=jnp.float32), 'adj': jax.random.randint(ks[1], (N, N), 0, 2, dtype=jnp.int32), 'W_self': jax.random.uniform(ks[2], (D_IN, D_OUT), jnp.float32, -scale_in, scale_in), 'b_self': jax.random.uniform(ks[3], (D_OUT,), jnp.float32, -scale_in, scale_in), 'W_nb': jax.random.uniform(ks[4], (D_IN, D_OUT), jnp.float32, -scale_in, scale_in), 'b_nb': jax.random.uniform(ks[5], (D_OUT,), jnp.float32, -scale_in, scale_in), 'W_comb': jax.random.uniform(ks[6], (2 * D_OUT, D_OUT), jnp.float32, -scale_cat, scale_cat), 'b_comb': jax.random.uniform(ks[7], (D_OUT,), jnp.float32, -scale_cat, scale_cat)}
    _L0_gnn_all = _L0_gnn_setup()
    _L0_gnn_in = {k: v for k, v in _L0_gnn_all.items() if k in ('W_self', 'b_self', 'W_nb', 'b_nb', 'W_comb', 'b_comb')}
    del _L0_gnn_all

    def _L1_gnn_setup():
        import jax, jax.numpy as jnp
        import numpy as np
        N = 2048
        IN_FEAT = 256
        EMBED = 256
        HEADS = 8
        HEAD_DIM = EMBED // HEADS
        SCALING = HEAD_DIM ** (-0.5)
        key = jax.random.key(seed)
        ks = jax.random.split(key, 7)
        x = jax.random.normal(ks[0], (N, IN_FEAT), dtype=jnp.float32)
        adj = jax.random.randint(ks[1], (N, N), 0, 2, dtype=jnp.int32)
        s = 0.04
        WQ = jax.random.normal(ks[2], (EMBED, IN_FEAT), dtype=jnp.float32) * s
        WK = jax.random.normal(ks[3], (EMBED, IN_FEAT), dtype=jnp.float32) * s
        WV = jax.random.normal(ks[4], (EMBED, IN_FEAT), dtype=jnp.float32) * s
        we = jax.random.normal(ks[5], (1, HEAD_DIM), dtype=jnp.float32) * 0.1
        be = jnp.zeros((1,), dtype=jnp.float32)
        return {'x': x, 'adj': adj, 'WQ': WQ, 'WK': WK, 'WV': WV, 'we': we, 'be': be}
    _L1_gnn_all = _L1_gnn_setup()
    _L1_gnn_in = {k: v for k, v in _L1_gnn_all.items() if k in ('WQ', 'WK', 'WV', 'we', 'be')}
    del _L1_gnn_all
    return {'x': x, 'adj': adj, 'L0_gnn_W_self': _L0_gnn_in['W_self'], 'L0_gnn_b_self': _L0_gnn_in['b_self'], 'L0_gnn_W_nb': _L0_gnn_in['W_nb'], 'L0_gnn_b_nb': _L0_gnn_in['b_nb'], 'L0_gnn_W_comb': _L0_gnn_in['W_comb'], 'L0_gnn_b_comb': _L0_gnn_in['b_comb'], 'L1_gnn_WQ': _L1_gnn_in['WQ'], 'L1_gnn_WK': _L1_gnn_in['WK'], 'L1_gnn_WV': _L1_gnn_in['WV'], 'L1_gnn_we': _L1_gnn_in['we'], 'L1_gnn_be': _L1_gnn_in['be']}

def reference(x, adj, L0_gnn_W_self, L0_gnn_b_self, L0_gnn_W_nb, L0_gnn_b_nb, L0_gnn_W_comb, L0_gnn_b_comb, L1_gnn_WQ, L1_gnn_WK, L1_gnn_WV, L1_gnn_we, L1_gnn_be):
    import jax
    import jax.numpy as jnp

    def _L0_gnn_ref(x, adj, W_self, b_self, W_nb, b_nb, W_comb, b_comb):
        import jax, jax.numpy as jnp
        import numpy as np
        N, D_IN, D_OUT = (4096, 256, 256)
        mask = (adj > 0).astype(x.dtype)
        deg = jnp.sum(mask, axis=1, keepdims=True)
        agg = mask @ x / jnp.maximum(deg, 1.0)
        self_f = x @ W_self + b_self
        nb_f = agg @ W_nb + b_nb
        combined = jnp.concatenate([self_f, nb_f], axis=-1)
        out = combined @ W_comb + b_comb
        return jax.nn.relu(out)

    def _L1_gnn_ref(x, adj, WQ, WK, WV, we, be):
        import jax, jax.numpy as jnp
        import numpy as np
        N = 2048
        IN_FEAT = 256
        EMBED = 256
        HEADS = 8
        HEAD_DIM = EMBED // HEADS
        SCALING = HEAD_DIM ** (-0.5)
        n = x.shape[0]
        Q = (x @ WQ.T).reshape(n, HEADS, HEAD_DIM).transpose(1, 0, 2)
        K = (x @ WK.T).reshape(n, HEADS, HEAD_DIM).transpose(1, 0, 2)
        V = (x @ WV.T).reshape(n, HEADS, HEAD_DIM).transpose(1, 0, 2)
        energy = Q @ we.T + be
        attn = jnp.einsum('hqd,hkd->hqk', Q, K) * SCALING + energy
        attn = attn + jnp.where(adj > 0, 0.0, -jnp.inf)
        attn = jax.nn.softmax(attn, axis=-1)
        hard = (attn == jnp.max(attn, axis=-1, keepdims=True)).astype(jnp.float32) / HEADS
        out = jnp.einsum('hqk,hkd->hqd', hard, V)
        return out.transpose(1, 0, 2).reshape(n, EMBED)
    x = _layernorm(x + _L0_gnn_ref(x, adj, L0_gnn_W_self, L0_gnn_b_self, L0_gnn_W_nb, L0_gnn_b_nb, L0_gnn_W_comb, L0_gnn_b_comb), axis=-1)
    x = _layernorm(x + _L1_gnn_ref(x, adj, L1_gnn_WQ, L1_gnn_WK, L1_gnn_WV, L1_gnn_we, L1_gnn_be), axis=-1)
    return x

_drawn_inputs = setup_inputs


def setup_inputs(seed=0):
    import zlib

    import numpy as np

    out = dict(_drawn_inputs(seed))
    spreads = {}
    factors = {'L0_gnn_b_self': 4.718, 'L0_gnn_b_nb': 4.036, 'L0_gnn_b_comb': 2.672}
    for name, (base, spread) in spreads.items():
        noise = np.random.default_rng([zlib.crc32(name.encode()), seed]).standard_normal(out[name].shape)
        drawn = base * np.exp(spread * noise) if base else spread * noise
        out[name] = jnp.asarray(drawn.astype(out[name].dtype))
    for name, factor in factors.items():
        out[name] = (out[name] * factor).astype(out[name].dtype)
    return out
```

```python
from contextlib import ExitStack

import concourse.bass as bass
from concourse import mybir

ALU = mybir.AluOpType
ACT = mybir.ActivationFunctionType
F32 = mybir.dt.float32
I32 = mybir.dt.int32
BF16 = mybir.dt.bfloat16
AX_X = mybir.AxisListType.X

P = 128
N = 4096
D = 256
HEADS = 8
HD = D // HEADS
TILES = N // P
KC = D // P
SCALING = HD ** -0.5
EPS = 1e-5
BIG = 1e30


def gnn_kernel(nc, x, adj, W_self, b_self, W_nb, b_nb, W_comb, b_comb, WQ, WK, WV, we, be, out):
    ctx = ExitStack()
    with ctx:
        def sb(name, shape, dt=F32):
            return ctx.enter_context(nc.sbuf_tensor(name, shape, dt))

        def sem(name):
            return ctx.enter_context(nc.semaphore(name))

        def dram(name, shape, dt=F32):
            return nc.dram_tensor(name, shape, dt, kind="Internal").ap()

        bank = [ctx.enter_context(nc.psum_tensor(f"bank{i}", [P, 512], F32)) for i in range(8)]

        agg_d = dram("agg_d", [N, D])
        x1_d = dram("x1_d", [N, D])
        qT_d = dram("qT_d", [D, N])
        kT_d = dram("kT_d", [D, N])
        v_d = dram("v_d", [N, D])
        att_d = dram("att_d", [N, D])

        ident = sb("ident", [P, P])
        identb = sb("identb", [P, P], BF16)
        ones = sb("ones", [1, P])
        w_raw = sb("w_raw", [P, 5, KC, D])
        w_comb = sb("w_comb", [P, 2 * KC, D])
        b_col = sb("b_col", [P, 2, KC])
        bc_row = sb("bc_row", [1, D])
        w_t = sb("w_t", [P, 5, KC, D])
        w_fused = sb("w_fused", [P, 2 * KC, D])
        b_fused = sb("b_fused", [1, D])
        we_col = sb("we_col", [HD, 1])
        be_col = sb("be_col", [P, 1])

        s_const = sem("s_const")
        s_wload = sem("s_wload")
        s_wtr = sem("s_wtr")
        s_wtc = sem("s_wtc")
        s_fuse = sem("s_fuse")
        s_fusec = sem("s_fusec")

        x_all = sb("x_all", [P, TILES, D])
        adjt = sb("adjt", [P, N], I32)
        mask = sb("mask", [P, N], BF16)
        maskT = sb("maskT", [P, TILES, P])
        deg = sb("deg", [P, 4])
        agg_sb = sb("agg_sb", [P, D])

        s_xall = sem("s_xall")
        s_adj = sem("s_adj")
        s_mask = sem("s_mask")
        s_deg = sem("s_deg")
        s_mT = sem("s_mT")
        s_mTc = sem("s_mTc")
        s_agg = sem("s_agg")
        s_aggs = sem("s_aggs")
        s_aggst = sem("s_aggst")

        xa = sb("xa", [P, 2, D])
        xaT = sb("xaT", [P, 2 * KC, P])
        y = sb("y", [P, D])
        st = sb("st", [P, 12])
        x1 = sb("x1", [P, D])
        x1T = sb("x1T", [P, KC, P])
        qkT = sb("qkT", [P, 4, P])
        v_sb = sb("v_sb", [P, D])
        s_xa = sem("s_xa")
        s_xaT = sem("s_xaT")
        s_xaTc = sem("s_xaTc")
        s_lin = sem("s_lin")
        s_ln = sem("s_ln")
        s_sq = sem("s_sq")
        s_x1 = sem("s_x1")
        s_x1T = sem("s_x1T")
        s_x1Tc = sem("s_x1Tc")
        s_qkv = sem("s_qkv")
        s_qkvc = sem("s_qkvc")
        s_tst = sem("s_tst")

        kT_h = sb("kT_h", [HD, N])
        v_h = sb("v_h", [P, TILES, HD])
        qT_h = sb("qT_h", [HD, P])
        sc = sb("sc", [P, N])
        madd = sb("madd", [P, N], BF16)
        hard = sb("hard", [P, N], BF16)
        hardT = maskT
        en = sb("en", [P, 1])
        sm = sb("sm", [P, 8])
        o_sb = sb("o_sb", [P, HD])
        s_kv = sem("s_kv")
        s_aq = sem("s_aq")
        s_m2 = sem("s_m2")
        s_en = sem("s_en")
        s_sc = sem("s_sc")
        s_scc = sem("s_scc")
        s_smx = sem("s_smx")
        s_exp = sem("s_exp")
        s_hard = sem("s_hard")
        s_hT = sem("s_hT")
        s_hTc = sem("s_hTc")
        s_o = sem("s_o")
        s_oc = sem("s_oc")
        s_ost = sem("s_ost")
        s_fl = sem("s_fl")
        s_fln = sem("s_fln")
        s_fsq = sem("s_fsq")
        s_fy = sem("s_fy")
        s_fst = sem("s_fst")

        s_held = {k: sem(f"s_held_{k}") for k in ("sp", "pe", "dve", "act")}

        def hold(eng, name):
            eng.sem_inc(s_held[name], 1)

        block = ctx.enter_context(nc.Block())

        def prep_sync(sp):
            for i, w in enumerate((W_self, W_nb, WQ, WK, WV)):
                sp.dma_start(w_raw[:, i, :, :], w.rearrange("(c p) n -> p c n", p=P)).then_inc(s_wload, 16)
            sp.dma_start(w_comb[:, :, :], W_comb.rearrange("(c p) n -> p c n", p=P)).then_inc(s_wload, 16)
            with nc.allow_non_contiguous_dma("bias columns, 1 KB each"):
                sp.dma_start(b_col[:, 0, :], b_self.rearrange("(c p) -> p c", p=P)).then_inc(s_wload, 16)
                sp.dma_start(b_col[:, 1, :], b_nb.rearrange("(c p) -> p c", p=P)).then_inc(s_wload, 16)
                sp.dma_start(we_col[:, :], we.rearrange("a d -> d a")).then_inc(s_wload, 16)
            sp.dma_start(bc_row[:, :], b_comb.rearrange("(a n) -> a n", a=1)).then_inc(s_wload, 16)
            sp.dma_start(be_col[:, :], be.rearrange("(a n) -> a n", a=1).partition_broadcast(P) if False else be.rearrange("(a n) -> a n", a=1).broadcast_to([P, 1])).then_inc(s_wload, 16)

        WLOADS = 11 * 16

        def prep_gpsimd(pool):
            pool.memset(ident[:, :], 0.0).then_inc(s_const, 1)
            pool.memset(identb[:, :], 0.0).then_inc(s_const, 1)
            pool.memset(ones[:, :], 1.0).then_inc(s_const, 1)
            pool.wait_ge(s_const, 3)
            for m in (ident, identb):
                pool.affine_select(out=m[:, :], in_=m[:, :], compare_op=ALU.not_equal, fill=1.0, base=0,
                                   pattern=[[-1, P]], channel_multiplier=1).then_inc(s_const, 1)

        def prep_tensor(pe):
            pe.wait_ge(s_const, 5)
            pe.wait_ge(s_wload, WLOADS)
            for i in range(5):
                for r in range(KC):
                    for c in range(KC):
                        last = pe.transpose(bank[i][:, c * D + r * P:c * D + (r + 1) * P],
                                            w_raw[:, i, r, c * P:(c + 1) * P], ident[:, :])
                last.then_inc(s_wtr, 1)
            pe.wait_ge(s_wtc, 2)
            for half in range(2):
                for m in range(KC):
                    for k in range(KC):
                        last = pe.matmul(bank[5 + half][:, m * D:(m + 1) * D],
                                         w_t[:, half, k, m * P:(m + 1) * P], w_comb[:, half * KC + k, :],
                                         start=(k == 0), stop=(k == KC - 1))
            for half in range(2):
                for k in range(KC):
                    pe.matmul(bank[7][0:1, 0:D], b_col[:, half, k:k + 1], w_comb[:, half * KC + k, :],
                              start=(half + k == 0), stop=False)
            last = pe.matmul(bank[7][0:1, 0:D], ones[0:1, 0:1], bc_row[:, :], start=False, stop=True)
            last.then_inc(s_fuse, 1)

        def prep_vector(dve):
            for i in range(5):
                dve.wait_ge(s_wtr, i + 1)
                dve.tensor_copy(w_t[:, i, :, :].rearrange("p c n -> p (c n)"), bank[i][:, :]).then_inc(s_wtc, 1)
            dve.wait_ge(s_fuse, 1)
            for half in range(2):
                dve.tensor_copy(w_fused[:, half * KC:(half + 1) * KC, :].rearrange("p c n -> p (c n)"),
                                bank[5 + half][:, :]).then_inc(s_fusec, 1)
            dve.tensor_copy(b_fused[:, :], bank[7][0:1, 0:D]).then_inc(s_fusec, 1)
            dve.wait_ge(s_wtc, 5)
            dve.wait_ge(s_fusec, 3)

        def agg_sync(sp):
            sp.dma_start(x_all[:, :, :], x.rearrange("(t p) d -> p t d", p=P)).then_inc(s_xall, 16)
            with sp.Fori(0, TILES) as t:
                sp.dma_start(adjt[:, :], adj[bass.ds(t * P, P), :]).then_inc(s_adj, 16)
                sp.wait_ge(s_aggs, t + 1)
                hold(sp, "sp")
                sp.dma_start(agg_d[bass.ds(t * P, P), :], agg_sb[:, :]).then_inc(s_aggst, 16)
                sp.wait_ge(s_aggst, t * 16 + 16)
                hold(sp, "sp")

        def agg_vector(dve):
            with dve.Fori(0, TILES) as t:
                dve.wait_ge(s_adj, t * 16 + 16)
                dve.tensor_scalar(mask[:, :], adjt[:, :], 0.0, None, ALU.is_gt).then_inc(s_mask, 1)
                dve.wait_ge(s_mask, t + 1)
                dve.tensor_reduce(deg[:, 0:1], mask[:, :], AX_X, ALU.add).then_inc(s_deg, 1)
                dve.wait_ge(s_deg, t * 3 + 1)
                dve.tensor_scalar(deg[:, 1:2], deg[:, 0:1], 1.0, None, ALU.max).then_inc(s_deg, 1)
                dve.wait_ge(s_deg, t * 3 + 2)
                dve.reciprocal(deg[:, 2:3], deg[:, 1:2]).then_inc(s_deg, 1)
                for b in range(4):
                    dve.wait_ge(s_mT, t * 4 + (b + 1))
                    dve.tensor_copy(maskT[:, 8 * b:8 * b + 8, :].rearrange("p c r -> p (c r)"),
                                    bank[b][:, :].bitcast(BF16)).then_inc(s_mTc, 1)
                dve.wait_ge(s_agg, t + 1)
                dve.wait_ge(s_deg, t * 3 + 3)
                dve.tensor_scalar(agg_sb[:, :], bank[4][:, 0:D], deg[:, 2:3], None, ALU.mult).then_inc(s_aggs, 1)

        def agg_tensor(pe):
            pe.wait_ge(s_xall, 16)
            with pe.Fori(0, TILES) as t:
                pe.wait_ge(s_mask, t + 1)
                for b in range(4):
                    for c in range(8):
                        last = pe.transpose(bank[b][:, :].bitcast(BF16)[:, c * P:(c + 1) * P],
                                            mask[:, (8 * b + c) * P:(8 * b + c + 1) * P], identb[:, :])
                    last.then_inc(s_mT, 1)
                for b in range(4):
                    pe.wait_ge(s_mTc, t * 4 + (b + 1))
                    for c in range(8 * b, 8 * b + 8):
                        last = pe.matmul(bank[4][:, 0:D], maskT[:, c, :], x_all[:, c, :],
                                         start=(c == 0), stop=(c == TILES - 1))
                last.then_inc(s_agg, 1)

        def tail_sync(sp):
            with sp.Fori(0, TILES) as t:
                sp.dma_start(xa[:, 0, :], x[bass.ds(t * P, P), :]).then_inc(s_xa, 16)
                sp.dma_start(xa[:, 1, :], agg_d[bass.ds(t * P, P), :]).then_inc(s_xa, 16)
                sp.wait_ge(s_x1, t + 1)
                hold(sp, "sp")
                sp.dma_start(x1_d[bass.ds(t * P, P), :], x1[:, :]).then_inc(s_tst, 16)
                sp.wait_ge(s_qkvc, t * 2 + 2)
                hold(sp, "sp")
                sp.dma_start(qT_d.rearrange("(c p) n -> p c n", p=P)[:, :, bass.ds(t * P, P)], qkT[:, 0:2, :]).then_inc(s_tst, 16)
                sp.dma_start(kT_d.rearrange("(c p) n -> p c n", p=P)[:, :, bass.ds(t * P, P)], qkT[:, 2:4, :]).then_inc(s_tst, 16)
                sp.dma_start(v_d[bass.ds(t * P, P), :], v_sb[:, :]).then_inc(s_tst, 16)
                sp.wait_ge(s_tst, t * 64 + 64)
                hold(sp, "sp")

        def tail_tensor(pe):
            with pe.Fori(0, TILES) as t:
                pe.wait_ge(s_xa, t * 32 + 32)
                for i in range(2 * KC):
                    last = pe.transpose(bank[0][:, i * P:(i + 1) * P], xa[:, i // KC, (i % KC) * P:(i % KC + 1) * P], ident[:, :])
                last.then_inc(s_xaT, 1)
                pe.wait_ge(s_xaTc, t + 1)
                for i in range(2 * KC):
                    pe.matmul(bank[1][:, 0:D], xaT[:, i, :], w_fused[:, i, :], start=(i == 0), stop=False)
                pe.matmul(bank[1][:, 0:D], ones[:, :], b_fused[:, :], start=False, stop=True).then_inc(s_lin, 1)
                pe.wait_ge(s_x1, t + 1)
                for i in range(KC):
                    last = pe.transpose(bank[2][:, i * P:(i + 1) * P], x1[:, i * P:(i + 1) * P], ident[:, :])
                last.then_inc(s_x1T, 1)
                pe.wait_ge(s_x1Tc, t + 1)
                for j in range(4):
                    for k in range(KC):
                        pe.matmul(bank[3][:, j * P:(j + 1) * P], w_t[:, 2 + j // 2, k, (j % 2) * P:(j % 2 + 1) * P],
                                  x1T[:, k, :], start=(k == 0), stop=(k == KC - 1))
                for k in range(KC):
                    last = pe.matmul(bank[4][:, 0:D], x1T[:, k, :], w_t[:, 4, k, :], start=(k == 0), stop=(k == KC - 1))
                last.then_inc(s_qkv, 1)

        def tail_vector(dve):
            with dve.Fori(0, TILES) as t:
                dve.wait_ge(s_xaT, t + 1)
                dve.tensor_copy(xaT[:, :, :].rearrange("p c r -> p (c r)"), bank[0][:, :]).then_inc(s_xaTc, 1)
                dve.wait_ge(s_lin, t + 1)
                dve.scalar_tensor_tensor(y[:, :], bank[1][:, 0:D], 0.0, xa[:, 0, :], ALU.max, ALU.add).then_inc(s_ln, 1)
                dve.wait_ge(s_ln, t * 4 + 1)
                dve.bn_stats(st[:, 0:6], y[:, :]).then_inc(s_ln, 1)
                dve.wait_ge(s_ln, t * 4 + 2)
                hold(dve, "dve")
                dve.bn_aggr(st[:, 6:8], st[:, 0:6]).then_inc(s_ln, 1)
                dve.wait_ge(s_ln, t * 4 + 3)
                dve.tensor_scalar(st[:, 8:9], st[:, 7:8], EPS, None, ALU.add).then_inc(s_ln, 1)
                dve.wait_ge(s_sq, t * 2 + 1)
                dve.reciprocal(st[:, 10:11], st[:, 9:10]).then_inc(s_sq, 1)
                dve.wait_ge(s_sq, t * 2 + 2)
                dve.tensor_scalar(x1[:, :], y[:, :], st[:, 6:7], st[:, 10:11], ALU.subtract, ALU.mult).then_inc(s_x1, 1)
                dve.wait_ge(s_x1T, t + 1)
                dve.tensor_copy(x1T[:, :, :].rearrange("p c r -> p (c r)"), bank[2][:, 0:D]).then_inc(s_x1Tc, 1)
                dve.wait_ge(s_qkv, t + 1)
                dve.tensor_copy(qkT[:, :, :].rearrange("p c r -> p (c r)"), bank[3][:, :]).then_inc(s_qkvc, 1)
                dve.tensor_copy(v_sb[:, :], bank[4][:, 0:D]).then_inc(s_qkvc, 1)

        def tail_scalar(act):
            with act.Fori(0, TILES) as t:
                act.wait_ge(s_ln, t * 4 + 4)
                act.activation(st[:, 9:10], st[:, 8:9], ACT.Sqrt).then_inc(s_sq, 1)

        def att_sync(sp):
            with sp.Fori(0, HEADS) as h:
                sp.dma_start(kT_h[:, :], kT_d[bass.ds(h * HD, HD), :]).then_inc(s_kv, 16)
                with nc.allow_non_contiguous_dma("a head's 128-byte rows of V"):
                    sp.dma_start(v_h[:, :, :], v_d.rearrange("(t p) d -> p t d", p=P)[:, :, bass.ds(h * HD, HD)]).then_inc(s_kv, 16)
                with sp.Fori(0, TILES) as t:
                    n = h * TILES + t
                    sp.dma_start(adjt[:, :], adj[bass.ds(t * P, P), :]).then_inc(s_aq, 16)
                    sp.dma_start(qT_h[:, :], qT_d[bass.ds(h * HD, HD), bass.ds(t * P, P)]).then_inc(s_aq, 16)
                    sp.wait_ge(s_oc, n + 1)
                    hold(sp, "sp")
                    with nc.allow_non_contiguous_dma("a head's 128-byte rows"):
                        sp.dma_start(att_d[bass.ds(t * P, P), bass.ds(h * HD, HD)], o_sb[:, :]).then_inc(s_ost, 16)
                    sp.wait_ge(s_ost, n * 16 + 16)
                    hold(sp, "sp")

        def att_tensor(pe):
            with pe.Fori(0, HEADS) as h:
                pe.wait_ge(s_kv, h * 32 + 32)
                hold(pe, "pe")
                with pe.Fori(0, TILES) as t:
                    n = h * TILES + t
                    pe.wait_ge(s_aq, n * 32 + 32)
                    pe.matmul(bank[4][:, 0:1], qT_h[:, :], we_col[:, :], start=True, stop=True).then_inc(s_en, 1)
                    for c in range(8):
                        if c >= 4:
                            pe.wait_ge(s_scc, n * 8 + (c - 3))
                        pe.matmul(bank[c % 4][:, :], qT_h[:, :], kT_h[:, c * 512:(c + 1) * 512],
                                  start=True, stop=True).then_inc(s_sc, 1)
                    pe.wait_ge(s_hard, n + 1)
                    for b in range(4):
                        if b >= 2:
                            pe.wait_ge(s_hTc, n * 4 + (b - 1))
                        for c in range(8):
                            last = pe.transpose(bank[5 + b % 2][:, :].bitcast(BF16)[:, c * P:(c + 1) * P],
                                                hard[:, (8 * b + c) * P:(8 * b + c + 1) * P], identb[:, :])
                        last.then_inc(s_hT, 1)
                    pe.wait_ge(s_hTc, n * 4 + 4)
                    for c in range(TILES):
                        last = pe.matmul(bank[7][:, 0:HD], hardT[:, c, :], v_h[:, c, :],
                                         start=(c == 0), stop=(c == TILES - 1))
                    last.then_inc(s_o, 1)

        def att_vector(dve):
            with dve.Fori(0, HEADS) as h:
                with dve.Fori(0, TILES) as t:
                    n = h * TILES + t
                    dve.wait_ge(s_aq, n * 32 + 32)
                    dve.tensor_scalar(mask[:, :], adjt[:, :], 0.0, None, ALU.is_gt).then_inc(s_m2, 1)
                    dve.wait_ge(s_m2, n * 3 + 1)
                    dve.tensor_scalar(madd[:, :], mask[:, :], 1.0, BIG, ALU.subtract, ALU.mult).then_inc(s_m2, 1)
                    dve.wait_ge(s_en, n + 1)
                    dve.tensor_scalar(en[:, :], bank[4][:, 0:1], be_col[:, :], None, ALU.add).then_inc(s_m2, 1)
                    dve.wait_ge(s_m2, n * 3 + 3)
                    for c in range(8):
                        dve.wait_ge(s_sc, n * 8 + (c + 1))
                        dve.tensor_scalar(sc[:, c * 512:(c + 1) * 512], bank[c % 4][:, :], SCALING, en[:, :],
                                          ALU.mult, ALU.add).then_inc(s_scc, 1)
                    dve.wait_ge(s_scc, n * 8 + 8)
                    dve.tensor_tensor(sc[:, :], sc[:, :], madd[:, :], ALU.add).then_inc(s_smx, 1)
                    dve.wait_ge(s_smx, n * 6 + 1)
                    dve.tensor_reduce(sm[:, 0:1], sc[:, :], AX_X, ALU.max, negate=True).then_inc(s_smx, 1)
                    dve.wait_ge(s_exp, n + 1)
                    dve.reciprocal(sm[:, 2:3], sm[:, 1:2]).then_inc(s_smx, 1)
                    dve.wait_ge(s_smx, n * 6 + 3)
                    dve.tensor_scalar(sc[:, :], sc[:, :], sm[:, 2:3], None, ALU.mult).then_inc(s_smx, 1)
                    dve.wait_ge(s_smx, n * 6 + 4)
                    dve.tensor_reduce(sm[:, 3:4], sc[:, :], AX_X, ALU.max).then_inc(s_smx, 1)
                    dve.wait_ge(s_smx, n * 6 + 5)
                    dve.scalar_tensor_tensor(hard[:, :], sc[:, :], sm[:, 3:4], mask[:, :], ALU.is_equal, ALU.mult).then_inc(s_hard, 1)
                    dve.tensor_scalar(sm[:, 4:5], sm[:, 3:4], 1.0, None, ALU.mult).then_inc(s_smx, 1)
                    for b in range(4):
                        dve.wait_ge(s_hT, n * 4 + (b + 1))
                        dve.tensor_copy(hardT[:, 8 * b:8 * b + 8, :].rearrange("p c r -> p (c r)"),
                                        bank[5 + b % 2][:, :].bitcast(BF16)).then_inc(s_hTc, 1)
                    dve.wait_ge(s_o, n + 1)
                    dve.tensor_scalar(o_sb[:, :], bank[7][:, 0:HD], 1.0 / HEADS, None, ALU.mult).then_inc(s_oc, 1)

        def att_scalar(act):
            with act.Fori(0, HEADS) as h:
                with act.Fori(0, TILES) as t:
                    n = h * TILES + t
                    act.wait_ge(s_smx, n * 6 + 2)
                    act.activation(sc[:, :], sc[:, :], ACT.Exp, bias=sm[:, 0:1], accum_out=sm[:, 1:2]).then_inc(s_exp, 1)

        def fin_sync(sp):
            with sp.Fori(0, TILES) as t:
                sp.dma_start(xa[:, 0, :], x1_d[bass.ds(t * P, P), :]).then_inc(s_fl, 16)
                sp.dma_start(xa[:, 1, :], att_d[bass.ds(t * P, P), :]).then_inc(s_fl, 16)
                sp.wait_ge(s_fy, t + 1)
                hold(sp, "sp")
                sp.dma_start(out[bass.ds(t * P, P), :], x1[:, :]).then_inc(s_fst, 16)
                sp.wait_ge(s_fst, t * 16 + 16)
                hold(sp, "sp")

        def fin_vector(dve):
            with dve.Fori(0, TILES) as t:
                dve.wait_ge(s_fl, t * 32 + 32)
                dve.tensor_tensor(y[:, :], xa[:, 0, :], xa[:, 1, :], ALU.add).then_inc(s_fln, 1)
                dve.wait_ge(s_fln, t * 4 + 1)
                dve.bn_stats(st[:, 0:6], y[:, :]).then_inc(s_fln, 1)
                dve.wait_ge(s_fln, t * 4 + 2)
                hold(dve, "dve")
                dve.bn_aggr(st[:, 6:8], st[:, 0:6]).then_inc(s_fln, 1)
                dve.wait_ge(s_fln, t * 4 + 3)
                dve.tensor_scalar(st[:, 8:9], st[:, 7:8], EPS, None, ALU.add).then_inc(s_fln, 1)
                dve.wait_ge(s_fsq, t * 2 + 1)
                dve.reciprocal(st[:, 10:11], st[:, 9:10]).then_inc(s_fsq, 1)
                dve.wait_ge(s_fsq, t * 2 + 2)
                dve.tensor_scalar(x1[:, :], y[:, :], st[:, 6:7], st[:, 10:11], ALU.subtract, ALU.mult).then_inc(s_fy, 1)

        def fin_scalar(act):
            with act.Fori(0, TILES) as t:
                act.wait_ge(s_fln, t * 4 + 4)
                act.activation(st[:, 9:10], st[:, 8:9], ACT.Sqrt).then_inc(s_fsq, 1)

        @block.sync
        def _(sp):
            prep_sync(sp)
            agg_sync(sp)
            tail_sync(sp)
            att_sync(sp)
            fin_sync(sp)

        @block.gpsimd
        def _(pool):
            prep_gpsimd(pool)

        @block.tensor
        def _(pe):
            prep_tensor(pe)
            agg_tensor(pe)
            pe.wait_ge(s_fusec, 3)
            pe.wait_ge(s_wtc, 5)
            tail_tensor(pe)
            att_tensor(pe)

        @block.vector
        def _(dve):
            prep_vector(dve)
            agg_vector(dve)
            tail_vector(dve)
            att_vector(dve)
            fin_vector(dve)

        @block.scalar
        def _(act):
            tail_scalar(act)
            att_scalar(act)
            fin_scalar(act)


_INS = ['x', 'adj', 'L0_gnn_W_self', 'L0_gnn_b_self', 'L0_gnn_W_nb', 'L0_gnn_b_nb', 'L0_gnn_W_comb', 'L0_gnn_b_comb',
        'L1_gnn_WQ', 'L1_gnn_WK', 'L1_gnn_WV', 'L1_gnn_we', 'L1_gnn_be']


def kernel(**inputs):
    import numpy as _np
    import concourse.bacc as _bacc
    from concourse import mybir as _mybir
    from concourse.bass_utils import run_bass_kernel_spmd as _run

    nc = _bacc.Bacc("TRN2", target_bir_lowering=False, num_devices=1)
    arrays, args = {}, []
    for name in _INS:
        a = _np.ascontiguousarray(inputs[name])
        arrays[f"in_{name}"] = a
        args.append(nc.dram_tensor(f"in_{name}", a.shape, _mybir.dt.from_np(a.dtype), kind="ExternalInput").ap())
    args.append(nc.dram_tensor("out_0", (N, D), _mybir.dt.float32, kind="ExternalOutput").ap())
    gnn_kernel(nc, *args)
    return _run(nc, [arrays], core_ids=[0]).results[0]["out_0"]
```

```python
from contextlib import ExitStack

import concourse.bass as bass
from concourse import mybir

ALU = mybir.AluOpType
ACT = mybir.ActivationFunctionType
F32 = mybir.dt.float32
F16 = mybir.dt.float16
I32 = mybir.dt.int32
U32 = mybir.dt.uint32
U16 = mybir.dt.uint16
BF16 = mybir.dt.bfloat16
AX_X = mybir.AxisListType.X
AX_XY = mybir.AxisListType.XY

P = 128
N = 4096
D = 256
HEADS = 8
HD = D // HEADS
TILES = N // P
KC = D // P
SCALING = HD ** -0.5
EPS = 1e-5
BIG = 1e30

CHUNKS = 8
CW = N // CHUNKS
SLOTS = 16
EB = 6
EDGES = EB * P
HALF = N // 2
SKIP = 2 * N

GT = 4
GROUPS = TILES // GT
GB = GT * EB
PT = 2
PAIRS = TILES // PT
PB = PT * EB
QW = D + HEADS
KVW = 2 * D
INFO = 2 + SLOTS


class At:

    def __init__(self, i, off, step=2):
        self.i, self.off, self.step = i, off, step

    def lin(self, a, b=0):
        c = a * self.off + b
        return c if self.i is None else self.i * (a * self.step) + c

    def back(self, n):
        return At(self.i, self.off - n, self.step)


def wait(eng, sem, value):
    if not isinstance(value, int) or value > 0:
        eng.wait_ge(sem, value)


def sparse_layer1(nc, g, dr):
    ctx = ExitStack()
    with ctx:
        def sb(name, shape, dt=F32):
            return ctx.enter_context(nc.sbuf_tensor(name, shape, dt))

        def sem(name):
            return ctx.enter_context(nc.semaphore(name))

        bank = g.bank
        adjt = sb("p1_adjt", [P, GT, N], I32)
        mk = sb("p1_mk", [P, 2, N], BF16)
        key = sb("p1_key", [P, N], U16)
        col1 = sb("p1_col1", [P, N], U16)
        found = sb("p1_found", [P, GT, CHUNKS, 8])
        rest = sb("p1_rest", [P, CHUNKS * 8])
        top = sb("p1_top", [P, GT, SLOTS])
        nz = sb("p1_nz", [P, GT, CHUNKS * 8], BF16)
        deg_h = sb("p1_deg_h", [P, GT], F16)
        rdeg = sb("p1_rdeg", [P, 2, GT])
        deg1 = sb("p1_deg1", [P, GT])
        deg_half = sb("p1_deg_half", [P, GT])
        info = sb("p1_info", [P, GT, INFO], F16)
        sel = sb("p1_sel", [P, GT, EDGES], F16)
        selT = sb("p1_selT", [P, GB, P])
        slot_e = sb("p1_slot_e", [P, GB])
        cs = sb("p1_cs", [P, GB, SLOTS], F16)
        colr = sb("p1_colr", [P, GB])
        unused = sb("p1_unused", [P, GB])
        colu = sb("p1_colu", [P, GB], U32)
        xg = sb("p1_xg", [P, GT, EB, D])
        xt = sb("p1_xt", [P, 2, GT, D])
        agg = sb("p1_agg", [P, GT, D])
        xaT = sb("p1_xaT", [P, 2, 2 * KC, P])
        y = agg
        stats = sb("p1_stats", [P, GT, 6])
        mv = sb("p1_mv", [P, GT, 2])
        rs = sb("p1_rs", [P, 3, GT])
        x1 = sb("p1_x1", [P, GT, D])
        x1T = sb("p1_x1T", [P, GT, KC, P])
        q_sb = sb("p1_q_sb", [P, GT, QW])
        kv_sb = sb("p1_kv_sb", [P, GT, KVW])
        w_raw = xg[:, 0:2, :, :].rearrange("p a b d -> p (a b) d")[:, 0:10, :].rearrange("p (i c) d -> p i c d", c=KC)
        w_comb = x1[:, :, :]

        s_const, s_zero, s_wload, s_weload = sem("p1_const"), sem("p1_zero"), sem("p1_wload"), sem("p1_weload")
        s_wtr, s_wtc, s_fuse, s_fusec = sem("p1_wtr"), sem("p1_wtc"), sem("p1_fuse"), sem("p1_fusec")
        s_xgz = sem("p1_xgz")
        s_adj = [sem(f"p1_adj{k}") for k in range(GT)]
        s_x = [sem(f"p1_x{k}") for k in range(2)]
        s_gather = [sem(f"p1_gather{k}") for k in range(GT)]
        s_mk, s_key, s_found, s_top = sem("p1_mk_ready"), sem("p1_key_ready"), sem("p1_found_ready"), sem("p1_top_ready")
        s_deg, s_start, s_rstd, s_info, s_sel = sem("p1_deg_ready"), sem("p1_start_ready"), sem("p1_rstd"), sem("p1_info_ready"), sem("p1_sel_ready")
        s_einfo, s_ix, s_colu, s_selT = sem("p1_einfo_ready"), sem("p1_index_steps"), sem("p1_colu_ready"), sem("p1_selT_ready")
        s_agg, s_aggsb, s_T, s_Tc, s_lin = sem("p1_agg_ready"), sem("p1_aggsb_ready"), sem("p1_T_ready"), sem("p1_T_copied"), sem("p1_lin_ready")
        s_y, s_ln, s_sqrt, s_x1 = sem("p1_y_ready"), sem("p1_ln_steps"), sem("p1_sqrt_ready"), sem("p1_x1_ready")
        s_x1T, s_x1Tc, s_qkv, s_qkvc = sem("p1_x1T_ready"), sem("p1_x1T_copied"), sem("p1_qkv_ready"), sem("p1_qkv_copied")
        s_slot, s_selps, s_x1store, s_tables, s_flag = sem("p1_slot_e_ready"), sem("p1_sel_transposed"), sem("p1_x1_stored"), sem("p1_tables_stored"), sem("p1_flag_steps")

        def hold(eng):
            g.hold(eng)

        iota_e = g.iota_e

        with nc.Block() as block:

            def sp_group(sp, a):
                for k in range(GT):
                    wait(sp, s_mk, a.lin(GT, k + 1 - GT))
                    if a.i is not None:
                        hold(sp)
                    sp.dma_start(adjt[:, k, :], dr.adj[bass.ds(a.lin(GT * P, k * P), P), :]).then_inc(s_adj[k], 16)

            @block.sync
            def _(sp):
                sp_group(sp, At(None, 0))
                sp_group(sp, At(None, 1))
                with sp.Fori(1, GROUPS // 2) as i:
                    for half in range(2):
                        sp_group(sp, At(i, half))

            def pool_group(pool, a):
                for k in range(GT):
                    if k == 0:
                        pool.wait_ge(s_colu, a.lin(1, 1))
                    wait(pool, s_agg, a.lin(GT, k + 1 - GT))
                    if a.i is not None:
                        hold(pool)
                    for b in range(EB):
                        pool.indirect_dma_start(out=xg[:, k, b, :], out_offset=None, in_=dr.x,
                                                in_offset=bass.IndirectOffsetOnAxis(ap=colu[:, k * EB + b:k * EB + b + 1], axis=0),
                                                bounds_check=N - 1, oob_is_err=False).then_inc(s_gather[k], 16)

            @block.gpsimd
            def _(pool):
                g.constants(pool, s_const)
                pool.iota(col1[:, :], [[1, N]], base=1, channel_multiplier=0,
                          allow_small_or_imprecise_dtypes=True).then_inc(s_const, 1)
                pool.iota(info[:, :, 1], [[0, GT]], base=1, channel_multiplier=1,
                          allow_small_or_imprecise_dtypes=True).then_inc(s_const, 1)
                pool.wait_ge(s_wtr, 5)
                pool.wait_ge(s_fuse, 1)
                pool.memset(xg[:, :, :, :], 0.0).then_inc(s_xgz, 1)
                pool.wait_ge(s_xgz, 1)
                pool_group(pool, At(None, 0))
                with pool.Fori(0, (GROUPS - 2) // 2) as i:
                    for half in range(2):
                        pool_group(pool, At(i, half + 1))
                pool_group(pool, At(None, GROUPS - 1))

            def act_mask(act, a, k):
                act.wait_ge(s_adj[k], a.lin(16, 16))
                wait(act, s_key, a.lin(GT, k - 1))
                act.activation(mk[:, k % 2, :], adjt[:, k, :], ACT.Sign).then_inc(s_mk, 1)

            def act_first(act, a):
                for k in range(GT):
                    act.wait_ge(s_agg, a.lin(GT, (k | 1) + 1))
                    if k == 0:
                        act.wait_ge(s_colu, a.lin(1, 1))
                        wait(act, s_x1, a.lin(GT, 0))
                    act.activation(agg[:, k, :], bank[k // 2][:, (k % 2) * D:(k % 2 + 1) * D], ACT.Copy,
                                   scale=rdeg[:, a.off % 2, k:k + 1]).then_inc(s_aggsb, 1)
                for k in range(GT):
                    act.wait_ge(s_T, a.lin(GT, k + 1))
                    wait(act, s_lin, a.lin(GT, k - 1))
                    act.activation(xaT[:, k % 2, :, :].rearrange("p c r -> p (c r)"), bank[2 + k % 2][:, :], ACT.Copy).then_inc(s_Tc, 1)

            def act_second(act, a):
                act.wait_ge(s_ln, a.lin(4, 4))
                act.activation(rs[:, 1, :], rs[:, 0, :], ACT.Sqrt).then_inc(s_sqrt, 1)
                act.wait_ge(s_x1, a.lin(GT, GT))
                hold(act)
                act.dma_start(dr.x1.rearrange("(t p) d -> p t d", p=P)[:, bass.ds(a.lin(GT), GT), :], x1[:, :, :]).then_inc(s_x1store, 16)
                for j in range(2):
                    act.wait_ge(s_x1T, a.lin(2, j + 1))
                    act.activation(x1T[:, 2 * j:2 * j + 2, :, :].rearrange("p k c r -> p (k c r)"), bank[2 + j][:, :], ACT.Copy).then_inc(s_x1Tc, 1)
                if a.i is not None or a.off > 0:
                    act.wait_ge(s_tables, a.lin(32, 0))
                    hold(act)
                for k in range(GT):
                    act.wait_ge(s_qkv, a.lin(GT, k + 1))
                    qb = bank[5] if k % 2 == 0 else bank[2]
                    act.activation(q_sb[:, k, 0:D], qb[:, 0:D], ACT.Copy, scale=SCALING)
                    act.activation(q_sb[:, k, D:QW], qb[:, D:QW], ACT.Copy)
                    act.activation(kv_sb[:, k, :], bank[4 + 2 * (k % 2)][:, :], ACT.Copy).then_inc(s_qkvc, 1)
                act.wait_ge(s_qkvc, a.lin(GT, GT))
                hold(act)
                act.dma_start(dr.q.rearrange("(t p) d -> p t d", p=P)[:, bass.ds(a.lin(GT), GT), :], q_sb[:, :, :]).then_inc(s_tables, 16)
                act.dma_start(dr.kv.rearrange("(t p) d -> p t d", p=P)[:, bass.ds(a.lin(GT), GT), :], kv_sb[:, :, :]).then_inc(s_tables, 16)

            def act_selT(act, a):
                for j in range(GB // 8):
                    act.wait_ge(s_selps, a.lin(3, j + 1))
                    act.activation(selT[:, 8 * j:8 * j + 8, :].rearrange("p b r -> p (b r)"), bank[4 + j][:, :].bitcast(F16), ACT.Copy).then_inc(s_selT, 1)

            def act_load_x(act, a):
                act.dma_start(xt[:, a.off % 2, :, :], dr.x.rearrange("(t p) d -> p t d", p=P)[:, bass.ds(a.lin(GT), GT), :]).then_inc(s_x[a.off % 2], 16)

            def act_period(act, a, first, second):
                if a is not None:
                    act_mask(act, a, 0)
                    act_mask(act, a, 1)
                if first is not None:
                    act_selT(act, first)
                if second is not None:
                    act_second(act, second)
                if a is not None:
                    act_load_x(act, a)
                if a is not None:
                    act_mask(act, a, 2)
                    act_mask(act, a, 3)
                if first is not None:
                    act_first(act, first)

            @block.scalar
            def _(act):
                for i, w in enumerate((dr.W_self, dr.W_nb, dr.WQ, dr.WK, dr.WV)):
                    act.dma_start(w_raw[:, i, :, :], w.rearrange("(c p) n -> p c n", p=P)).then_inc(s_wload, 16)
                act.dma_start(w_comb, dr.W_comb.rearrange("(c p) n -> p c n", p=P)).then_inc(s_wload, 16)
                with nc.allow_non_contiguous_dma("bias columns, 1 KB each"):
                    act.dma_start(g.b_col[:, 0, :], dr.b_self.rearrange("(c p) -> p c", p=P)).then_inc(s_wload, 16)
                    act.dma_start(g.b_col[:, 1, :], dr.b_nb.rearrange("(c p) -> p c", p=P)).then_inc(s_wload, 16)
                    act.dma_start(g.we_col[:, :], dr.we.rearrange("a d -> d a")).then_inc(s_wload, 16)
                    act.wait_ge(s_const, g.N_CONST)
                    for h in range(HEADS):
                        act.dma_start(g.we_heads[(h % 4) * HD:(h % 4 + 1) * HD, h // 4, h:h + 1], dr.we.rearrange("a d -> d a")).then_inc(s_weload, 16)
                act.dma_start(g.bc_row[:, :], dr.b_comb.rearrange("(a n) -> a n", a=1)).then_inc(s_wload, 16)
                act.dma_start(g.be_col[:, :], dr.be.rearrange("(a n) -> a n", a=1).broadcast_to([P, 1])).then_inc(s_wload, 16)
                act_period(act, At(None, 0), None, None)
                act_period(act, At(None, 1), At(None, 0), None)
                act_period(act, At(None, 2), At(None, 1), At(None, 0))
                with act.Fori(0, (GROUPS - 4) // 2) as i:
                    for half in range(2):
                        act_period(act, At(i, 3 + half), At(i, 2 + half), At(i, 1 + half))
                act_period(act, At(None, GROUPS - 1), At(None, GROUPS - 2), At(None, GROUPS - 3))
                act_period(act, None, At(None, GROUPS - 1), At(None, GROUPS - 2))
                act_period(act, None, None, At(None, GROUPS - 1))
                act.wait_ge(s_x1store, 16 * GROUPS)
                act.wait_ge(s_tables, 32 * GROUPS)

            def pe_prep(pe):
                pe.wait_ge(s_const, g.N_CONST)
                pe.wait_ge(s_wload, 16 * 11)
                pe.wait_ge(s_weload, 16 * HEADS)
                for i in range(5):
                    for r in range(KC):
                        for c in range(KC):
                            last = pe.transpose(bank[i][:, c * D + r * P:c * D + (r + 1) * P],
                                                w_raw[:, i, r, c * P:(c + 1) * P], g.ident[:, :])
                    last.then_inc(s_wtr, 1)
                pe.wait_ge(s_wtc, 2)
                for half in range(2):
                    for m in range(KC):
                        for k in range(KC):
                            pe.matmul(bank[5 + half][:, m * D:(m + 1) * D],
                                      g.w_t[:, half, k, m * P:(m + 1) * P], w_comb[:, half * KC + k, :],
                                      start=(k == 0), stop=(k == KC - 1))
                for half in range(2):
                    for k in range(KC):
                        pe.matmul(bank[7][0:1, 0:D], g.b_col[:, half, k:k + 1], w_comb[:, half * KC + k, :],
                                  start=(half + k == 0), stop=False)
                pe.matmul(bank[7][0:1, 0:D], g.ones[0:1, 0:1], g.bc_row[:, :], start=False, stop=True)
                pe.wait_ge(s_wtc, 5)
                for m in range(KC):
                    for k in range(KC):
                        last = pe.matmul(bank[0][:, m * HEADS:(m + 1) * HEADS], w_raw[:, 2, k, m * P:(m + 1) * P],
                                         g.we_heads[:, k, :], start=(k == 0), stop=(k == KC - 1))
                last.then_inc(s_fuse, 1)
                pe.wait_ge(s_fusec, 5)

            def pe_starts(pe, a):
                pe.wait_ge(s_deg, a.lin(1, 1))
                pe.matmul(bank[7][:, GB * INFO:GB * INFO + GT], g.below[:, :], deg_h[:, :], start=True, stop=True).then_inc(s_start, 1)
                pe.wait_ge(s_info, a.lin(1, 1))
                pe.wait_ge(s_sel, a.lin(2, 2))
                for b in range(GB):
                    last = pe.matmul(bank[7][:, b * INFO:(b + 1) * INFO], sel[:, b // EB, (b % EB) * P:(b % EB + 1) * P],
                                     info[:, b // EB, :], start=True, stop=True)
                last.then_inc(s_einfo, 1)
                wait(pe, s_qkvc, a.lin(GT, -GT))
                for b in range(GB):
                    last = pe.transpose(bank[4 + b // 8][:, :].bitcast(F16)[:, (b % 8) * P:(b % 8 + 1) * P],
                                        sel[:, b // EB, (b % EB) * P:(b % EB + 1) * P], g.identh[:, :])
                    if b % 8 == 7:
                        last.then_inc(s_selps, 1)

            def pe_first(pe, a):
                pe.wait_ge(s_selT, a.lin(3, 3))
                wait(pe, s_y, a.lin(GT, 0))
                for k in range(GT):
                    pe.wait_ge(s_gather[k], a.lin(16 * EB, 16 * EB))
                    for b in range(EB):
                        last = pe.matmul(bank[k // 2][:, (k % 2) * D:(k % 2 + 1) * D], selT[:, k * EB + b, :], xg[:, k, b, :],
                                         start=(b == 0), stop=(b == EB - 1))
                    last.then_inc(s_agg, 1)
                wait(pe, s_qkvc, a.lin(GT, 0))
                pe.wait_ge(s_x[a.off % 2], x_count(a))
                for k in range(GT):
                    pe.wait_ge(s_aggsb, a.lin(GT, (k | 1) + 1))
                    wait(pe, s_Tc, a.lin(GT, k - 1))
                    for c in range(2 * KC):
                        src = xt[:, a.off % 2, k, :] if c < KC else agg[:, k, :]
                        last = pe.transpose(bank[2 + k % 2][:, c * P:(c + 1) * P], src[:, (c % KC) * P:(c % KC + 1) * P], g.ident[:, :])
                    last.then_inc(s_T, 1)
                    if k >= 1:
                        pe_linear(pe, a, k - 1)
                pe_linear(pe, a, GT - 1)

            def x_count(a):
                return 16 * (a.off // 2 + 1) if a.i is None else a.i * 16 + 16 * (a.off // 2 + 1)

            def pe_linear(pe, a, k):
                pe.wait_ge(s_Tc, a.lin(GT, k + 1))
                reg = bank[k // 2][:, (k % 2) * D:(k % 2 + 1) * D]
                for c in range(2 * KC):
                    pe.matmul(reg, xaT[:, k % 2, c, :], g.w_fused[:, c, :], start=(c == 0), stop=False)
                pe.matmul(reg, g.ones[:, :], g.b_fused[:, :], start=False, stop=True).then_inc(s_lin, 1)

            def pe_second(pe, a):
                pe.wait_ge(s_Tc, a.lin(GT, GT))
                pe.wait_ge(s_selT, a.lin(3, 6) if a.i is not None else min(a.lin(3, 6), 3 * GROUPS))
                for k in range(GT):
                    pe.wait_ge(s_x1, a.lin(GT, k + 1))
                    for c in range(KC):
                        last = pe.transpose(bank[2 + k // 2][:, (k % 2) * D + c * P:(k % 2) * D + (c + 1) * P],
                                            x1[:, k, c * P:(c + 1) * P], g.ident[:, :])
                    if k % 2:
                        last.then_inc(s_x1T, 1)
                for k in range(GT):
                    pe.wait_ge(s_x1Tc, a.lin(2, k // 2 + 1))
                    wait(pe, s_qkvc, a.lin(GT, k - 1))
                    kvb, qb = bank[4 + 2 * (k % 2)], (bank[5] if k % 2 == 0 else bank[2])
                    for w, reg in ((3, kvb[:, 0:D]), (4, kvb[:, D:2 * D]), (2, qb[:, 0:D])):
                        for c in range(KC):
                            pe.matmul(reg, x1T[:, k, c, :], g.w_t[:, w, c, :], start=(c == 0), stop=(c == KC - 1))
                    for c in range(KC):
                        pe.matmul(qb[:, D:QW], x1T[:, k, c, :], g.w_en[:, c, :], start=(c == 0), stop=False)
                    pe.matmul(qb[:, D:QW], g.ones[:, :], g.be_row[:, :], start=False, stop=True).then_inc(s_qkv, 1)

            @block.tensor
            def _(pe):
                pe_prep(pe)
                pe_starts(pe, At(None, 0))
                pe_first(pe, At(None, 0))
                pe_starts(pe, At(None, 1))
                pe_second(pe, At(None, 0))
                with pe.Fori(0, (GROUPS - 2) // 2) as i:
                    for half in range(2):
                        pe_first(pe, At(i, half + 1))
                        pe_starts(pe, At(i, half + 2))
                        pe_second(pe, At(i, half + 1))
                pe_first(pe, At(None, GROUPS - 1))
                pe_second(pe, At(None, GROUPS - 1))
                pe.wait_ge(s_flag, 4)
                pe.matmul(bank[7][0:1, 0:1], g.over[:, 3:4], g.ones_col[:, :], start=True, stop=True).then_inc(s_flag, 1)

            def dve_prep(dve):
                for i in range(5):
                    dve.wait_ge(s_wtr, i + 1)
                    dve.tensor_copy(g.w_t[:, i, :, :].rearrange("p c n -> p (c n)"), bank[i][:, :]).then_inc(s_wtc, 1)
                dve.wait_ge(s_fuse, 1)
                for half in range(2):
                    dve.tensor_copy(g.w_fused[:, half * KC:(half + 1) * KC, :].rearrange("p c n -> p (c n)"),
                                    bank[5 + half][:, :]).then_inc(s_fusec, 1)
                dve.tensor_copy(g.b_fused[:, :], bank[7][0:1, 0:D]).then_inc(s_fusec, 1)
                dve.tensor_copy(g.w_en[:, :, :].rearrange("p c h -> p (c h)"), bank[0][:, 0:KC * HEADS]).then_inc(s_fusec, 1)
                dve.tensor_scalar(g.be_row[:, :], g.ones[0:1, 0:HEADS], g.be_col[0:1, :], None, ALU.mult).then_inc(s_fusec, 1)
                dve.wait_ge(s_const, g.N_CONST + 2)

            def dve_scan(dve, a, k):
                dve.wait_ge(s_mk, a.lin(GT, k + 1))
                dve.tensor_tensor(key[:, :], mk[:, k % 2, :], col1[:, :], ALU.mult).then_inc(s_key, 1)
                dve.wait_ge(s_key, a.lin(GT, k + 1))
                if a.i is not None:
                    hold(dve)
                for c in range(CHUNKS):
                    last = dve.max(found[:, k, c, :], key[:, c * CW:(c + 1) * CW])
                last.then_inc(s_found, 1)
                dve.wait_ge(s_found, a.lin(GT, k + 1))
                if a.i is not None:
                    hold(dve)
                dve.max(top[:, k, 0:8], found[:, k, :, :].rearrange("p c j -> p (c j)")).then_inc(s_top, 1)
                dve.wait_ge(s_top, a.lin(3 * GT, 3 * k + 1))
                if a.i is not None:
                    hold(dve)
                dve.match_replace(rest[:, :], top[:, k, 0:8], found[:, k, :, :].rearrange("p c j -> p (c j)"), 0.0).then_inc(s_top, 1)
                dve.wait_ge(s_top, a.lin(3 * GT, 3 * k + 2))
                if a.i is not None:
                    hold(dve)
                dve.max(top[:, k, 8:16], rest[:, :]).then_inc(s_top, 1)

            def dve_index(dve, a):
                t0 = a.lin(GT)
                deg = g.deg_all[:, bass.ds(t0, GT)]
                start = g.start_all[:, bass.ds(t0, GT)]
                end = g.end_all[:, bass.ds(t0, GT)]
                slotm = g.slot_all[:, bass.ds(a.lin(GB), GB), :]
                n = 9

                def step(j):
                    dve.wait_ge(s_ix, a.lin(n, j))

                dve.wait_ge(s_top, a.lin(3 * GT, 3 * GT))
                dve.tensor_scalar(nz[:, :, :], found[:, :, :, :].rearrange("p t c j -> p t (c j)"), 0.0, None, ALU.is_gt).then_inc(s_ix, 1)
                dve.tensor_copy(g.full_all[:, bass.ds(t0, GT), :], found[:, :, :, 7])
                step(1)
                hold(dve)
                dve.tensor_reduce(deg, nz[:, :, :], AX_X, ALU.add).then_inc(s_ix, 1)
                step(2)
                hold(dve)
                dve.tensor_copy(deg_h[:, :], deg).then_inc(s_deg, 1)
                dve.tensor_scalar(deg1[:, :], deg, 1.0, None, ALU.max).then_inc(s_ix, 1)
                dve.tensor_scalar(info[:, :, 2:INFO], top[:, :, :], -(1.0 + HALF), None, ALU.add).then_inc(s_info, 1)
                dve.tensor_scalar(deg_half[:, :], deg, 0.5, None, ALU.subtract).then_inc(s_ix, 1)
                step(3)
                dve.reciprocal(rdeg[:, a.off % 2, :], deg1[:, :])
                dve.wait_ge(s_start, a.lin(1, 1))
                ps = bank[7][:, GB * INFO:GB * INFO + GT]
                dve.tensor_copy(info[:, :, 0], ps)
                dve.tensor_copy(start, ps)
                step(4)
                dve.tensor_tensor(end, ps, deg_half[:, :], ALU.add).then_inc(s_ix, 1)
                step(5)
                for k in range(GT):
                    last = dve.tensor_scalar(sel[:, k, :], iota_e[:, :], g.start_all[:, bass.ds(a.lin(GT, k), 1)],
                                             g.end_all[:, bass.ds(a.lin(GT, k), 1)], ALU.max, ALU.min)
                last.then_inc(s_sel, 1)
                dve.wait_ge(s_sel, a.lin(2, 1))
                dve.tensor_tensor(sel[:, :, :], sel[:, :, :], iota_e[:, :].unsqueeze(1).to_broadcast([P, GT, EDGES]),
                                  ALU.is_equal).then_inc(s_sel, 1)
                dve.wait_ge(s_einfo, a.lin(1, 1))
                e = bank[7][:, 0:GB * INFO].rearrange("p (b f) -> p b f", f=INFO)
                dve.tensor_tensor(slot_e[:, :], g.edge_no[:, :], e[:, :, 0], ALU.subtract).then_inc(s_slot, 1)
                dve.tensor_scalar(unused[:, :], e[:, :, 1], 0.0, float(SKIP), ALU.is_equal, ALU.mult)
                dve.wait_ge(s_slot, a.lin(1, 1))
                dve.tensor_tensor(slotm, g.iota_s[:, :].unsqueeze(1).to_broadcast([P, GB, SLOTS]),
                                  slot_e[:, :].unsqueeze(2).to_broadcast([P, GB, SLOTS]), ALU.is_equal).then_inc(s_ix, 1)
                dve.tensor_scalar(g.shift_all[:, bass.ds(a.lin(GB), GB)], slot_e[:, :], 0.0, SLOTS - 1.0, ALU.max, ALU.min)
                step(6)
                dve.tensor_tensor(cs[:, :, :], slotm, e[:, :, 2:INFO], ALU.mult).then_inc(s_ix, 1)
                step(7)
                dve.tensor_reduce(colr[:, :], cs[:, :, :], AX_X, ALU.add).then_inc(s_ix, 1)
                step(8)
                dve.scalar_tensor_tensor(colu[:, :], colr[:, :], float(HALF), unused[:, :], ALU.add, ALU.add).then_inc(s_colu, 1)
                dve.wait_ge(s_colu, a.lin(1, 1))
                hold(dve)
                dve.tensor_copy(g.colu_all[:, bass.ds(a.lin(GB), GB)], colu[:, :]).then_inc(s_ix, 1)

            def dve_tail(dve, a):
                for k in range(GT):
                    dve.wait_ge(s_lin, a.lin(GT, (k | 1) + 1))
                    dve.scalar_tensor_tensor(y[:, k, :], bank[k // 2][:, (k % 2) * D:(k % 2 + 1) * D], 0.0,
                                             xt[:, a.off % 2, k, :], ALU.max, ALU.add).then_inc(s_y, 1)
                for k in range(GT):
                    dve.wait_ge(s_y, a.lin(GT, k + 1))
                    last = dve.bn_stats(stats[:, k, :], y[:, k, :])
                last.then_inc(s_ln, 1)
                dve.wait_ge(s_ln, a.lin(4, 1))
                if a.i is not None:
                    hold(dve)
                for k in range(GT):
                    last = dve.bn_aggr(mv[:, k, :], stats[:, k, :])
                last.then_inc(s_ln, 1)
                dve.wait_ge(s_ln, a.lin(4, 2))
                dve.tensor_scalar(rs[:, 0, :], mv[:, :, 1], EPS, None, ALU.add).then_inc(s_ln, 2)
                dve.wait_ge(s_sqrt, a.lin(1, 1))
                dve.reciprocal(rs[:, 2, :], rs[:, 1, :]).then_inc(s_rstd, 1)
                dve.wait_ge(s_rstd, a.lin(1, 1))
                wait(dve, s_x1store, a.lin(16, 0))
                for k in range(GT):
                    dve.tensor_scalar(x1[:, k, :], y[:, k, :], mv[:, k, 0:1], rs[:, 2, k:k + 1], ALU.subtract, ALU.mult).then_inc(s_x1, 1)

            def dve_period(dve, a, tail):
                for k in range(GT):
                    dve_scan(dve, a, k)
                dve_index(dve, a)
                if tail is not None:
                    dve_tail(dve, tail)

            def dve_flag(dve):
                n = 9 * GROUPS
                dve.wait_ge(s_ix, n)
                dve.tensor_reduce(g.over[:, 0:1], g.deg_all[:, :], AX_X, ALU.max)
                dve.tensor_reduce(g.over[:, 1:2], g.full_all[:, :, :], AX_XY, ALU.max)
                dve.tensor_reduce(g.over[:, 2:3], g.end_all[:, :], AX_X, ALU.max).then_inc(s_flag, 1)
                dve.wait_ge(s_flag, 1)
                dve.tensor_scalar(g.over[:, 4:5], g.over[:, 0:1], float(SLOTS), None, ALU.is_gt)
                dve.tensor_scalar(g.over[:, 5:6], g.over[:, 1:2], 0.0, None, ALU.is_gt)
                dve.tensor_scalar(g.over[:, 6:7], g.over[:, 2:3], EDGES - 0.5, None, ALU.is_gt).then_inc(s_flag, 1)
                dve.wait_ge(s_flag, 2)
                dve.tensor_tensor(g.over[:, 7:8], g.over[:, 4:5], g.over[:, 5:6], ALU.add).then_inc(s_flag, 1)
                dve.wait_ge(s_flag, 3)
                dve.tensor_tensor(g.over[:, 3:4], g.over[:, 7:8], g.over[:, 6:7], ALU.add).then_inc(s_flag, 1)
                dve.wait_ge(s_flag, 5)
                dve.tensor_scalar(g.flag[:, :], bank[7][0:1, 0:1], 1.0, None, ALU.mult).then_inc(s_flag, 1)
                dve.wait_ge(s_flag, 6)

            @block.vector
            def _(dve):
                dve_prep(dve)
                dve_period(dve, At(None, 0), None)
                dve_period(dve, At(None, 1), At(None, 0))
                with dve.Fori(0, (GROUPS - 2) // 2) as i:
                    for half in range(2):
                        dve_period(dve, At(i, half + 2), At(i, half + 1))
                dve_tail(dve, At(None, GROUPS - 1))
                dve_flag(dve)


def sparse_layer2(nc, g, dr, m):
    bank = g.bank
    hold = g.hold

    def ring(a, j):
        return (PB // 2 * (a.off % 2) + j) % 4

    def sp_pair(sp, a, load, store):
        if load is not None:
            half = load.off % 2
            wait(sp, m.s_em, load.lin(1, -1))
            hold(sp)
            sp.dma_start(m.qt[:, half, :, :], dr.q.rearrange("(t p) d -> p t d", p=P)[:, bass.ds(load.lin(PT), PT), :]).then_inc(m.s_q[half], 16)
            wait(sp, m.s_res, load.lin(PT, -PT))
            hold(sp)
            sp.dma_start(m.x1t[:, half, :, :], dr.x1.rearrange("(t p) d -> p t d", p=P)[:, bass.ds(load.lin(PT), PT), :]).then_inc(m.s_x1[half], 16)
        if store is not None:
            sp.wait_ge(m.s_out, store.lin(PT, PT))
            hold(sp)
            sp.dma_start(dr.out.rearrange("(t p) d -> p t d", p=P)[:, bass.ds(store.lin(PT), PT), :], m.o_sb[:, :, :]).then_inc(m.s_store, 16)

    def count(a):
        c = 16 * (a.off // 2 + 1)
        return c if a.i is None else a.i * 16 + c

    def pool_gather(pool, a):
        half = a.off % 2
        pool.wait_ge(m.s_colu, a.lin(1, 1))
        wait(pool, m.s_prod, a.lin(PB // 2, -(PB // 2)))
        wait(pool, m.s_vw, a.lin(1, -1))
        hold(pool)
        for b in range(PB):
            pool.indirect_dma_start(out=m.kv[:, half, b, :], out_offset=None, in_=dr.kv,
                                    in_offset=bass.IndirectOffsetOnAxis(ap=m.colu[:, half, b:b + 1], axis=0),
                                    bounds_check=N - 1, oob_is_err=False).then_inc(m.s_gather[half], 16)

    def pool_weigh(pool, a):
        half = a.off % 2
        pool.wait_ge(m.s_w, a.lin(1, 1))
        wait(pool, m.s_o, a.lin(1, 0))
        pool.tensor_tensor(m.vw[:, :, :].rearrange("p b (h d) -> p b h d", d=HD),
                           m.kv[:, half, :, D:KVW].rearrange("p b (h d) -> p b h d", d=HD),
                           m.w[:, :, :].unsqueeze(3).to_broadcast([P, PB, HEADS, HD]), ALU.mult).then_inc(m.s_vw, 1)

    def act_sel(act, a):
        act.wait_ge(m.s_sel, a.lin(2, 2))
        wait(act, m.s_qe, a.lin(PB // 2, 0))
        act.activation(m.sel32[:, :, :], m.sel[:, a.off % 2, :, :], ACT.Copy).then_inc(m.s_sel32, 1)

    def act_selT(act, a):
        for j in range(2):
            act.wait_ge(m.s_selps, a.lin(2, j + 1))
            n = min(8, PB - 8 * j)
            act.activation(m.selT[:, a.off % 2, 8 * j:8 * j + n, :].rearrange("p b r -> p (b r)"),
                           bank[6][:, :].bitcast(F16)[:, 0:n * P], ACT.Copy).then_inc(m.s_selT, 1)

    def act_exp(act, a):
        act.wait_ge(m.s_sm, a.lin(6, 3))
        act.activation(m.att[:, :, :], m.att[:, :, :], ACT.Exp).then_inc(m.s_exp, 1)

    def act_sqrt(act, a):
        act.wait_ge(m.s_ln, a.lin(3, 3))
        act.activation(m.rs[:, 1, :], m.rs[:, 0, :], ACT.Sqrt).then_inc(m.s_sqrt, 1)

    def pe_queries(pe, a):
        half = a.off % 2
        pe.wait_ge(m.s_sel32, a.lin(1, 1))
        pe.wait_ge(m.s_q[half], count(a))
        for j in range(PB // 2):
            wait(pe, m.s_prod, a.lin(PB // 2, j - 3))
            for b in (2 * j, 2 * j + 1):
                last = pe.matmul(bank[ring(a, j)][:, (b % 2) * D:(b % 2 + 1) * D],
                                 m.sel32[:, b // EB, (b % EB) * P:(b % EB + 1) * P], m.qt[:, half, b // EB, 0:D],
                                 start=True, stop=True)
            last.then_inc(m.s_qe, 1)

    def pe_scores(pe, a):
        pe.wait_ge(m.s_rhs, a.lin(1, 1))
        pe.wait_ge(m.s_selT, a.lin(2, 2))
        for t in range(PT):
            for b in range(EB):
                last = pe.matmul(bank[4][:, t * P:(t + 1) * P], m.selT[:, a.off % 2, t * EB + b, :],
                                 m.rhs[:, t * EB + b, :], start=(b == 0), stop=(b == EB - 1))
        last.then_inc(m.s_s, 1)

    def pe_hard(pe, a):
        pe.wait_ge(m.s_hard, a.lin(1, 1))
        for b in range(PB):
            last = pe.matmul(bank[5][:, b * 2 * HEADS:(b + 1) * 2 * HEADS],
                             m.sel[:, a.off % 2, b // EB, (b % EB) * P:(b % EB + 1) * P],
                             m.hard[:, b // EB, :], start=True, stop=True)
        last.then_inc(m.s_hg, 1)

    def pe_selT(pe, a, j):
        pe.wait_ge(m.s_sel, a.lin(2, 2))
        wait(pe, m.s_selT, a.lin(2, j))
        for b in range(8 * j, min(8 * j + 8, PB)):
            last = pe.transpose(bank[6][:, :].bitcast(F16)[:, (b % 8) * P:(b % 8 + 1) * P],
                                m.sel[:, a.off % 2, b // EB, (b % EB) * P:(b % EB + 1) * P], g.identh[:, :])
        last.then_inc(m.s_selps, 1)

    def pe_sum(pe, a):
        pe.wait_ge(m.s_vw, a.lin(1, 1))
        wait(pe, m.s_res, a.lin(PT, 0))
        for t in range(PT):
            for b in range(EB):
                last = pe.matmul(bank[7][:, t * D:(t + 1) * D], m.selT[:, a.off % 2, t * EB + b, :],
                                 m.vw[:, t * EB + b, :], start=(b == 0), stop=(b == EB - 1))
        last.then_inc(m.s_o, 1)

    def dve_lists(dve, a):
        half = a.off % 2
        dve.tensor_copy(m.colu[:, half, :], g.colu_all[:, bass.ds(a.lin(PB), PB)]).then_inc(m.s_colu, 1)
        wait(dve, m.s_selT, a.lin(2, -2))
        hold(dve)
        for k in range(PT):
            last = dve.tensor_scalar(m.sel[:, half, k, :], g.iota_e[:, :], g.start_all[:, bass.ds(a.lin(PT, k), 1)],
                                     g.end_all[:, bass.ds(a.lin(PT, k), 1)], ALU.max, ALU.min)
        last.then_inc(m.s_sel, 1)
        dve.wait_ge(m.s_sel, a.lin(2, 1))
        dve.tensor_tensor(m.sel[:, half, :, :], m.sel[:, half, :, :], g.iota_e[:, :].unsqueeze(1).to_broadcast([P, PT, EDGES]),
                          ALU.is_equal).then_inc(m.s_sel, 1)

    def dve_products(dve, a):
        half = a.off % 2
        dve.wait_ge(m.s_gather[half], gathered(a))
        for j in range(PB // 2):
            dve.wait_ge(m.s_qe, a.lin(PB // 2, j + 1))
            dve.tensor_tensor(m.prod[:, 2 * j:2 * j + 2, :], bank[ring(a, j)][:, :].rearrange("p (b d) -> p b d", d=D),
                              m.kv[:, half, 2 * j:2 * j + 2, 0:D], ALU.mult).then_inc(m.s_prod, 1)
        dve.wait_ge(m.s_prod, a.lin(PB // 2, PB // 2))
        dve.tensor_reduce(m.se[:, :, :], m.prod[:, :, :].rearrange("p b (h d) -> p b h d", d=HD), AX_X, ALU.add).then_inc(m.s_se, 1)
        for k in range(PT):
            deg = g.deg_all[:, bass.ds(a.lin(PT, k), 1)]
            dve.tensor_scalar(m.past[:, 0, k, :], g.iota_s[:, :], deg, -BIG, ALU.is_ge, ALU.mult)
            dve.scalar_tensor_tensor(m.past[:, 1, k, :], g.iota_s[:, :], deg, g.two_to[:, :], ALU.is_lt, ALU.mult).then_inc(m.s_past, 1)
        dve.wait_ge(m.s_se, a.lin(1, 1))
        dve.tensor_tensor(m.rhs[:, :, :].rearrange("p b (h s) -> p b h s", h=HEADS),
                          g.slot_all[:, bass.ds(a.lin(PB), PB), :].unsqueeze(2).to_broadcast([P, PB, HEADS, SLOTS]),
                          m.se[:, :, :].unsqueeze(3).to_broadcast([P, PB, HEADS, SLOTS]), ALU.mult).then_inc(m.s_rhs, 1)
        dve.wait_ge(m.s_past, a.lin(2, 2))
        dve.tensor_tensor(m.em[:, :, :].rearrange("p t (h s) -> p t h s", h=HEADS),
                          m.past[:, 0, :, :].unsqueeze(2).to_broadcast([P, PT, HEADS, SLOTS]),
                          m.qt[:, half, :, D:QW].unsqueeze(3).to_broadcast([P, PT, HEADS, SLOTS]), ALU.add).then_inc(m.s_em, 1)

    def gathered(a):
        c = 16 * PB * (a.off // 2 + 1)
        return c if a.i is None else a.i * (16 * PB) + c

    def dve_softmax(dve, a):
        def by_head(x):
            return x.rearrange("p t (h s) -> p t h s", h=HEADS)

        def over_slots(x):
            return x.unsqueeze(3).to_broadcast([P, PT, HEADS, SLOTS])

        att = by_head(m.att[:, :, :])
        dve.wait_ge(m.s_s, a.lin(1, 1))
        dve.wait_ge(m.s_em, a.lin(1, 1))
        dve.tensor_tensor(m.att[:, :, :], bank[4][:, 0:PT * P].rearrange("p (t n) -> p t n", n=P), m.em[:, :, :], ALU.add).then_inc(m.s_sm, 1)
        dve.wait_ge(m.s_sm, a.lin(6, 1))
        dve.tensor_reduce(m.mx[:, 0, :, :], att, AX_X, ALU.max).then_inc(m.s_sm, 1)
        dve.wait_ge(m.s_sm, a.lin(6, 2))
        dve.tensor_tensor(att, att, over_slots(m.mx[:, 0, :, :]), ALU.subtract).then_inc(m.s_sm, 1)
        dve.wait_ge(m.s_exp, a.lin(1, 1))
        dve.tensor_reduce(m.mx[:, 1, :, :], att, AX_X, ALU.add).then_inc(m.s_sm, 1)
        dve.wait_ge(m.s_sm, a.lin(6, 4))
        dve.reciprocal(m.mx[:, 2, :, :], m.mx[:, 1, :, :]).then_inc(m.s_sm, 1)
        dve.wait_ge(m.s_sm, a.lin(6, 5))
        dve.tensor_tensor(att, att, over_slots(m.mx[:, 2, :, :]), ALU.mult).then_inc(m.s_sm, 1)
        dve.wait_ge(m.s_sm, a.lin(6, 6))
        dve.tensor_reduce(m.mx[:, 3, :, :], att, AX_X, ALU.max).then_inc(m.s_top, 1)
        dve.wait_ge(m.s_top, a.lin(3, 1))
        dve.tensor_tensor(by_head(m.top[:, :, :]), att, over_slots(m.mx[:, 3, :, :]), ALU.is_equal).then_inc(m.s_top, 1)
        dve.wait_ge(m.s_top, a.lin(3, 2))
        dve.tensor_tensor(by_head(m.top[:, :, :]), by_head(m.top[:, :, :]),
                          m.past[:, 1, :, :].unsqueeze(2).to_broadcast([P, PT, HEADS, SLOTS]), ALU.mult).then_inc(m.s_top, 1)
        dve.wait_ge(m.s_top, a.lin(3, 3))
        with nc.allow_low_precision("whole numbers up to 255"):
            dve.tensor_reduce(m.hard[:, :, :], m.top[:, :, :].rearrange("p t (n s) -> p t n s", s=8), AX_X, ALU.add).then_inc(m.s_hard, 1)

    def dve_weights(dve, a):
        dve.wait_ge(m.s_hg, a.lin(1, 1))
        bits = bank[5][:, 0:PB * 2 * HEADS].rearrange("p (b h n) -> p b h n", h=HEADS, n=2)
        dve.tensor_scalar(m.high[:, :, :], bits[:, :, :, 1], 256.0, None, ALU.mult).then_inc(m.s_bits, 1)
        dve.wait_ge(m.s_bits, a.lin(4, 1))
        dve.tensor_tensor(m.code[:, :, :], m.high[:, :, :], bits[:, :, :, 0], ALU.add).then_inc(m.s_bits, 1)
        dve.wait_ge(m.s_bits, a.lin(4, 2))
        dve.tensor_tensor(m.code[:, :, :], m.code[:, :, :],
                          g.shift_all[:, bass.ds(a.lin(PB), PB)].unsqueeze(2).to_broadcast([P, PB, HEADS]),
                          ALU.logical_shift_right).then_inc(m.s_bits, 1)
        dve.wait_ge(m.s_bits, a.lin(4, 3))
        dve.tensor_scalar(m.code[:, :, :], m.code[:, :, :], 1, None, ALU.bitwise_and).then_inc(m.s_bits, 1)
        wait(dve, m.s_vw, a.lin(1, 0))
        dve.wait_ge(m.s_bits, a.lin(4, 4))
        dve.tensor_copy(m.w[:, :, :], m.code[:, :, :]).then_inc(m.s_w, 1)

    def dve_norm(dve, a):
        half = a.off % 2
        dve.wait_ge(m.s_o, a.lin(1, 1))
        dve.wait_ge(m.s_x1[half], count(a))
        wait(dve, m.s_out, a.lin(PT, 0))
        for k in range(PT):
            dve.scalar_tensor_tensor(m.y[:, k, :], bank[7][:, k * D:(k + 1) * D], 1.0 / HEADS, m.x1t[:, half, k, :],
                                     ALU.mult, ALU.add).then_inc(m.s_res, 1)
        dve.wait_ge(m.s_res, a.lin(PT, PT))
        for k in range(PT):
            last = dve.bn_stats(m.stats[:, k, :], m.y[:, k, :])
        last.then_inc(m.s_ln, 1)
        dve.wait_ge(m.s_ln, a.lin(3, 1))
        hold(dve)
        for k in range(PT):
            last = dve.bn_aggr(m.mv[:, k, :], m.stats[:, k, :])
        last.then_inc(m.s_ln, 1)
        dve.wait_ge(m.s_ln, a.lin(3, 2))
        dve.tensor_scalar(m.rs[:, 0, :], m.mv[:, :, 1], EPS, None, ALU.add).then_inc(m.s_ln, 1)

    def dve_apply(dve, a):
        dve.wait_ge(m.s_sqrt, a.lin(1, 1))
        dve.reciprocal(m.rs[:, 2, :], m.rs[:, 1, :]).then_inc(m.s_rstd, 1)
        wait(dve, m.s_store, a.lin(16, 0))
        dve.wait_ge(m.s_rstd, a.lin(1, 1))
        for k in range(PT):
            dve.tensor_scalar(m.o_sb[:, k, :], m.y[:, k, :], m.mv[:, k, 0:1], m.rs[:, 2, k:k + 1], ALU.subtract, ALU.mult).then_inc(m.s_out, 1)

    def steps(eng, body):
        for q in range(2):
            body(eng, At(None, q))
        with eng.Fori(0, (PAIRS - 2) // 2) as i:
            for half in range(2):
                body(eng, At(i, 2 + half))
        for q in range(PAIRS, PAIRS + 2):
            body(eng, At(None, q))

    def there(a, back):
        if a.i is None and not 0 <= a.off - back < PAIRS:
            return None
        return a.back(back)

    def sync(sp):
        def body(sp, a):
            sp_pair(sp, a, there(a, 0), there(a, 2))
        steps(sp, body)
        sp.wait_ge(m.s_store, 16 * PAIRS)

    def gpsimd(pool):
        pool.memset(m.kv[:, :, :, :], 0.0).then_inc(m.s_kvz, 1)
        pool.wait_ge(m.s_kvz, 1)
        pool_gather(pool, At(None, 0))

        def body(pool, a):
            if (b := there(a, 1)) is not None:
                pool_weigh(pool, b)
            if (b := there(a, -1)) is not None:
                pool_gather(pool, b)
        for q in range(2):
            body(pool, At(None, q))
        with pool.Fori(0, (PAIRS - 4) // 2) as i:
            for half in range(2):
                body(pool, At(i, 2 + half))
        for q in range(PAIRS - 2, PAIRS + 1):
            body(pool, At(None, q))

    def scalar(act):
        act_sel(act, At(None, 0))
        act_selT(act, At(None, 0))

        def body(act, a):
            if (b := there(a, 2)) is not None:
                act_sqrt(act, b)
            if (b := there(a, -1)) is not None:
                act_sel(act, b)
                act_selT(act, b)
            if (b := there(a, 0)) is not None:
                act_exp(act, b)
        for q in range(2):
            body(act, At(None, q))
        with act.Fori(0, (PAIRS - 4) // 2) as i:
            for half in range(2):
                body(act, At(i, 2 + half))
        for q in range(PAIRS - 2, PAIRS + 2):
            body(act, At(None, q))

    def tensor(pe):
        def body(pe, a):
            if (b := there(a, 0)) is not None:
                pe_queries(pe, b)
            if (b := there(a, 1)) is not None:
                pe_sum(pe, b)
            if (b := there(a, -1)) is not None:
                pe_selT(pe, b, 0)
            if (b := there(a, 0)) is not None:
                pe_scores(pe, b)
            if (b := there(a, -1)) is not None:
                pe_selT(pe, b, 1)
            if (b := there(a, 0)) is not None:
                pe_hard(pe, b)
        pe_selT(pe, At(None, 0), 0)
        pe_selT(pe, At(None, 0), 1)
        for q in range(2):
            body(pe, At(None, q))
        with pe.Fori(0, (PAIRS - 4) // 2) as i:
            for half in range(2):
                body(pe, At(i, 2 + half))
        for q in range(PAIRS - 2, PAIRS + 1):
            body(pe, At(None, q))

    def vector(dve):
        dve_lists(dve, At(None, 0))

        def body(dve, a):
            if (b := there(a, 1)) is not None:
                dve_weights(dve, b)
            if (b := there(a, -1)) is not None:
                dve_lists(dve, b)
            if (b := there(a, 2)) is not None:
                dve_norm(dve, b)
            if (b := there(a, 0)) is not None:
                dve_products(dve, b)
            if (b := there(a, 2)) is not None:
                dve_apply(dve, b)
            if (b := there(a, 0)) is not None:
                dve_softmax(dve, b)
        for q in range(3):
            body(dve, At(None, q))
        with dve.Fori(0, (PAIRS - 4) // 2) as i:
            for half in range(2):
                body(dve, At(i, 3 + half))
        for q in range(PAIRS - 1, PAIRS + 2):
            body(dve, At(None, q))

    return dict(sync=sync, gpsimd=gpsimd, scalar=scalar, tensor=tensor, vector=vector)


def dense_layers(nc, g, dr, m):
    def agg_sync(sp):
        sp.dma_start(m.x_all[:, :, :], dr.x.rearrange("(t p) d -> p t d", p=P)).then_inc(m.s_xall, 16)
        with sp.Fori(0, TILES) as t:
            sp.dma_start(m.adjt[:, :], dr.adj[bass.ds(t * P, P), :]).then_inc(m.s_adj, 16)
            sp.wait_ge(m.s_aggs, t + 1)
            g.hold(sp)
            sp.dma_start(dr.agg[bass.ds(t * P, P), :], m.agg_sb[:, :]).then_inc(m.s_aggst, 16)
            sp.wait_ge(m.s_aggst, t * 16 + 16)
            g.hold(sp)

    def agg_vector(dve):
        with dve.Fori(0, TILES) as t:
            dve.wait_ge(m.s_adj, t * 16 + 16)
            dve.tensor_scalar(m.mask[:, :], m.adjt[:, :], 0.0, None, ALU.is_gt).then_inc(m.s_mask, 1)
            dve.wait_ge(m.s_mask, t + 1)
            dve.tensor_reduce(m.deg[:, 0:1], m.mask[:, :], AX_X, ALU.add).then_inc(m.s_deg, 1)
            dve.wait_ge(m.s_deg, t * 3 + 1)
            dve.tensor_scalar(m.deg[:, 1:2], m.deg[:, 0:1], 1.0, None, ALU.max).then_inc(m.s_deg, 1)
            dve.wait_ge(m.s_deg, t * 3 + 2)
            dve.reciprocal(m.deg[:, 2:3], m.deg[:, 1:2]).then_inc(m.s_deg, 1)
            for b in range(4):
                dve.wait_ge(m.s_mT, t * 4 + (b + 1))
                dve.tensor_copy(m.maskT[:, 8 * b:8 * b + 8, :].rearrange("p c r -> p (c r)"),
                                g.bank[b][:, :].bitcast(BF16)).then_inc(m.s_mTc, 1)
            dve.wait_ge(m.s_agg, t + 1)
            dve.wait_ge(m.s_deg, t * 3 + 3)
            dve.tensor_scalar(m.agg_sb[:, :], g.bank[4][:, 0:D], m.deg[:, 2:3], None, ALU.mult).then_inc(m.s_aggs, 1)

    def agg_tensor(pe):
        pe.wait_ge(m.s_xall, 16)
        with pe.Fori(0, TILES) as t:
            pe.wait_ge(m.s_mask, t + 1)
            for b in range(4):
                for c in range(8):
                    last = pe.transpose(g.bank[b][:, :].bitcast(BF16)[:, c * P:(c + 1) * P],
                                        m.mask[:, (8 * b + c) * P:(8 * b + c + 1) * P], g.identb[:, :])
                last.then_inc(m.s_mT, 1)
            for b in range(4):
                pe.wait_ge(m.s_mTc, t * 4 + (b + 1))
                for c in range(8 * b, 8 * b + 8):
                    last = pe.matmul(g.bank[4][:, 0:D], m.maskT[:, c, :], m.x_all[:, c, :],
                                     start=(c == 0), stop=(c == TILES - 1))
            last.then_inc(m.s_agg, 1)

    def tail_sync(sp):
        with sp.Fori(0, TILES) as t:
            sp.dma_start(m.xa[:, 0, :], dr.x[bass.ds(t * P, P), :]).then_inc(m.s_xa, 16)
            sp.dma_start(m.xa[:, 1, :], dr.agg[bass.ds(t * P, P), :]).then_inc(m.s_xa, 16)
            sp.wait_ge(m.s_x1, t + 1)
            g.hold(sp)
            sp.dma_start(dr.x1[bass.ds(t * P, P), :], m.x1[:, :]).then_inc(m.s_tst, 16)
            sp.wait_ge(m.s_qkvc, t * 2 + 2)
            g.hold(sp)
            sp.dma_start(dr.qT.rearrange("(c p) n -> p c n", p=P)[:, :, bass.ds(t * P, P)], m.qkT[:, 0:2, :]).then_inc(m.s_tst, 16)
            sp.dma_start(dr.kT.rearrange("(c p) n -> p c n", p=P)[:, :, bass.ds(t * P, P)], m.qkT[:, 2:4, :]).then_inc(m.s_tst, 16)
            sp.dma_start(dr.v[bass.ds(t * P, P), :], m.v_sb[:, :]).then_inc(m.s_tst, 16)
            sp.wait_ge(m.s_tst, t * 64 + 64)
            g.hold(sp)

    def tail_tensor(pe):
        with pe.Fori(0, TILES) as t:
            pe.wait_ge(m.s_xa, t * 32 + 32)
            for i in range(2 * KC):
                last = pe.transpose(g.bank[0][:, i * P:(i + 1) * P], m.xa[:, i // KC, (i % KC) * P:(i % KC + 1) * P], g.ident[:, :])
            last.then_inc(m.s_xaT, 1)
            pe.wait_ge(m.s_xaTc, t + 1)
            for i in range(2 * KC):
                pe.matmul(g.bank[1][:, 0:D], m.xaT[:, i, :], g.w_fused[:, i, :], start=(i == 0), stop=False)
            pe.matmul(g.bank[1][:, 0:D], g.ones[:, :], g.b_fused[:, :], start=False, stop=True).then_inc(m.s_lin, 1)
            pe.wait_ge(m.s_x1, t + 1)
            for i in range(KC):
                last = pe.transpose(g.bank[2][:, i * P:(i + 1) * P], m.x1[:, i * P:(i + 1) * P], g.ident[:, :])
            last.then_inc(m.s_x1T, 1)
            pe.wait_ge(m.s_x1Tc, t + 1)
            for j in range(4):
                for k in range(KC):
                    pe.matmul(g.bank[3][:, j * P:(j + 1) * P], g.w_t[:, 2 + j // 2, k, (j % 2) * P:(j % 2 + 1) * P],
                              m.x1T[:, k, :], start=(k == 0), stop=(k == KC - 1))
            for k in range(KC):
                last = pe.matmul(g.bank[4][:, 0:D], m.x1T[:, k, :], g.w_t[:, 4, k, :], start=(k == 0), stop=(k == KC - 1))
            last.then_inc(m.s_qkv, 1)

    def tail_vector(dve):
        with dve.Fori(0, TILES) as t:
            dve.wait_ge(m.s_xaT, t + 1)
            dve.tensor_copy(m.xaT[:, :, :].rearrange("p c r -> p (c r)"), g.bank[0][:, :]).then_inc(m.s_xaTc, 1)
            dve.wait_ge(m.s_lin, t + 1)
            dve.scalar_tensor_tensor(m.y[:, :], g.bank[1][:, 0:D], 0.0, m.xa[:, 0, :], ALU.max, ALU.add).then_inc(m.s_ln, 1)
            dve.wait_ge(m.s_ln, t * 4 + 1)
            dve.bn_stats(m.st[:, 0:6], m.y[:, :]).then_inc(m.s_ln, 1)
            dve.wait_ge(m.s_ln, t * 4 + 2)
            g.hold(dve)
            dve.bn_aggr(m.st[:, 6:8], m.st[:, 0:6]).then_inc(m.s_ln, 1)
            dve.wait_ge(m.s_ln, t * 4 + 3)
            dve.tensor_scalar(m.st[:, 8:9], m.st[:, 7:8], EPS, None, ALU.add).then_inc(m.s_ln, 1)
            dve.wait_ge(m.s_sq, t * 2 + 1)
            dve.reciprocal(m.st[:, 10:11], m.st[:, 9:10]).then_inc(m.s_sq, 1)
            dve.wait_ge(m.s_sq, t * 2 + 2)
            dve.tensor_scalar(m.x1[:, :], m.y[:, :], m.st[:, 6:7], m.st[:, 10:11], ALU.subtract, ALU.mult).then_inc(m.s_x1, 1)
            dve.wait_ge(m.s_x1T, t + 1)
            dve.tensor_copy(m.x1T[:, :, :].rearrange("p c r -> p (c r)"), g.bank[2][:, 0:D]).then_inc(m.s_x1Tc, 1)
            dve.wait_ge(m.s_qkv, t + 1)
            dve.tensor_copy(m.qkT[:, :, :].rearrange("p c r -> p (c r)"), g.bank[3][:, :]).then_inc(m.s_qkvc, 1)
            dve.tensor_copy(m.v_sb[:, :], g.bank[4][:, 0:D]).then_inc(m.s_qkvc, 1)

    def tail_scalar(act):
        with act.Fori(0, TILES) as t:
            act.wait_ge(m.s_ln, t * 4 + 4)
            act.activation(m.st[:, 9:10], m.st[:, 8:9], ACT.Sqrt).then_inc(m.s_sq, 1)

    def att_sync(sp):
        with sp.Fori(0, HEADS) as h:
            sp.dma_start(m.kT_h[:, :], dr.kT[bass.ds(h * HD, HD), :]).then_inc(m.s_kv, 16)
            with nc.allow_non_contiguous_dma("a head's 128-byte rows of V"):
                sp.dma_start(m.v_h[:, :, :], dr.v.rearrange("(t p) d -> p t d", p=P)[:, :, bass.ds(h * HD, HD)]).then_inc(m.s_kv, 16)
            with sp.Fori(0, TILES) as t:
                n = h * TILES + t
                sp.dma_start(m.adjt[:, :], dr.adj[bass.ds(t * P, P), :]).then_inc(m.s_aq, 16)
                sp.dma_start(m.qT_h[:, :], dr.qT[bass.ds(h * HD, HD), bass.ds(t * P, P)]).then_inc(m.s_aq, 16)
                sp.wait_ge(m.s_oc, n + 1)
                g.hold(sp)
                with nc.allow_non_contiguous_dma("a head's 128-byte rows"):
                    sp.dma_start(dr.att[bass.ds(t * P, P), bass.ds(h * HD, HD)], m.o_sb[:, :]).then_inc(m.s_ost, 16)
                sp.wait_ge(m.s_ost, n * 16 + 16)
                g.hold(sp)

    def att_tensor(pe):
        with pe.Fori(0, HEADS) as h:
            pe.wait_ge(m.s_kv, h * 32 + 32)
            g.hold(pe)
            with pe.Fori(0, TILES) as t:
                n = h * TILES + t
                pe.wait_ge(m.s_aq, n * 32 + 32)
                pe.matmul(g.bank[4][:, 0:1], m.qT_h[:, :], g.we_col[:, :], start=True, stop=True).then_inc(m.s_en, 1)
                for c in range(8):
                    if c >= 4:
                        pe.wait_ge(m.s_scc, n * 8 + (c - 3))
                    pe.matmul(g.bank[c % 4][:, :], m.qT_h[:, :], m.kT_h[:, c * 512:(c + 1) * 512],
                              start=True, stop=True).then_inc(m.s_sc, 1)
                pe.wait_ge(m.s_hard, n + 1)
                for b in range(4):
                    if b >= 2:
                        pe.wait_ge(m.s_hTc, n * 4 + (b - 1))
                    for c in range(8):
                        last = pe.transpose(g.bank[5 + b % 2][:, :].bitcast(BF16)[:, c * P:(c + 1) * P],
                                            m.hard[:, (8 * b + c) * P:(8 * b + c + 1) * P], g.identb[:, :])
                    last.then_inc(m.s_hT, 1)
                pe.wait_ge(m.s_hTc, n * 4 + 4)
                for c in range(TILES):
                    last = pe.matmul(g.bank[7][:, 0:HD], m.maskT[:, c, :], m.v_h[:, c, :],
                                     start=(c == 0), stop=(c == TILES - 1))
                last.then_inc(m.s_o, 1)

    def att_vector(dve):
        with dve.Fori(0, HEADS) as h:
            with dve.Fori(0, TILES) as t:
                n = h * TILES + t
                dve.wait_ge(m.s_aq, n * 32 + 32)
                dve.tensor_scalar(m.mask[:, :], m.adjt[:, :], 0.0, None, ALU.is_gt).then_inc(m.s_m2, 1)
                dve.wait_ge(m.s_m2, n * 3 + 1)
                dve.tensor_scalar(m.madd[:, :], m.mask[:, :], 1.0, BIG, ALU.subtract, ALU.mult).then_inc(m.s_m2, 1)
                dve.wait_ge(m.s_en, n + 1)
                dve.tensor_scalar(m.en[:, :], g.bank[4][:, 0:1], g.be_col[:, :], None, ALU.add).then_inc(m.s_m2, 1)
                dve.wait_ge(m.s_m2, n * 3 + 3)
                for c in range(8):
                    dve.wait_ge(m.s_sc, n * 8 + (c + 1))
                    dve.tensor_scalar(m.sc[:, c * 512:(c + 1) * 512], g.bank[c % 4][:, :], SCALING, m.en[:, :],
                                      ALU.mult, ALU.add).then_inc(m.s_scc, 1)
                dve.wait_ge(m.s_scc, n * 8 + 8)
                dve.tensor_tensor(m.sc[:, :], m.sc[:, :], m.madd[:, :], ALU.add).then_inc(m.s_smx, 1)
                dve.wait_ge(m.s_smx, n * 6 + 1)
                dve.tensor_reduce(m.sm[:, 0:1], m.sc[:, :], AX_X, ALU.max, negate=True).then_inc(m.s_smx, 1)
                dve.wait_ge(m.s_exp, n + 1)
                dve.reciprocal(m.sm[:, 2:3], m.sm[:, 1:2]).then_inc(m.s_smx, 1)
                dve.wait_ge(m.s_smx, n * 6 + 3)
                dve.tensor_scalar(m.sc[:, :], m.sc[:, :], m.sm[:, 2:3], None, ALU.mult).then_inc(m.s_smx, 1)
                dve.wait_ge(m.s_smx, n * 6 + 4)
                dve.tensor_reduce(m.sm[:, 3:4], m.sc[:, :], AX_X, ALU.max).then_inc(m.s_smx, 1)
                dve.wait_ge(m.s_smx, n * 6 + 5)
                dve.scalar_tensor_tensor(m.hard[:, :], m.sc[:, :], m.sm[:, 3:4], m.mask[:, :], ALU.is_equal, ALU.mult).then_inc(m.s_hard, 1)
                dve.tensor_scalar(m.sm[:, 4:5], m.sm[:, 3:4], 1.0, None, ALU.mult).then_inc(m.s_smx, 1)
                for b in range(4):
                    dve.wait_ge(m.s_hT, n * 4 + (b + 1))
                    dve.tensor_copy(m.maskT[:, 8 * b:8 * b + 8, :].rearrange("p c r -> p (c r)"),
                                    g.bank[5 + b % 2][:, :].bitcast(BF16)).then_inc(m.s_hTc, 1)
                dve.wait_ge(m.s_o, n + 1)
                dve.tensor_scalar(m.o_sb[:, :], g.bank[7][:, 0:HD], 1.0 / HEADS, None, ALU.mult).then_inc(m.s_oc, 1)

    def att_scalar(act):
        with act.Fori(0, HEADS) as h:
            with act.Fori(0, TILES) as t:
                n = h * TILES + t
                act.wait_ge(m.s_smx, n * 6 + 2)
                act.activation(m.sc[:, :], m.sc[:, :], ACT.Exp, bias=m.sm[:, 0:1], accum_out=m.sm[:, 1:2]).then_inc(m.s_exp, 1)

    def fin_sync(sp):
        with sp.Fori(0, TILES) as t:
            sp.dma_start(m.xa[:, 0, :], dr.x1[bass.ds(t * P, P), :]).then_inc(m.s_fl, 16)
            sp.dma_start(m.xa[:, 1, :], dr.att[bass.ds(t * P, P), :]).then_inc(m.s_fl, 16)
            sp.wait_ge(m.s_fy, t + 1)
            g.hold(sp)
            sp.dma_start(dr.out[bass.ds(t * P, P), :], m.x1[:, :]).then_inc(m.s_fst, 16)
            sp.wait_ge(m.s_fst, t * 16 + 16)
            g.hold(sp)

    def fin_vector(dve):
        with dve.Fori(0, TILES) as t:
            dve.wait_ge(m.s_fl, t * 32 + 32)
            dve.tensor_tensor(m.y[:, :], m.xa[:, 0, :], m.xa[:, 1, :], ALU.add).then_inc(m.s_fln, 1)
            dve.wait_ge(m.s_fln, t * 4 + 1)
            dve.bn_stats(m.st[:, 0:6], m.y[:, :]).then_inc(m.s_fln, 1)
            dve.wait_ge(m.s_fln, t * 4 + 2)
            g.hold(dve)
            dve.bn_aggr(m.st[:, 6:8], m.st[:, 0:6]).then_inc(m.s_fln, 1)
            dve.wait_ge(m.s_fln, t * 4 + 3)
            dve.tensor_scalar(m.st[:, 8:9], m.st[:, 7:8], EPS, None, ALU.add).then_inc(m.s_fln, 1)
            dve.wait_ge(m.s_fsq, t * 2 + 1)
            dve.reciprocal(m.st[:, 10:11], m.st[:, 9:10]).then_inc(m.s_fsq, 1)
            dve.wait_ge(m.s_fsq, t * 2 + 2)
            dve.tensor_scalar(m.x1[:, :], m.y[:, :], m.st[:, 6:7], m.st[:, 10:11], ALU.subtract, ALU.mult).then_inc(m.s_fy, 1)

    def fin_scalar(act):
        with act.Fori(0, TILES) as t:
            act.wait_ge(m.s_fln, t * 4 + 4)
            act.activation(m.st[:, 9:10], m.st[:, 8:9], ACT.Sqrt).then_inc(m.s_fsq, 1)


    def sync(sp):
        agg_sync(sp)
        tail_sync(sp)
        att_sync(sp)
        fin_sync(sp)

    def tensor(pe):
        agg_tensor(pe)
        tail_tensor(pe)
        att_tensor(pe)

    def vector(dve):
        agg_vector(dve)
        tail_vector(dve)
        att_vector(dve)
        fin_vector(dve)

    def scalar(act):
        tail_scalar(act)
        att_scalar(act)
        fin_scalar(act)

    return dict(sync=sync, gpsimd=None, scalar=scalar, tensor=tensor, vector=vector)


class Names:
    pass


def gnn_kernel(nc, x, adj, W_self, b_self, W_nb, b_nb, W_comb, b_comb, WQ, WK, WV, we, be, out):
    ctx = ExitStack()
    with ctx:
        def dram(name, shape):
            return nc.dram_tensor(name, shape, F32, kind="Internal").ap()

        dr = Names()
        dr.x, dr.adj, dr.W_self, dr.b_self, dr.W_nb, dr.b_nb = x, adj, W_self, b_self, W_nb, b_nb
        dr.W_comb, dr.b_comb, dr.WQ, dr.WK, dr.WV, dr.we, dr.be, dr.out = W_comb, b_comb, WQ, WK, WV, we, be, out
        dr.x1, dr.q, dr.kv = dram("x1_d", [N, D]), dram("q_d", [N, QW]), dram("kv_d", [N, KVW])
        dr.agg, dr.qT, dr.kT, dr.v, dr.att = (dram("agg_d", [N, D]), dram("qT_d", [D, N]), dram("kT_d", [D, N]),
                                              dram("v_d", [N, D]), dram("att_d", [N, D]))

        def sb(stack, name, shape, dt=F32):
            return stack.enter_context(nc.sbuf_tensor(name, shape, dt))

        def sem(name):
            return ctx.enter_context(nc.semaphore(name))

        g = Names()
        g.ident = sb(ctx, "g_ident", [P, P])
        g.identb = sb(ctx, "g_identb", [P, P], BF16)
        g.identh = sb(ctx, "g_identh", [P, P], F16)
        g.two_to = sb(ctx, "g_two_to", [P, SLOTS])
        g.ones = sb(ctx, "g_ones", [1, P])
        g.ones_col = sb(ctx, "g_ones_col", [P, 1])
        g.below = sb(ctx, "g_below", [P, P], F16)
        g.iota_e = sb(ctx, "g_iota_e", [P, EDGES], F16)
        g.iota_s = sb(ctx, "g_iota_s", [P, SLOTS])
        g.iota_r1 = sb(ctx, "g_iota_r1", [P, P])
        g.edge_no = sb(ctx, "g_edge_no", [P, GB])
        g.w_t = sb(ctx, "g_w_t", [P, 5, KC, D])
        g.w_fused = sb(ctx, "g_w_fused", [P, 2 * KC, D])
        g.w_en = sb(ctx, "g_w_en", [P, KC, HEADS])
        g.b_fused = sb(ctx, "g_b_fused", [1, D])
        g.b_col = sb(ctx, "g_b_col", [P, 2, KC])
        g.bc_row = sb(ctx, "g_bc_row", [1, D])
        g.we_col = sb(ctx, "g_we_col", [HD, 1])
        g.we_heads = sb(ctx, "g_we_heads", [P, KC, HEADS])
        g.be_col = sb(ctx, "g_be_col", [P, 1])
        g.be_row = sb(ctx, "g_be_row", [1, HEADS])
        g.deg_all = sb(ctx, "g_deg_all", [P, TILES])
        g.start_all = sb(ctx, "g_start_all", [P, TILES])
        g.end_all = sb(ctx, "g_end_all", [P, TILES])
        g.full_all = sb(ctx, "g_full_all", [P, TILES, CHUNKS])
        g.slot_all = sb(ctx, "g_slot_all", [P, TILES * EB, SLOTS], BF16)
        g.shift_all = sb(ctx, "g_shift_all", [P, TILES * EB], I32)
        g.colu_all = sb(ctx, "g_colu_all", [P, TILES * EB], U32)
        g.over = sb(ctx, "g_over", [P, 8])
        g.flag = sb(ctx, "g_flag", [1, 1], I32)
        g.bank = [ctx.enter_context(nc.psum_tensor(f"bank{i}", [P, 512], F32)) for i in range(8)]
        g.held = {}

        def hold(eng):
            name = str(eng.engine)
            if name not in g.held:
                g.held[name] = ctx.enter_context(nc.semaphore(f"held{len(g.held)}"))
            eng.sem_inc(g.held[name], 1)

        g.hold = hold
        g.N_CONST = 15 + SLOTS

        def constants(pool, s_const):
            pool.memset(g.ident[:, :], 0.0).then_inc(s_const, 1)
            pool.memset(g.identb[:, :], 0.0).then_inc(s_const, 1)
            pool.memset(g.identh[:, :], 0.0).then_inc(s_const, 1)
            for s in range(SLOTS):
                pool.memset(g.two_to[:, s:s + 1], float(1 << (s % 8))).then_inc(s_const, 1)
            pool.memset(g.below[:, :], 1.0).then_inc(s_const, 1)
            pool.memset(g.ones[:, :], 1.0).then_inc(s_const, 1)
            pool.memset(g.ones_col[:, :], 1.0).then_inc(s_const, 1)
            pool.memset(g.we_heads[:, :, :], 0.0).then_inc(s_const, 1)
            pool.wait_ge(s_const, 7 + SLOTS)
            for eye in (g.ident, g.identb, g.identh):
                pool.affine_select(out=eye[:, :], in_=eye[:, :], compare_op=ALU.not_equal, fill=1.0, base=0,
                                   pattern=[[-1, P]], channel_multiplier=1).then_inc(s_const, 1)
            pool.affine_select(out=g.below[:, :], in_=g.below[:, :], compare_op=ALU.is_gt, fill=0.0, base=0,
                               pattern=[[1, P]], channel_multiplier=-1).then_inc(s_const, 1)
            loose = dict(allow_small_or_imprecise_dtypes=True)
            pool.iota(g.iota_e[:, :], [[1, EDGES]], base=0, channel_multiplier=0, **loose).then_inc(s_const, 1)
            pool.iota(g.iota_s[:, :], [[1, SLOTS]], base=0, channel_multiplier=0, **loose).then_inc(s_const, 1)
            pool.iota(g.iota_r1[:, :], [[1, P]], base=1, channel_multiplier=0, **loose).then_inc(s_const, 1)
            pool.iota(g.edge_no[:, :], [[0, GT], [P, EB]], base=0, channel_multiplier=1, **loose).then_inc(s_const, 1)

        g.constants = constants
        sparse_layer1(nc, g, dr)

        m = Names()
        with ExitStack() as stack:
            m.qt = sb(stack, "p2_qt", [P, 2, PT, QW])
            m.x1t = sb(stack, "p2_x1t", [P, 2, PT, D])
            m.colu = sb(stack, "p2_colu", [P, 2, PB], U32)
            m.kv = sb(stack, "p2_kv", [P, 2, PB, KVW])
            m.vw = sb(stack, "p2_vw", [P, PB, D])
            m.sel = sb(stack, "p2_sel", [P, 2, PT, EDGES], F16)
            m.sel32 = sb(stack, "p2_sel32", [P, PT, EDGES])
            m.selT = sb(stack, "p2_selT", [P, 2, PB, P])
            m.prod = sb(stack, "p2_prod", [P, PB, D])
            m.se = sb(stack, "p2_se", [P, PB, HEADS])
            m.rhs = sb(stack, "p2_rhs", [P, PB, P])
            m.past = sb(stack, "p2_past", [P, 2, PT, SLOTS])
            m.em = sb(stack, "p2_em", [P, PT, P])
            m.att = sb(stack, "p2_att", [P, PT, P])
            m.mx = sb(stack, "p2_mx", [P, 4, PT, HEADS])
            m.top = sb(stack, "p2_top", [P, PT, P])
            m.hard = sb(stack, "p2_hard", [P, PT, 2 * HEADS], F16)
            m.high = sb(stack, "p2_high", [P, PB, HEADS])
            m.code = sb(stack, "p2_code", [P, PB, HEADS], I32)
            m.w = sb(stack, "p2_w", [P, PB, HEADS])
            m.y = sb(stack, "p2_y", [P, PT, D])
            m.stats = sb(stack, "p2_stats", [P, PT, 6])
            m.mv = sb(stack, "p2_mv", [P, PT, 2])
            m.rs = sb(stack, "p2_rs", [P, 3, PT])
            m.o_sb = sb(stack, "p2_o_sb", [P, PT, D])
        m.s_em = sem("p2_em")
        m.s_res = sem("p2_res")
        m.s_out = sem("p2_out")
        m.s_store = sem("p2_store")
        m.s_kvz = sem("p2_kvz")
        m.s_colu = sem("p2_colu")
        m.s_prod = sem("p2_prod")
        m.s_vw = sem("p2_vw")
        m.s_w = sem("p2_w")
        m.s_o = sem("p2_o")
        m.s_sel = sem("p2_sel")
        m.s_sel32 = sem("p2_sel32")
        m.s_selT = sem("p2_selT")
        m.s_qe = sem("p2_qe")
        m.s_sm = sem("p2_sm")
        m.s_exp = sem("p2_exp")
        m.s_ln = sem("p2_ln")
        m.s_sqrt = sem("p2_sqrt")
        m.s_rhs = sem("p2_rhs")
        m.s_s = sem("p2_s")
        m.s_hard = sem("p2_hard")
        m.s_hg = sem("p2_hg")
        m.s_se = sem("p2_se")
        m.s_past = sem("p2_past")
        m.s_top = sem("p2_top")
        m.s_bits = sem("p2_bits")
        m.s_selps = sem("p2_selps")
        m.s_rstd = sem("p2_rstd")
        m.s_q, m.s_x1, m.s_gather = ([ctx.enter_context(nc.semaphore(f"p2_{n}{half}")) for half in range(2)]
                                     for n in ("s_q", "s_x1", "s_gather"))
        d = Names()
        with ExitStack() as stack:
            d.x_all = sb(stack, "d_x_all", [P, TILES, D])
            d.adjt = sb(stack, "d_adjt", [P, N], I32)
            d.mask = sb(stack, "d_mask", [P, N], BF16)
            d.maskT = sb(stack, "d_maskT", [P, TILES, P])
            d.deg = sb(stack, "d_deg", [P, 4])
            d.agg_sb = sb(stack, "d_agg_sb", [P, D])
            d.xa = sb(stack, "d_xa", [P, 2, D])
            d.xaT = sb(stack, "d_xaT", [P, 2 * KC, P])
            d.y = sb(stack, "d_y", [P, D])
            d.st = sb(stack, "d_st", [P, 12])
            d.x1 = sb(stack, "d_x1", [P, D])
            d.x1T = sb(stack, "d_x1T", [P, KC, P])
            d.qkT = sb(stack, "d_qkT", [P, 4, P])
            d.v_sb = sb(stack, "d_v_sb", [P, D])
            d.kT_h = sb(stack, "d_kT_h", [HD, N])
            d.v_h = sb(stack, "d_v_h", [P, TILES, HD])
            d.qT_h = sb(stack, "d_qT_h", [HD, P])
            d.sc = sb(stack, "d_sc", [P, N])
            d.madd = sb(stack, "d_madd", [P, N], BF16)
            d.hard = sb(stack, "d_hard", [P, N], BF16)
            d.en = sb(stack, "d_en", [P, 1])
            d.sm = sb(stack, "d_sm", [P, 8])
            d.o_sb = sb(stack, "d_o_sb", [P, HD])
        d.s_adj = sem("d_adj")
        d.s_agg = sem("d_agg")
        d.s_aggs = sem("d_aggs")
        d.s_aggst = sem("d_aggst")
        d.s_aq = sem("d_aq")
        d.s_deg = sem("d_deg")
        d.s_en = sem("d_en")
        d.s_exp = sem("d_exp")
        d.s_fl = sem("d_fl")
        d.s_fln = sem("d_fln")
        d.s_fsq = sem("d_fsq")
        d.s_fst = sem("d_fst")
        d.s_fy = sem("d_fy")
        d.s_hT = sem("d_hT")
        d.s_hTc = sem("d_hTc")
        d.s_hard = sem("d_hard")
        d.s_kv = sem("d_kv")
        d.s_lin = sem("d_lin")
        d.s_ln = sem("d_ln")
        d.s_m2 = sem("d_m2")
        d.s_mT = sem("d_mT")
        d.s_mTc = sem("d_mTc")
        d.s_mask = sem("d_mask")
        d.s_o = sem("d_o")
        d.s_oc = sem("d_oc")
        d.s_ost = sem("d_ost")
        d.s_qkv = sem("d_qkv")
        d.s_qkvc = sem("d_qkvc")
        d.s_sc = sem("d_sc")
        d.s_scc = sem("d_scc")
        d.s_smx = sem("d_smx")
        d.s_sq = sem("d_sq")
        d.s_tst = sem("d_tst")
        d.s_x1 = sem("d_x1")
        d.s_x1T = sem("d_x1T")
        d.s_x1Tc = sem("d_x1Tc")
        d.s_xa = sem("d_xa")
        d.s_xaT = sem("d_xaT")
        d.s_xaTc = sem("d_xaTc")
        d.s_xall = sem("d_xall")
        fast, slow = sparse_layer2(nc, g, dr, m), dense_layers(nc, g, dr, d)

        with nc.Block() as block:
            def either(eng, part):
                over = eng.value_load(g.flag[0:1, 0:1], min_val=0, max_val=3)
                with eng.If(over > 0):
                    if slow[part] is not None:
                        slow[part](eng)
                with eng.Else():
                    fast[part](eng)

            @block.sync
            def _(sp):
                either(sp, "sync")

            @block.gpsimd
            def _(pool):
                either(pool, "gpsimd")

            @block.scalar
            def _(act):
                either(act, "scalar")

            @block.tensor
            def _(pe):
                either(pe, "tensor")

            @block.vector
            def _(dve):
                either(dve, "vector")


_INS = ['x', 'adj', 'L0_gnn_W_self', 'L0_gnn_b_self', 'L0_gnn_W_nb', 'L0_gnn_b_nb', 'L0_gnn_W_comb', 'L0_gnn_b_comb',
        'L1_gnn_WQ', 'L1_gnn_WK', 'L1_gnn_WV', 'L1_gnn_we', 'L1_gnn_be']


def kernel(**inputs):
    import numpy as _np
    import concourse.bacc as _bacc
    from concourse import mybir as _mybir
    from concourse.bass_utils import run_bass_kernel_spmd as _run

    nc = _bacc.Bacc("TRN2", target_bir_lowering=False, num_devices=1)
    arrays, args = {}, []
    for name in _INS:
        a = _np.ascontiguousarray(inputs[name])
        arrays[f"in_{name}"] = a
        args.append(nc.dram_tensor(f"in_{name}", a.shape, _mybir.dt.from_np(a.dtype), kind="ExternalInput").ap())
    args.append(nc.dram_tensor("out_0", (N, D), _mybir.dt.float32, kind="ExternalOutput").ap())
    gnn_kernel(nc, *args)
    return _run(nc, [arrays], core_ids=[0]).results[0]["out_0"]
```

```python
from contextlib import ExitStack

import concourse.bass as bass
from concourse import mybir

ALU = mybir.AluOpType
ACT = mybir.ActivationFunctionType
F32 = mybir.dt.float32
F16 = mybir.dt.float16
I32 = mybir.dt.int32
U32 = mybir.dt.uint32
U16 = mybir.dt.uint16
BF16 = mybir.dt.bfloat16
AX_X = mybir.AxisListType.X
AX_XY = mybir.AxisListType.XY

P = 128
N = 4096
D = 256
HEADS = 8
HD = D // HEADS
TILES = N // P
KC = D // P
SCALING = HD ** -0.5
EPS = 1e-5
BIG = 1e30

CHUNKS = 8
CW = N // CHUNKS
SLOTS = 16
EB = 6
EDGES = EB * P
HALF = N // 2
SKIP = 2 * N

GT = 4
GROUPS = TILES // GT
GB = GT * EB
PT = 2
PAIRS = TILES // PT
PB = PT * EB
QW = D + HEADS
KVW = 2 * D
INFO = 2 + SLOTS


class At:

    def __init__(self, i, off, step=2):
        self.i, self.off, self.step = i, off, step

    def lin(self, a, b=0):
        c = a * self.off + b
        return c if self.i is None else self.i * (a * self.step) + c

    def back(self, n):
        return At(self.i, self.off - n, self.step)


def wait(eng, sem, value):
    if not isinstance(value, int) or value > 0:
        eng.wait_ge(sem, value)


def sparse_layer1(nc, g, dr):
    ctx = ExitStack()
    with ctx:
        def sb(name, shape, dt=F32):
            return ctx.enter_context(nc.sbuf_tensor(name, shape, dt))

        def sem(name):
            return ctx.enter_context(nc.semaphore(name))

        bank = g.bank
        adjt = g.adjt
        mk = sb("p1_mk", [P, 2, N], BF16)
        key = sb("p1_key", [P, N], U16)
        col1 = sb("p1_col1", [P, N], U16)
        found = sb("p1_found", [P, GT, CHUNKS, 8])
        rest = sb("p1_rest", [P, CHUNKS * 8])
        top = sb("p1_top", [P, GT, SLOTS])
        nz = sb("p1_nz", [P, GT, CHUNKS * 8], BF16)
        deg_h = sb("p1_deg_h", [P, GT], F16)
        rdeg = sb("p1_rdeg", [P, 2, GT])
        deg1 = sb("p1_deg1", [P, GT])
        deg_half = sb("p1_deg_half", [P, GT])
        info = sb("p1_info", [P, GT, INFO], F16)
        sel = sb("p1_sel", [P, GT, EDGES], F16)
        selT = sb("p1_selT", [P, GB, P])
        slot_e = sb("p1_slot_e", [P, GB])
        cs = sb("p1_cs", [P, GB, SLOTS], F16)
        colr = sb("p1_colr", [P, GB])
        unused = sb("p1_unused", [P, GB])
        colu = sb("p1_colu", [P, 2, GB], U32)
        xg = sb("p1_xg", [P, GT, EB, D])
        xt = sb("p1_xt", [P, 2, GT, D])
        agg = sb("p1_agg", [P, GT, D])
        xaT = sb("p1_xaT", [P, 2, 2 * KC, P])
        y = agg
        stats = sb("p1_stats", [P, GT, 6])
        mv = sb("p1_mv", [P, GT, 2])
        rs = sb("p1_rs", [P, 3, GT])
        x1 = sb("p1_x1", [P, GT, D])
        x1T = sb("p1_x1T", [P, GT, KC, P])
        q_sb = sb("p1_q_sb", [P, GT, QW])
        kv_sb = sb("p1_kv_sb", [P, GT, KVW])
        w_raw = xg[:, 0:2, :, :].rearrange("p a b d -> p (a b) d")[:, 0:10, :].rearrange("p (i c) d -> p i c d", c=KC)
        w_comb = x1

        const_ready = sem("p1_const_ready")
        weights_loaded = sem("p1_weights_loaded")
        we_loaded = sem("p1_we_loaded")
        weights_transposed = sem("p1_weights_transposed")
        weightsT_copied = sem("p1_weightsT_copied")
        fused_ready = sem("p1_fused_ready")
        fused_copied = sem("p1_fused_copied")
        gathered_zeroed = sem("p1_gathered_zeroed")
        adj_loaded = [sem(f"p1_adj_loaded_{k}") for k in range(GT)]
        x_loaded = [sem(f"p1_x_loaded_{k}") for k in range(2)]
        x_gathered = [sem(f"p1_x_gathered_{k}") for k in range(GT)]
        mask_ready = sem("p1_mask_ready")
        keys_ready = sem("p1_keys_ready")
        found_ready = sem("p1_found_ready")
        top_steps = sem("p1_top_steps")
        degree_ready = sem("p1_degree_ready")
        starts_ready = sem("p1_starts_ready")
        rstd_ready = sem("p1_rstd_ready")
        info_ready = sem("p1_info_ready")
        sel_steps = sem("p1_sel_steps")
        edge_info_ready = sem("p1_edge_info_ready")
        index_steps = sem("p1_index_steps")
        indices_ready = sem("p1_indices_ready")
        selT_copied = sem("p1_selT_copied")
        sums_ready = sem("p1_sums_ready")
        means_ready = sem("p1_means_ready")
        operands_transposed = sem("p1_operands_transposed")
        operandsT_copied = sem("p1_operandsT_copied")
        linear_ready = sem("p1_linear_ready")
        y_ready = sem("p1_y_ready")
        norm_steps = sem("p1_norm_steps")
        sqrt_ready = sem("p1_sqrt_ready")
        x1_ready = sem("p1_x1_ready")
        x1_transposed = sem("p1_x1_transposed")
        x1T_copied = sem("p1_x1T_copied")
        qkv_ready = sem("p1_qkv_ready")
        qkv_copied = sem("p1_qkv_copied")
        slot_ready = sem("p1_slot_ready")
        sel_transposed = sem("p1_sel_transposed")
        x1_stored = sem("p1_x1_stored")
        tables_stored = sem("p1_tables_stored")
        flag_steps = sem("p1_flag_steps")

        def hold(eng):
            g.hold(eng)

        iota_e = g.iota_e

        def group(a, ahead):
            if a.i is None and not 0 <= a.off + ahead < GROUPS:
                return None
            return a.back(-ahead)

        def steps(eng, step):
            for q in range(3):
                step(eng, At(None, q))
            with eng.Fori(0, (GROUPS - 4) // 2) as i:
                for half in range(2):
                    step(eng, At(i, 3 + half))
            for q in range(GROUPS - 1, GROUPS + 2):
                step(eng, At(None, q))

        with nc.Block() as block:

            def sp_group(sp, a, tiles=range(GT)):
                for k in tiles:
                    wait(sp, mask_ready, a.lin(GT, k + 1 - GT))
                    if a.i is not None:
                        hold(sp)
                    sp.dma_start(adjt[:, k, :], dr.adj[bass.ds(a.lin(GT * P, k * P), P), :]).then_inc(adj_loaded[k], 16)

            @block.sync
            def _(sp):
                sp_group(sp, At(None, 0), (0, 1))
                for i, w in enumerate((dr.W_self, dr.W_nb, dr.WQ, dr.WK, dr.WV)):
                    sp.dma_start(w_raw[:, i, :, :], w.rearrange("(c p) n -> p c n", p=P)).then_inc(weights_loaded, 16)
                sp.dma_start(w_comb[:, :, :], dr.W_comb.rearrange("(c p) n -> p c n", p=P)).then_inc(weights_loaded, 16)
                with nc.allow_non_contiguous_dma("bias columns, 1 KB each"):
                    sp.dma_start(g.b_col[:, 0, :], dr.b_self.rearrange("(c p) -> p c", p=P)).then_inc(weights_loaded, 16)
                    sp.dma_start(g.b_col[:, 1, :], dr.b_nb.rearrange("(c p) -> p c", p=P)).then_inc(weights_loaded, 16)
                    sp.dma_start(g.we_col[:, :], dr.we.rearrange("a d -> d a")).then_inc(weights_loaded, 16)
                sp.dma_start(g.bc_row[:, :], dr.b_comb.rearrange("(a n) -> a n", a=1)).then_inc(weights_loaded, 16)
                sp.dma_start(g.be_col[:, :], dr.be.rearrange("(a n) -> a n", a=1).broadcast_to([P, 1])).then_inc(weights_loaded, 16)
                sp_group(sp, At(None, 0), (2, 3))
                sp.wait_ge(const_ready, g.N_CONST)
                with nc.allow_non_contiguous_dma("a column of 32 numbers"):
                    for h in range(HEADS):
                        sp.dma_start(g.we_heads[(h % 4) * HD:(h % 4 + 1) * HD, h // 4, h:h + 1], dr.we.rearrange("a d -> d a")).then_inc(we_loaded, 16)
                sp_group(sp, At(None, 1))
                with sp.Fori(1, GROUPS // 2) as i:
                    for half in range(2):
                        sp_group(sp, At(i, half))

            def pool_group(pool, a):
                for k in range(GT):
                    if k == 0:
                        pool.wait_ge(indices_ready, a.lin(1, 1))
                    wait(pool, sums_ready, a.lin(GT, k + 1 - GT))
                    if a.i is not None:
                        hold(pool)
                    for b in range(EB):
                        pool.indirect_dma_start(out=xg[:, k, b, :], out_offset=None, in_=dr.x,
                                                in_offset=bass.IndirectOffsetOnAxis(ap=colu[:, a.off % 2, k * EB + b:k * EB + b + 1], axis=0),
                                                bounds_check=N - 1, oob_is_err=False).then_inc(x_gathered[k], 16)

            @block.gpsimd
            def _(pool):
                g.constants(pool, const_ready)
                pool.iota(col1[:, :], [[1, N]], base=1, channel_multiplier=0,
                          allow_small_or_imprecise_dtypes=True).then_inc(const_ready, 1)
                pool.iota(info[:, :, 1], [[0, GT]], base=1, channel_multiplier=1,
                          allow_small_or_imprecise_dtypes=True).then_inc(const_ready, 1)
                pool.wait_ge(weights_transposed, 5)
                pool.wait_ge(fused_ready, 1)
                pool.memset(xg[:, :, :, :], 0.0).then_inc(gathered_zeroed, 1)
                pool.wait_ge(gathered_zeroed, 1)
                pool_group(pool, At(None, 0))
                with pool.Fori(0, (GROUPS - 2) // 2) as i:
                    for half in range(2):
                        pool_group(pool, At(i, half + 1))
                pool_group(pool, At(None, GROUPS - 1))
                pool.wait_ge(mask_ready, TILES)
                pool.memset(g.kv, 0.0).then_inc(gathered_zeroed, 1)

            def act_mask(act, a, k):
                act.wait_ge(adj_loaded[k], a.lin(16, 16))
                wait(act, keys_ready, a.lin(GT, k - 1))
                act.activation(mk[:, k % 2, :], adjt[:, k, :], ACT.Sign).then_inc(mask_ready, 1)

            def act_means(act, a):
                for k in range(GT):
                    act.wait_ge(sums_ready, a.lin(GT, (k | 1) + 1))
                    if k == 0:
                        act.wait_ge(indices_ready, a.lin(1, 1))
                        wait(act, x1_ready, a.lin(GT, 0))
                    act.activation(agg[:, k, :], bank[k // 2][:, (k % 2) * D:(k % 2 + 1) * D], ACT.Copy,
                                   scale=rdeg[:, a.off % 2, k:k + 1]).then_inc(means_ready, 1)

            def act_operands(act, a, tiles):
                for k in tiles:
                    act.wait_ge(operands_transposed, a.lin(GT, k + 1))
                    wait(act, linear_ready, a.lin(GT, k - 1))
                    act.activation(xaT[:, k % 2, :, :].rearrange("p c r -> p (c r)"), bank[2 + k % 2][:, :], ACT.Copy).then_inc(operandsT_copied, 1)

            def act_second(act, a, masks=None):
                act.wait_ge(norm_steps, a.lin(4, 4))
                act.activation(rs[:, 1, :], rs[:, 0, :], ACT.Sqrt).then_inc(sqrt_ready, 1)
                act.wait_ge(x1_ready, a.lin(GT, GT))
                hold(act)
                act.dma_start(dr.x1.rearrange("(t p) d -> p t d", p=P)[:, bass.ds(a.lin(GT), GT), :], x1[:, :, :]).then_inc(x1_stored, 16)
                for j in range(2):
                    act.wait_ge(x1_transposed, a.lin(2, j + 1))
                    act.activation(x1T[:, 2 * j:2 * j + 2, :, :].rearrange("p k c r -> p (k c r)"), bank[2 + j][:, :], ACT.Copy).then_inc(x1T_copied, 1)
                if masks is not None:
                    act_mask(act, masks, 0)
                if a.i is not None or a.off > 0:
                    act.wait_ge(tables_stored, a.lin(64, 0))
                    hold(act)
                for k in range(GT):
                    act.wait_ge(qkv_ready, a.lin(GT, k + 1))
                    qb = bank[5] if k % 2 == 0 else bank[2]
                    act.activation(q_sb[:, k, 0:D], qb[:, 0:D], ACT.Copy, scale=SCALING)
                    act.activation(q_sb[:, k, D:QW], qb[:, D:QW], ACT.Copy)
                    act.activation(kv_sb[:, k, :], bank[4 + 2 * (k % 2)][:, :], ACT.Copy).then_inc(qkv_copied, 1)
                    if k % 2:
                        act.wait_ge(qkv_copied, a.lin(GT, k + 1))
                        hold(act)
                        act.dma_start(dr.q.rearrange("(t p) d -> p t d", p=P)[:, bass.ds(a.lin(GT, k - 1), 2), :], q_sb[:, k - 1:k + 1, :]).then_inc(tables_stored, 16)
                        act.dma_start(dr.kv.rearrange("(t p) d -> p t d", p=P)[:, bass.ds(a.lin(GT, k - 1), 2), :], kv_sb[:, k - 1:k + 1, :]).then_inc(tables_stored, 16)

            def act_selT(act, a):
                for j in range(GB // 8):
                    act.wait_ge(sel_transposed, a.lin(3, j + 1))
                    act.activation(selT[:, 8 * j:8 * j + 8, :].rearrange("p b r -> p (b r)"), bank[4 + j][:, :].bitcast(F16), ACT.Copy).then_inc(selT_copied, 1)

            def act_load_x(act, a):
                act.dma_start(xt[:, a.off % 2, :, :], dr.x.rearrange("(t p) d -> p t d", p=P)[:, bass.ds(a.lin(GT), GT), :]).then_inc(x_loaded[a.off % 2], 16)

            def act_step(act, a):
                after, here, last, before = group(a, 1), group(a, 0), group(a, -1), group(a, -2)
                if before is not None:
                    act_second(act, before, after)
                elif after is not None:
                    act_mask(act, after, 0)
                if after is not None:
                    act_mask(act, after, 1)
                if here is not None and (a.i is not None or a.off > 0):
                    act_load_x(act, here)
                if last is not None:
                    act_means(act, last)
                    act_operands(act, last, (0, 1))
                if here is not None:
                    act_selT(act, here)
                if last is not None:
                    act_operands(act, last, (2, 3))
                if after is not None:
                    act_mask(act, after, 2)
                    act_mask(act, after, 3)

            def act_prep(act):
                for i in range(5):
                    act.wait_ge(weights_transposed, i + 1)
                    act.activation(g.w_t[:, i, :, :].rearrange("p c n -> p (c n)"), bank[i][:, :], ACT.Copy).then_inc(weightsT_copied, 1)
                act.wait_ge(fused_ready, 1)
                for half in range(2):
                    act.activation(g.w_fused[:, half * KC:(half + 1) * KC, :].rearrange("p c n -> p (c n)"),
                                   bank[5 + half][:, :], ACT.Copy).then_inc(fused_copied, 1)
                act.activation(g.b_fused[:, :], bank[7][0:1, 0:D], ACT.Copy).then_inc(fused_copied, 1)
                act.activation(g.w_en[:, :, :].rearrange("p c h -> p (c h)"), bank[0][:, 0:KC * HEADS], ACT.Copy).then_inc(fused_copied, 1)
                act.activation(g.be_row[:, :], g.ones[0:1, 0:HEADS], ACT.Copy, scale=g.be_col[0:1, :]).then_inc(fused_copied, 1)

            @block.scalar
            def _(act):
                act_mask(act, At(None, 0), 0)
                act_mask(act, At(None, 0), 1)
                act_load_x(act, At(None, 0))
                act_mask(act, At(None, 0), 2)
                act_mask(act, At(None, 0), 3)
                act_prep(act)
                steps(act, act_step)
                act.wait_ge(x1_stored, 16 * GROUPS)
                act.wait_ge(tables_stored, 64 * GROUPS)

            def pe_prep(pe):
                pe.wait_ge(const_ready, g.N_CONST)
                pe.wait_ge(weights_loaded, 16 * 11)
                pe.wait_ge(we_loaded, 16 * HEADS)
                for i in range(5):
                    for r in range(KC):
                        for c in range(KC):
                            last = pe.transpose(bank[i][:, c * D + r * P:c * D + (r + 1) * P],
                                                w_raw[:, i, r, c * P:(c + 1) * P], g.ident[:, :])
                    last.then_inc(weights_transposed, 1)
                pe.wait_ge(weightsT_copied, 2)
                for half in range(2):
                    for m in range(KC):
                        for k in range(KC):
                            pe.matmul(bank[5 + half][:, m * D:(m + 1) * D],
                                      g.w_t[:, half, k, m * P:(m + 1) * P], w_comb[:, half * KC + k, :],
                                      start=(k == 0), stop=(k == KC - 1))
                for half in range(2):
                    for k in range(KC):
                        pe.matmul(bank[7][0:1, 0:D], g.b_col[:, half, k:k + 1], w_comb[:, half * KC + k, :],
                                  start=(half + k == 0), stop=False)
                pe.matmul(bank[7][0:1, 0:D], g.ones[0:1, 0:1], g.bc_row[:, :], start=False, stop=True)
                pe.wait_ge(weightsT_copied, 5)
                for m in range(KC):
                    for k in range(KC):
                        last = pe.matmul(bank[0][:, m * HEADS:(m + 1) * HEADS], w_raw[:, 2, k, m * P:(m + 1) * P],
                                         g.we_heads[:, k, :], start=(k == 0), stop=(k == KC - 1))
                last.then_inc(fused_ready, 1)
                pe.wait_ge(fused_copied, 5)

            def pe_starts(pe, a):
                pe.wait_ge(degree_ready, a.lin(1, 1))
                pe.matmul(bank[7][:, GB * INFO:GB * INFO + GT], g.below[:, :], deg_h[:, :], start=True, stop=True).then_inc(starts_ready, 1)

            def pe_info(pe, a):
                pe.wait_ge(info_ready, a.lin(1, 1))
                pe.wait_ge(sel_steps, a.lin(2, 2))
                for b in range(GB):
                    last = pe.matmul(bank[7][:, b * INFO:(b + 1) * INFO], sel[:, b // EB, (b % EB) * P:(b % EB + 1) * P],
                                     info[:, b // EB, :], start=True, stop=True)
                last.then_inc(edge_info_ready, 1)

            def pe_selT(pe, a):
                wait(pe, qkv_copied, a.lin(GT, -GT))
                for b in range(GB):
                    last = pe.transpose(bank[4 + b // 8][:, :].bitcast(F16)[:, (b % 8) * P:(b % 8 + 1) * P],
                                        sel[:, b // EB, (b % EB) * P:(b % EB + 1) * P], g.identh[:, :])
                    if b % 8 == 7:
                        last.then_inc(sel_transposed, 1)

            def pe_sums(pe, a, tiles):
                pe.wait_ge(selT_copied, a.lin(3, 3))
                for k in tiles:
                    wait(pe, y_ready, a.lin(GT, (k | 1) + 1 - GT))
                    pe.wait_ge(x_gathered[k], a.lin(16 * EB, 16 * EB))
                    for b in range(EB):
                        last = pe.matmul(bank[k // 2][:, (k % 2) * D:(k % 2 + 1) * D], selT[:, k * EB + b, :], xg[:, k, b, :],
                                         start=(b == 0), stop=(b == EB - 1))
                    last.then_inc(sums_ready, 1)

            def pe_layer(pe, a, after):
                wait(pe, qkv_copied, a.lin(GT, 0))
                pe.wait_ge(x_loaded[a.off % 2], x_count(a))
                for k in range(GT):
                    pe.wait_ge(means_ready, a.lin(GT, (k | 1) + 1))
                    wait(pe, operandsT_copied, a.lin(GT, k - 1))
                    for c in range(2 * KC):
                        src = xt[:, a.off % 2, k, :] if c < KC else agg[:, k, :]
                        last = pe.transpose(bank[2 + k % 2][:, c * P:(c + 1) * P], src[:, (c % KC) * P:(c % KC + 1) * P], g.ident[:, :])
                    last.then_inc(operands_transposed, 1)
                    if k == 1 and after is not None:
                        pe_selT(pe, after)
                    if k >= 1:
                        pe_linear(pe, a, k - 1)
                pe_linear(pe, a, GT - 1)

            def x_count(a):
                return 16 * (a.off // 2 + 1) if a.i is None else a.i * 16 + 16 * (a.off // 2 + 1)

            def pe_linear(pe, a, k):
                pe.wait_ge(operandsT_copied, a.lin(GT, k + 1))
                reg = bank[k // 2][:, (k % 2) * D:(k % 2 + 1) * D]
                for c in range(2 * KC):
                    pe.matmul(reg, xaT[:, k % 2, c, :], g.w_fused[:, c, :], start=(c == 0), stop=False)
                pe.matmul(reg, g.ones[:, :], g.b_fused[:, :], start=False, stop=True).then_inc(linear_ready, 1)

            def pe_second(pe, a):
                pe.wait_ge(operandsT_copied, a.lin(GT, GT))
                pe.wait_ge(selT_copied, a.lin(3, 6) if a.i is not None else min(a.lin(3, 6), 3 * GROUPS))
                for k in range(GT):
                    pe.wait_ge(x1_ready, a.lin(GT, k + 1))
                    for c in range(KC):
                        last = pe.transpose(bank[2 + k // 2][:, (k % 2) * D + c * P:(k % 2) * D + (c + 1) * P],
                                            x1[:, k, c * P:(c + 1) * P], g.ident[:, :])
                    if k % 2:
                        last.then_inc(x1_transposed, 1)
                for k in range(GT):
                    pe.wait_ge(x1T_copied, a.lin(2, k // 2 + 1))
                    wait(pe, qkv_copied, a.lin(GT, k - 1))
                    kvb, qb = bank[4 + 2 * (k % 2)], (bank[5] if k % 2 == 0 else bank[2])
                    for w, reg in ((3, kvb[:, 0:D]), (4, kvb[:, D:2 * D]), (2, qb[:, 0:D])):
                        for c in range(KC):
                            pe.matmul(reg, x1T[:, k, c, :], g.w_t[:, w, c, :], start=(c == 0), stop=(c == KC - 1))
                    for c in range(KC):
                        pe.matmul(qb[:, D:QW], x1T[:, k, c, :], g.w_en[:, c, :], start=(c == 0), stop=False)
                    pe.matmul(qb[:, D:QW], g.ones[:, :], g.be_row[:, :], start=False, stop=True).then_inc(qkv_ready, 1)

            def pe_step(pe, a):
                here, last, before = group(a, 0), group(a, -1), group(a, -2)
                if last is not None:
                    pe_sums(pe, last, (0, 1))
                if before is not None:
                    pe_second(pe, before)
                if here is not None:
                    pe_starts(pe, here)
                if last is not None:
                    pe_sums(pe, last, (2,))
                if here is not None:
                    pe_info(pe, here)
                if last is not None:
                    pe_sums(pe, last, (3,))
                    pe_layer(pe, last, here)
                elif here is not None:
                    pe_selT(pe, here)

            @block.tensor
            def _(pe):
                pe_prep(pe)
                steps(pe, pe_step)
                pe.wait_ge(flag_steps, 4)
                pe.matmul(bank[7][0:1, 0:1], g.over[:, 3:4], g.ones_col[:, :], start=True, stop=True).then_inc(flag_steps, 1)

            def dve_top(dve, a, k, step):
                if step == 0:
                    dve.wait_ge(found_ready, a.lin(GT, k + 1))
                else:
                    dve.wait_ge(top_steps, a.lin(3 * GT, 3 * k + step))
                if a.i is not None:
                    hold(dve)
                keys = found[:, k, :, :].rearrange("p c j -> p (c j)")
                if step == 0:
                    dve.max(top[:, k, 0:8], keys).then_inc(top_steps, 1)
                elif step == 1:
                    dve.match_replace(rest[:, :], top[:, k, 0:8], keys, 0.0).then_inc(top_steps, 1)
                else:
                    dve.max(top[:, k, 8:16], rest[:, :]).then_inc(top_steps, 1)

            def dve_scan(dve, a, k):
                dve.wait_ge(mask_ready, a.lin(GT, k + 1))
                if k > 0:
                    dve.wait_ge(found_ready, a.lin(GT, k))
                dve.tensor_tensor(key[:, :], mk[:, k % 2, :], col1[:, :], ALU.mult).then_inc(keys_ready, 1)
                if k > 0:
                    dve_top(dve, a, k - 1, 0)
                dve.wait_ge(keys_ready, a.lin(GT, k + 1))
                if a.i is not None:
                    hold(dve)
                for c in range(CHUNKS):
                    last = dve.max(found[:, k, c, :], key[:, c * CW:(c + 1) * CW])
                    if k > 0 and c == CHUNKS // 2:
                        dve_top(dve, a, k - 1, 1)
                last.then_inc(found_ready, 1)
                if k > 0:
                    dve_top(dve, a, k - 1, 2)

            def dve_index(dve, a):
                t0 = a.lin(GT)
                deg = g.deg_all[:, bass.ds(t0, GT)]
                start = g.start_all[:, bass.ds(t0, GT)]
                end = g.end_all[:, bass.ds(t0, GT)]
                slotm = g.slot_all[:, bass.ds(a.lin(GB), GB), :]
                n = 9

                def step(j):
                    dve.wait_ge(index_steps, a.lin(n, j))

                dve.wait_ge(found_ready, a.lin(GT, GT))
                dve.tensor_scalar(nz[:, :, :], found[:, :, :, :].rearrange("p t c j -> p t (c j)"), 0.0, None, ALU.is_gt).then_inc(index_steps, 1)
                dve.tensor_copy(g.full_all[:, bass.ds(t0, GT), :], found[:, :, :, 7])
                dve_top(dve, a, GT - 1, 0)
                step(1)
                hold(dve)
                dve.tensor_reduce(deg, nz[:, :, :], AX_X, ALU.add).then_inc(index_steps, 1)
                dve_top(dve, a, GT - 1, 1)
                step(2)
                hold(dve)
                dve.tensor_copy(deg_h[:, :], deg).then_inc(degree_ready, 1)
                dve.tensor_scalar(deg1[:, :], deg, 1.0, None, ALU.max).then_inc(index_steps, 1)
                dve_top(dve, a, GT - 1, 2)
                dve.wait_ge(top_steps, a.lin(3 * GT, 3 * GT))
                dve.tensor_scalar(info[:, :, 2:INFO], top[:, :, :], -(1.0 + HALF), None, ALU.add).then_inc(info_ready, 1)
                dve.tensor_scalar(deg_half[:, :], deg, 0.5, None, ALU.subtract).then_inc(index_steps, 1)
                step(3)
                dve.reciprocal(rdeg[:, a.off % 2, :], deg1[:, :])
                dve.wait_ge(starts_ready, a.lin(1, 1))
                ps = bank[7][:, GB * INFO:GB * INFO + GT]
                dve.tensor_copy(info[:, :, 0], ps)
                dve.tensor_copy(start, ps)
                step(4)
                dve.tensor_tensor(end, ps, deg_half[:, :], ALU.add).then_inc(index_steps, 1)
                step(5)
                for k in range(GT):
                    last = dve.tensor_scalar(sel[:, k, :], iota_e[:, :], g.start_all[:, bass.ds(a.lin(GT, k), 1)],
                                             g.end_all[:, bass.ds(a.lin(GT, k), 1)], ALU.max, ALU.min)
                last.then_inc(sel_steps, 1)
                dve.wait_ge(sel_steps, a.lin(2, 1))
                dve.tensor_tensor(sel[:, :, :], sel[:, :, :], iota_e[:, :].unsqueeze(1).to_broadcast([P, GT, EDGES]),
                                  ALU.is_equal).then_inc(sel_steps, 1)
                dve.wait_ge(edge_info_ready, a.lin(1, 1))
                e = bank[7][:, 0:GB * INFO].rearrange("p (b f) -> p b f", f=INFO)
                dve.tensor_tensor(slot_e[:, :], g.edge_no[:, :], e[:, :, 0], ALU.subtract).then_inc(slot_ready, 1)
                dve.tensor_scalar(unused[:, :], e[:, :, 1], 0.0, float(SKIP), ALU.is_equal, ALU.mult)
                dve.wait_ge(slot_ready, a.lin(1, 1))
                dve.tensor_tensor(slotm, g.iota_s[:, :].unsqueeze(1).to_broadcast([P, GB, SLOTS]),
                                  slot_e[:, :].unsqueeze(2).to_broadcast([P, GB, SLOTS]), ALU.is_equal).then_inc(index_steps, 1)
                dve.tensor_scalar(g.shift_all[:, bass.ds(a.lin(GB), GB)], slot_e[:, :], 0.0, SLOTS - 1.0, ALU.max, ALU.min)
                step(6)
                dve.tensor_tensor(cs[:, :, :], slotm, e[:, :, 2:INFO], ALU.mult).then_inc(index_steps, 1)
                step(7)
                dve.tensor_reduce(colr[:, :], cs[:, :, :], AX_X, ALU.add).then_inc(index_steps, 1)
                step(8)
                dve.scalar_tensor_tensor(colu[:, a.off % 2, :], colr[:, :], float(HALF), unused[:, :], ALU.add, ALU.add).then_inc(indices_ready, 1)
                dve.wait_ge(indices_ready, a.lin(1, 1))
                hold(dve)
                dve.tensor_copy(g.colu_all[:, bass.ds(a.lin(GB), GB)], colu[:, a.off % 2, :]).then_inc(index_steps, 1)

            def dve_tail(dve, a):
                for k in range(GT):
                    dve.wait_ge(linear_ready, a.lin(GT, (k | 1) + 1))
                    dve.scalar_tensor_tensor(y[:, k, :], bank[k // 2][:, (k % 2) * D:(k % 2 + 1) * D], 0.0,
                                             xt[:, a.off % 2, k, :], ALU.max, ALU.add).then_inc(y_ready, 1)
                for k in range(GT):
                    dve.wait_ge(y_ready, a.lin(GT, k + 1))
                    last = dve.bn_stats(stats[:, k, :], y[:, k, :])
                last.then_inc(norm_steps, 1)
                dve.wait_ge(norm_steps, a.lin(4, 1))
                if a.i is not None:
                    hold(dve)
                for k in range(GT):
                    last = dve.bn_aggr(mv[:, k, :], stats[:, k, :])
                last.then_inc(norm_steps, 1)
                dve.wait_ge(norm_steps, a.lin(4, 2))
                dve.tensor_scalar(rs[:, 0, :], mv[:, :, 1], EPS, None, ALU.add).then_inc(norm_steps, 2)
                dve.wait_ge(sqrt_ready, a.lin(1, 1))
                dve.reciprocal(rs[:, 2, :], rs[:, 1, :]).then_inc(rstd_ready, 1)
                dve.wait_ge(rstd_ready, a.lin(1, 1))
                wait(dve, x1_stored, a.lin(16, 0))
                for k in range(GT):
                    dve.tensor_scalar(x1[:, k, :], y[:, k, :], mv[:, k, 0:1], rs[:, 2, k:k + 1], ALU.subtract, ALU.mult).then_inc(x1_ready, 1)

            def dve_step(dve, a):
                here, before = group(a, 0), group(a, -2)
                if here is not None:
                    dve_scan(dve, here, 0)
                    dve_scan(dve, here, 1)
                if before is not None:
                    dve_tail(dve, before)
                if here is not None:
                    dve_scan(dve, here, 2)
                    dve_scan(dve, here, 3)
                    dve_index(dve, here)

            def dve_flag(dve):
                n = 9 * GROUPS
                dve.wait_ge(index_steps, n)
                dve.tensor_reduce(g.over[:, 0:1], g.deg_all[:, :], AX_X, ALU.max)
                dve.tensor_reduce(g.over[:, 1:2], g.full_all[:, :, :], AX_XY, ALU.max)
                dve.tensor_reduce(g.over[:, 2:3], g.end_all[:, :], AX_X, ALU.max).then_inc(flag_steps, 1)
                dve.wait_ge(flag_steps, 1)
                dve.tensor_scalar(g.over[:, 4:5], g.over[:, 0:1], float(SLOTS), None, ALU.is_gt)
                dve.tensor_scalar(g.over[:, 5:6], g.over[:, 1:2], 0.0, None, ALU.is_gt)
                dve.tensor_scalar(g.over[:, 6:7], g.over[:, 2:3], EDGES - 0.5, None, ALU.is_gt).then_inc(flag_steps, 1)
                dve.wait_ge(flag_steps, 2)
                dve.tensor_tensor(g.over[:, 7:8], g.over[:, 4:5], g.over[:, 5:6], ALU.add).then_inc(flag_steps, 1)
                dve.wait_ge(flag_steps, 3)
                dve.tensor_tensor(g.over[:, 3:4], g.over[:, 7:8], g.over[:, 6:7], ALU.add).then_inc(flag_steps, 1)
                dve.wait_ge(flag_steps, 5)
                dve.tensor_scalar(g.flag[:, :], bank[7][0:1, 0:1], 1.0, None, ALU.mult).then_inc(flag_steps, 1)
                dve.wait_ge(flag_steps, 6)

            @block.vector
            def _(dve):
                dve.wait_ge(const_ready, g.N_CONST + 2)
                steps(dve, dve_step)
                dve_flag(dve)


def sparse_layer2(nc, g, dr, m):
    bank = g.bank
    hold = g.hold

    def queries(a, j):
        return bank[j] if j < 4 else bank[6] if j == 4 else sums(a.back(1))

    def vector_share(a):
        return 1 if a.i is not None or a.off < PAIRS - 1 else 7

    def sums(a):
        return bank[5 + 2 * (a.off % 2)]

    bits_of = bank[4][:, PT * P:PT * P + PB * HEADS]

    def sp_load_q(sp, a):
        wait(sp, m.energies_ready, a.lin(1, -1))
        hold(sp)
        sp.dma_start(m.qt[:, a.off % 2, :, :], dr.q.rearrange("(t p) d -> p t d", p=P)[:, bass.ds(a.lin(PT), PT), :]).then_inc(m.q_loaded[a.off % 2], 16)

    def sp_load_x1(sp, a):
        wait(sp, m.residual_ready, a.lin(PT, -PT))
        hold(sp)
        sp.dma_start(m.x1t[:, a.off % 2, :, :], dr.x1.rearrange("(t p) d -> p t d", p=P)[:, bass.ds(a.lin(PT), PT), :]).then_inc(m.x1_loaded[a.off % 2], 16)

    def sp_store(sp, a):
        sp.wait_ge(m.output_ready, a.lin(PT, PT))
        hold(sp)
        sp.dma_start(dr.out.rearrange("(t p) d -> p t d", p=P)[:, bass.ds(a.lin(PT), PT), :], m.o_sb[:, :, :]).then_inc(m.output_stored, 16)

    def count(a):
        c = 16 * (a.off // 2 + 1)
        return c if a.i is None else a.i * 16 + c

    def pool_gather(pool, a):
        half = a.off % 2
        pool.wait_ge(m.indices_ready, a.lin(1, 1))
        wait(pool, m.products_ready, a.lin(PB // 2, -(PB // 2)))
        wait(pool, m.weighed_by_pool, a.lin(1, -1))
        wait(pool, m.weighed_by_vector, a.lin(1, -1))
        hold(pool)
        for b in range(PB):
            pool.indirect_dma_start(out=m.kv[:, half, b, :], out_offset=None, in_=dr.kv,
                                    in_offset=bass.IndirectOffsetOnAxis(ap=m.colu[:, half, b:b + 1], axis=0),
                                    bounds_check=N - 1, oob_is_err=False).then_inc(m.kv_gathered[half], 16)

    def pool_weigh(pool, a):
        half = a.off % 2
        pool.wait_ge(m.weights_ready, a.lin(1, 1))
        wait(pool, m.sums_ready, a.lin(PT, 0))
        n = vector_share(a)
        pool.tensor_tensor(m.vw[:, n:PB, :].rearrange("p b (h d) -> p b h d", d=HD),
                           m.kv[:, half, n:PB, D:KVW].rearrange("p b (h d) -> p b h d", d=HD),
                           m.w[:, n:PB, :].unsqueeze(3).to_broadcast([P, PB - n, HEADS, HD]), ALU.mult).then_inc(m.weighed_by_pool, 1)

    def act_sel(act, a):
        act.wait_ge(m.sel_steps, a.lin(2, 2))
        wait(act, m.queries_ready, a.lin(PB // 2, 0))
        act.activation(m.sel32[:, :, :], m.sel[:, a.off % 2, :, :], ACT.Copy).then_inc(m.sel32_ready, 1)

    def act_selT(act, a, j):
        act.wait_ge(m.sel_transposed, a.lin(2, j + 1))
        act.activation(m.selT[:, a.off % 2, EB * j:EB * (j + 1), :].rearrange("p b r -> p (b r)"),
                       bank[6][:, :].bitcast(F16)[:, 0:EB * P], ACT.Copy).then_inc(m.selT_copied, 1)

    def act_exp(act, a):
        act.wait_ge(m.softmax_steps, a.lin(6, 3))
        act.activation(m.att[:, :, :], m.att[:, :, :], ACT.Exp).then_inc(m.exp_ready, 1)

    def act_sqrt(act, a):
        act.wait_ge(m.norm_steps, a.lin(3, 3))
        act.activation(m.rs[:, 1, :], m.rs[:, 0, :], ACT.Sqrt).then_inc(m.sqrt_ready, 1)

    def act_apply(act, a):
        wait(act, m.output_stored, a.lin(16, 0))
        act.wait_ge(m.rstd_steps, a.lin(2, 2))
        for k in range(PT):
            act.activation(m.o_sb[:, k, :], m.y[:, k, :], ACT.Identity, scale=m.rs[:, 2, k:k + 1], bias=m.rs[:, 3, k:k + 1]).then_inc(m.output_ready, 1)

    def pe_queries(pe, a, banks):
        half = a.off % 2
        pe.wait_ge(m.sel32_ready, a.lin(1, 1))
        pe.wait_ge(m.q_loaded[half], count(a))
        wait(pe, m.products_ready, a.lin(PB // 2, 0))
        for j in banks:
            if j == 4:
                pe.wait_ge(m.selT_copied, a.lin(2, 2))
            if j == 5:
                wait(pe, m.residual_ready, a.lin(PT, -2 * PT))
            for b in (2 * j, 2 * j + 1):
                last = pe.matmul(queries(a, j)[:, (b % 2) * D:(b % 2 + 1) * D],
                                 m.sel32[:, b // EB, (b % EB) * P:(b % EB + 1) * P], m.qt[:, half, b // EB, 0:D],
                                 start=True, stop=True)
            last.then_inc(m.queries_ready, 1)

    def pe_scores(pe, a):
        pe.wait_ge(m.selT_copied, a.lin(2, 2))
        for t in range(PT):
            pe.wait_ge(m.spread_ready, a.lin(PT, t + 1))
            for b in range(EB):
                last = pe.matmul(bank[4][:, t * P:(t + 1) * P], m.selT[:, a.off % 2, t * EB + b, :],
                                 m.rhs[:, t * EB + b, :], start=(b == 0), stop=(b == EB - 1))
        last.then_inc(m.scores_ready, 1)

    def pe_hard(pe, a):
        pe.wait_ge(m.bits_ready, a.lin(1, 1))
        for b in range(PB):
            for n in range(2):
                last = pe.matmul(bits_of[:, b * HEADS:(b + 1) * HEADS],
                                 m.sel[:, a.off % 2, b // EB, (b % EB) * P:(b % EB + 1) * P],
                                 m.hard[:, b // EB, :].rearrange("p (h n) -> p n h", n=2)[:, n, :], start=(n == 0), stop=(n == 1))
        last.then_inc(m.edge_bits_ready, 1)

    def pe_selT(pe, a, j):
        pe.wait_ge(m.sel_steps, a.lin(2, 2))
        wait(pe, m.selT_copied, a.lin(2, j))
        wait(pe, m.products_ready, a.lin(PB // 2, 0))
        for b in range(EB):
            last = pe.transpose(bank[6][:, :].bitcast(F16)[:, b * P:(b + 1) * P],
                                m.sel[:, a.off % 2, j, b * P:(b + 1) * P], g.identh[:, :])
        last.then_inc(m.sel_transposed, 1)

    def pe_sum(pe, a, tiles):
        pe.wait_ge(m.weighed_by_pool, a.lin(1, 1))
        pe.wait_ge(m.weighed_by_vector, a.lin(1, 1))
        last_pair = PAIRS - 1
        pe.wait_ge(m.products_ready, a.lin(PB // 2, PB) if a.i is not None or a.off < last_pair else PAIRS * (PB // 2))
        for t in tiles:
            for b in range(EB):
                last = pe.matmul(sums(a)[:, t * D:(t + 1) * D], m.selT[:, a.off % 2, t * EB + b, :],
                                 m.vw[:, t * EB + b, :], start=(b == 0), stop=(b == EB - 1))
            last.then_inc(m.sums_ready, 1)

    def dve_indices(dve, a):
        half = a.off % 2
        dve.tensor_copy(m.colu[:, half, :], g.colu_all[:, bass.ds(a.lin(PB), PB)]).then_inc(m.indices_ready, 1)

    def dve_sel(dve, a):
        half = a.off % 2
        wait(dve, m.selT_copied, a.lin(2, -2))
        hold(dve)
        for k in range(PT):
            last = dve.tensor_scalar(m.sel[:, half, k, :], g.iota_e[:, :], g.start_all[:, bass.ds(a.lin(PT, k), 1)],
                                     g.end_all[:, bass.ds(a.lin(PT, k), 1)], ALU.max, ALU.min)
        last.then_inc(m.sel_steps, 1)
        dve.wait_ge(m.sel_steps, a.lin(2, 1))
        dve.tensor_tensor(m.sel[:, half, :, :], m.sel[:, half, :, :], g.iota_e[:, :].unsqueeze(1).to_broadcast([P, PT, EDGES]),
                          ALU.is_equal).then_inc(m.sel_steps, 1)

    def dve_products(dve, a):
        half = a.off % 2
        dve.wait_ge(m.kv_gathered[half], gathered(a))
        for j in range(PB // 2):
            dve.wait_ge(m.queries_ready, a.lin(PB // 2, j + 1))
            dve.tensor_tensor(m.prod[:, 2 * j:2 * j + 2, :], queries(a, j)[:, :].rearrange("p (b d) -> p b d", d=D),
                              m.kv[:, half, 2 * j:2 * j + 2, 0:D], ALU.mult).then_inc(m.products_ready, 1)
        dve.wait_ge(m.products_ready, a.lin(PB // 2, PB // 2))
        dve.tensor_reduce(m.se[:, :, :], m.prod[:, :, :].rearrange("p b (h d) -> p b h d", d=HD), AX_X, ALU.add).then_inc(m.edge_scores_ready, 1)
        dve.wait_ge(m.edge_scores_ready, a.lin(1, 1))
        for t in range(PT):
            dve.tensor_tensor(m.rhs[:, t * EB:(t + 1) * EB, :].rearrange("p b (h s) -> p b h s", h=HEADS),
                              g.slot_all[:, bass.ds(a.lin(PB, t * EB), EB), :].unsqueeze(2).to_broadcast([P, EB, HEADS, SLOTS]),
                              m.se[:, t * EB:(t + 1) * EB, :].unsqueeze(3).to_broadcast([P, EB, HEADS, SLOTS]), ALU.mult).then_inc(m.spread_ready, 1)
        dve.tensor_tensor(m.em[:, :, :].rearrange("p t (h s) -> p t h s", h=HEADS),
                          m.past[:, bass.ds(a.lin(PT), PT), :].unsqueeze(2).to_broadcast([P, PT, HEADS, SLOTS]),
                          m.qt[:, half, :, D:QW].unsqueeze(3).to_broadcast([P, PT, HEADS, SLOTS]), ALU.add).then_inc(m.energies_ready, 1)

    def gathered(a):
        c = 16 * PB * (a.off // 2 + 1)
        return c if a.i is None else a.i * (16 * PB) + c

    def by_head(x):
        return x.rearrange("p t (h s) -> p t h s", h=HEADS)

    def over_slots(x):
        return x.unsqueeze(3).to_broadcast([P, PT, HEADS, SLOTS])

    def dve_exponent(dve, a):
        att = by_head(m.att[:, :, :])
        dve.wait_ge(m.scores_ready, a.lin(1, 1))
        dve.wait_ge(m.energies_ready, a.lin(1, 1))
        dve.tensor_tensor(m.att[:, :, :], bank[4][:, 0:PT * P].rearrange("p (t n) -> p t n", n=P), m.em[:, :, :], ALU.add).then_inc(m.softmax_steps, 1)
        dve.wait_ge(m.softmax_steps, a.lin(6, 1))
        dve.tensor_reduce(m.mx[:, 0, :, :], att, AX_X, ALU.max).then_inc(m.softmax_steps, 1)
        dve.wait_ge(m.softmax_steps, a.lin(6, 2))
        dve.tensor_tensor(att, att, over_slots(m.mx[:, 0, :, :]), ALU.subtract).then_inc(m.softmax_steps, 1)

    def dve_choice(dve, a):
        att = by_head(m.att[:, :, :])
        dve.wait_ge(m.exp_ready, a.lin(1, 1))
        dve.tensor_reduce(m.mx[:, 1, :, :], att, AX_X, ALU.add).then_inc(m.softmax_steps, 1)
        dve.wait_ge(m.softmax_steps, a.lin(6, 4))
        dve.reciprocal(m.mx[:, 2, :, :], m.mx[:, 1, :, :]).then_inc(m.softmax_steps, 1)
        dve.wait_ge(m.softmax_steps, a.lin(6, 5))
        dve.tensor_tensor(att, att, over_slots(m.mx[:, 2, :, :]), ALU.mult).then_inc(m.softmax_steps, 1)
        dve.wait_ge(m.softmax_steps, a.lin(6, 6))
        dve.tensor_reduce(m.mx[:, 3, :, :], att, AX_X, ALU.max).then_inc(m.top_steps, 1)
        dve.wait_ge(m.top_steps, a.lin(3, 1))
        dve.tensor_tensor(by_head(m.top[:, :, :]), att, over_slots(m.mx[:, 3, :, :]), ALU.is_equal).then_inc(m.top_steps, 1)
        dve.wait_ge(m.top_steps, a.lin(3, 2))
        slots = m.top[:, :, :].rearrange("p t (h s) -> p (t h) s", s=SLOTS)
        dve.tensor_tensor(slots, slots, g.two_to[:, :].unsqueeze(1).to_broadcast([P, PT * HEADS, SLOTS]), ALU.mult).then_inc(m.top_steps, 1)
        dve.wait_ge(m.top_steps, a.lin(3, 3))
        with nc.allow_low_precision("whole numbers of eight bits and their multiples of 256"):
            dve.tensor_reduce(m.hard[:, :, :], m.top[:, :, :].rearrange("p t (n s) -> p t n s", s=8), AX_X, ALU.add).then_inc(m.bits_ready, 1)

    def dve_weights(dve, a):
        dve.wait_ge(m.edge_bits_ready, a.lin(1, 1))
        dve.tensor_copy(m.code[:, :, :], bits_of.rearrange("p (b h) -> p b h", h=HEADS)).then_inc(m.decode_steps, 1)
        dve.wait_ge(m.decode_steps, a.lin(2, 1))
        dve.tensor_tensor(m.code[:, :, :], m.code[:, :, :],
                          m.bit_of[:, bass.ds(a.lin(PB), PB)].unsqueeze(2).to_broadcast([P, PB, HEADS]),
                          ALU.bitwise_and).then_inc(m.decode_steps, 1)
        wait(dve, m.weighed_by_pool, a.lin(1, 0))
        dve.wait_ge(m.decode_steps, a.lin(2, 2))
        dve.tensor_scalar(m.w[:, :, :], m.code[:, :, :], 0.0, None, ALU.is_gt).then_inc(m.weights_ready, 1)

    def dve_weigh(dve, a):
        dve.wait_ge(m.weights_ready, a.lin(1, 1))
        wait(dve, m.sums_ready, a.lin(PT, 0))
        n = vector_share(a)
        dve.tensor_tensor(m.vw[:, 0:n, :].rearrange("p b (h d) -> p b h d", d=HD),
                          m.kv[:, a.off % 2, 0:n, D:KVW].rearrange("p b (h d) -> p b h d", d=HD),
                          m.w[:, 0:n, :].unsqueeze(3).to_broadcast([P, n, HEADS, HD]), ALU.mult).then_inc(m.weighed_by_vector, 1)

    def dve_norm(dve, a):
        half = a.off % 2
        dve.wait_ge(m.sums_ready, a.lin(PT, PT))
        dve.wait_ge(m.x1_loaded[half], count(a))
        wait(dve, m.output_ready, a.lin(PT, 0))
        for k in range(PT):
            dve.scalar_tensor_tensor(m.y[:, k, :], sums(a)[:, k * D:(k + 1) * D], 1.0 / HEADS, m.x1t[:, half, k, :],
                                     ALU.mult, ALU.add).then_inc(m.residual_ready, 1)
        dve.wait_ge(m.residual_ready, a.lin(PT, PT))
        for k in range(PT):
            last = dve.bn_stats(m.stats[:, k, :], m.y[:, k, :])
        last.then_inc(m.norm_steps, 1)

    def dve_variance(dve, a):
        dve.wait_ge(m.norm_steps, a.lin(3, 1))
        hold(dve)
        for k in range(PT):
            last = dve.bn_aggr(m.mv[:, k, :], m.stats[:, k, :])
        last.then_inc(m.norm_steps, 1)
        dve.wait_ge(m.norm_steps, a.lin(3, 2))
        dve.tensor_scalar(m.rs[:, 0, :], m.mv[:, :, 1], EPS, None, ALU.add).then_inc(m.norm_steps, 1)

    def dve_rstd(dve, a):
        dve.wait_ge(m.sqrt_ready, a.lin(1, 1))
        dve.reciprocal(m.rs[:, 2, :], m.rs[:, 1, :]).then_inc(m.rstd_steps, 1)
        dve.wait_ge(m.rstd_steps, a.lin(2, 1))
        dve.scalar_tensor_tensor(m.rs[:, 3, :], m.mv[:, :, 0], -1.0, m.rs[:, 2, :], ALU.mult, ALU.mult).then_inc(m.rstd_steps, 1)

    def there(a, back):
        if a.i is None and not 0 <= a.off - back < PAIRS:
            return None
        return a.back(back)

    def sync(sp):
        def body(sp, a):
            if (b := there(a, -1)) is not None:
                sp_load_q(sp, b)
            if (b := there(a, 0)) is not None:
                sp_load_x1(sp, b)
            if (b := there(a, 2)) is not None:
                sp_store(sp, b)
        sp_load_q(sp, At(None, 0))
        for q in range(2):
            body(sp, At(None, q))
        with sp.Fori(0, (PAIRS - 4) // 2) as i:
            for half in range(2):
                body(sp, At(i, 2 + half))
        for q in range(PAIRS - 2, PAIRS + 2):
            body(sp, At(None, q))
        sp.wait_ge(m.output_stored, 16 * PAIRS)

    def gpsimd(pool):
        pool_gather(pool, At(None, 0))

        def body(pool, a):
            if (b := there(a, 1)) is not None:
                pool_weigh(pool, b)
            if (b := there(a, -1)) is not None:
                pool_gather(pool, b)
        for q in range(2):
            body(pool, At(None, q))
        with pool.Fori(0, (PAIRS - 4) // 2) as i:
            for half in range(2):
                body(pool, At(i, 2 + half))
        for q in range(PAIRS - 2, PAIRS + 1):
            body(pool, At(None, q))

    def scalar(act):
        act_sel(act, At(None, 0))
        act_selT(act, At(None, 0), 0)
        act_selT(act, At(None, 0), 1)

        def body(act, a):
            if (b := there(a, -1)) is not None:
                act_sel(act, b)
            if (b := there(a, 0)) is not None:
                act_exp(act, b)
            if (b := there(a, -1)) is not None:
                act_selT(act, b, 0)
                act_selT(act, b, 1)
            if (b := there(a, 2)) is not None:
                act_sqrt(act, b)
                act_apply(act, b)
        for q in range(3):
            body(act, At(None, q))
        with act.Fori(0, (PAIRS - 5) // 2) as i:
            for half in range(2):
                body(act, At(i, 3 + half))
        for q in range(3 + (PAIRS - 5) // 2 * 2, PAIRS + 2):
            body(act, At(None, q))

    def tensor(pe):
        def body(pe, a):
            if (b := there(a, 1)) is not None:
                pe_sum(pe, b, (0,))
            if (b := there(a, 0)) is not None:
                pe_scores(pe, b)
            if (b := there(a, -1)) is not None:
                pe_selT(pe, b, 0)
            if (b := there(a, 1)) is not None:
                pe_sum(pe, b, (1,))
            if (b := there(a, -1)) is not None:
                pe_selT(pe, b, 1)
                pe_queries(pe, b, range(3))
            if (b := there(a, 0)) is not None:
                pe_hard(pe, b)
            if (b := there(a, -1)) is not None:
                pe_queries(pe, b, range(3, PB // 2))
        pe_selT(pe, At(None, 0), 0)
        pe_selT(pe, At(None, 0), 1)
        pe_queries(pe, At(None, 0), range(PB // 2))
        for q in range(3):
            body(pe, At(None, q))
        with pe.Fori(0, (PAIRS - 5) // 2) as i:
            for half in range(2):
                body(pe, At(i, 3 + half))
        for q in range(3 + (PAIRS - 5) // 2 * 2, PAIRS + 1):
            body(pe, At(None, q))

    def vector(dve):
        dve.tensor_tensor(m.past[:, :, :], g.iota_s[:, :].unsqueeze(1).to_broadcast([P, TILES, SLOTS]),
                          g.deg_all[:, :].unsqueeze(2).to_broadcast([P, TILES, SLOTS]), ALU.is_ge).then_inc(m.start_steps, 1)
        dve_indices(dve, At(None, 0))
        dve_indices(dve, At(None, 1))
        dve_sel(dve, At(None, 0))
        dve.memset(m.one[:, :], 1).then_inc(m.start_steps, 1)
        dve.wait_ge(m.start_steps, 2)
        dve.tensor_tensor(m.bit_of[:, :], m.one[:, :].to_broadcast([P, TILES * EB]), g.shift_all[:, :], ALU.logical_shift_left).then_inc(m.start_steps, 1)
        dve.tensor_scalar(m.past[:, :, :], m.past[:, :, :], -BIG, None, ALU.mult).then_inc(m.start_steps, 1)
        dve.wait_ge(m.start_steps, 4)

        def body(dve, a):
            if (b := there(a, 0)) is not None:
                dve_products(dve, b)
            if (b := there(a, -1)) is not None:
                dve_sel(dve, b)
            if (b := there(a, 2)) is not None:
                dve_norm(dve, b)
            if (b := there(a, 0)) is not None:
                dve_exponent(dve, b)
            if (b := there(a, 2)) is not None:
                dve_variance(dve, b)
            if (b := there(a, 0)) is not None:
                dve_choice(dve, b)
            if (b := there(a, 2)) is not None:
                dve_rstd(dve, b)
            if (b := there(a, -2)) is not None:
                dve_indices(dve, b)
            if (b := there(a, 0)) is not None:
                dve_weights(dve, b)
                dve_weigh(dve, b)
        for q in range(3):
            body(dve, At(None, q))
        with dve.Fori(0, (PAIRS - 5) // 2) as i:
            for half in range(2):
                body(dve, At(i, 3 + half))
        for q in range(3 + (PAIRS - 5) // 2 * 2, PAIRS + 2):
            body(dve, At(None, q))

    return dict(sync=sync, gpsimd=gpsimd, scalar=scalar, tensor=tensor, vector=vector)


def dense_layers(nc, g, dr, m):
    def agg_sync(sp):
        sp.dma_start(m.x_all[:, :, :], dr.x.rearrange("(t p) d -> p t d", p=P)).then_inc(m.x_loaded, 16)
        with sp.Fori(0, TILES) as t:
            sp.dma_start(m.adjt[:, :], dr.adj[bass.ds(t * P, P), :]).then_inc(m.adj_loaded, 16)
            sp.wait_ge(m.means_ready, t + 1)
            g.hold(sp)
            sp.dma_start(dr.agg[bass.ds(t * P, P), :], m.agg_sb[:, :]).then_inc(m.means_stored, 16)
            sp.wait_ge(m.means_stored, t * 16 + 16)
            g.hold(sp)

    def agg_vector(dve):
        with dve.Fori(0, TILES) as t:
            dve.wait_ge(m.adj_loaded, t * 16 + 16)
            dve.tensor_scalar(m.mask[:, :], m.adjt[:, :], 0.0, None, ALU.is_gt).then_inc(m.mask_ready, 1)
            dve.wait_ge(m.mask_ready, t + 1)
            dve.tensor_reduce(m.deg[:, 0:1], m.mask[:, :], AX_X, ALU.add).then_inc(m.degree_steps, 1)
            dve.wait_ge(m.degree_steps, t * 3 + 1)
            dve.tensor_scalar(m.deg[:, 1:2], m.deg[:, 0:1], 1.0, None, ALU.max).then_inc(m.degree_steps, 1)
            dve.wait_ge(m.degree_steps, t * 3 + 2)
            dve.reciprocal(m.deg[:, 2:3], m.deg[:, 1:2]).then_inc(m.degree_steps, 1)
            for b in range(4):
                dve.wait_ge(m.mask_transposed, t * 4 + (b + 1))
                dve.tensor_copy(m.maskT[:, 8 * b:8 * b + 8, :].rearrange("p c r -> p (c r)"),
                                g.bank[b][:, :].bitcast(BF16)).then_inc(m.maskT_copied, 1)
            dve.wait_ge(m.sums_ready, t + 1)
            dve.wait_ge(m.degree_steps, t * 3 + 3)
            dve.tensor_scalar(m.agg_sb[:, :], g.bank[4][:, 0:D], m.deg[:, 2:3], None, ALU.mult).then_inc(m.means_ready, 1)

    def agg_tensor(pe):
        pe.wait_ge(m.x_loaded, 16)
        with pe.Fori(0, TILES) as t:
            pe.wait_ge(m.mask_ready, t + 1)
            for b in range(4):
                for c in range(8):
                    last = pe.transpose(g.bank[b][:, :].bitcast(BF16)[:, c * P:(c + 1) * P],
                                        m.mask[:, (8 * b + c) * P:(8 * b + c + 1) * P], g.identb[:, :])
                last.then_inc(m.mask_transposed, 1)
            for b in range(4):
                pe.wait_ge(m.maskT_copied, t * 4 + (b + 1))
                for c in range(8 * b, 8 * b + 8):
                    last = pe.matmul(g.bank[4][:, 0:D], m.maskT[:, c, :], m.x_all[:, c, :],
                                     start=(c == 0), stop=(c == TILES - 1))
            last.then_inc(m.sums_ready, 1)

    def tail_sync(sp):
        with sp.Fori(0, TILES) as t:
            sp.dma_start(m.xa[:, 0, :], dr.x[bass.ds(t * P, P), :]).then_inc(m.inputs_loaded, 16)
            sp.dma_start(m.xa[:, 1, :], dr.agg[bass.ds(t * P, P), :]).then_inc(m.inputs_loaded, 16)
            sp.wait_ge(m.x1_ready, t + 1)
            g.hold(sp)
            sp.dma_start(dr.x1[bass.ds(t * P, P), :], m.x1[:, :]).then_inc(m.tables_stored, 16)
            sp.wait_ge(m.qkv_copied, t * 2 + 2)
            g.hold(sp)
            sp.dma_start(dr.qT.rearrange("(c p) n -> p c n", p=P)[:, :, bass.ds(t * P, P)], m.qkT[:, 0:2, :]).then_inc(m.tables_stored, 16)
            sp.dma_start(dr.kT.rearrange("(c p) n -> p c n", p=P)[:, :, bass.ds(t * P, P)], m.qkT[:, 2:4, :]).then_inc(m.tables_stored, 16)
            sp.dma_start(dr.v[bass.ds(t * P, P), :], m.v_sb[:, :]).then_inc(m.tables_stored, 16)
            sp.wait_ge(m.tables_stored, t * 64 + 64)
            g.hold(sp)

    def tail_tensor(pe):
        with pe.Fori(0, TILES) as t:
            pe.wait_ge(m.inputs_loaded, t * 32 + 32)
            for i in range(2 * KC):
                last = pe.transpose(g.bank[0][:, i * P:(i + 1) * P], m.xa[:, i // KC, (i % KC) * P:(i % KC + 1) * P], g.ident[:, :])
            last.then_inc(m.inputs_transposed, 1)
            pe.wait_ge(m.inputsT_copied, t + 1)
            for i in range(2 * KC):
                pe.matmul(g.bank[1][:, 0:D], m.xaT[:, i, :], g.w_fused[:, i, :], start=(i == 0), stop=False)
            pe.matmul(g.bank[1][:, 0:D], g.ones[:, :], g.b_fused[:, :], start=False, stop=True).then_inc(m.linear_ready, 1)
            pe.wait_ge(m.x1_ready, t + 1)
            for i in range(KC):
                last = pe.transpose(g.bank[2][:, i * P:(i + 1) * P], m.x1[:, i * P:(i + 1) * P], g.ident[:, :])
            last.then_inc(m.x1_transposed, 1)
            pe.wait_ge(m.x1T_copied, t + 1)
            for j in range(4):
                for k in range(KC):
                    pe.matmul(g.bank[3][:, j * P:(j + 1) * P], g.w_t[:, 2 + j // 2, k, (j % 2) * P:(j % 2 + 1) * P],
                              m.x1T[:, k, :], start=(k == 0), stop=(k == KC - 1))
            for k in range(KC):
                last = pe.matmul(g.bank[4][:, 0:D], m.x1T[:, k, :], g.w_t[:, 4, k, :], start=(k == 0), stop=(k == KC - 1))
            last.then_inc(m.qkv_ready, 1)

    def tail_vector(dve):
        with dve.Fori(0, TILES) as t:
            dve.wait_ge(m.inputs_transposed, t + 1)
            dve.tensor_copy(m.xaT[:, :, :].rearrange("p c r -> p (c r)"), g.bank[0][:, :]).then_inc(m.inputsT_copied, 1)
            dve.wait_ge(m.linear_ready, t + 1)
            dve.scalar_tensor_tensor(m.y[:, :], g.bank[1][:, 0:D], 0.0, m.xa[:, 0, :], ALU.max, ALU.add).then_inc(m.norm_steps, 1)
            dve.wait_ge(m.norm_steps, t * 4 + 1)
            dve.bn_stats(m.st[:, 0:6], m.y[:, :]).then_inc(m.norm_steps, 1)
            dve.wait_ge(m.norm_steps, t * 4 + 2)
            g.hold(dve)
            dve.bn_aggr(m.st[:, 6:8], m.st[:, 0:6]).then_inc(m.norm_steps, 1)
            dve.wait_ge(m.norm_steps, t * 4 + 3)
            dve.tensor_scalar(m.st[:, 8:9], m.st[:, 7:8], EPS, None, ALU.add).then_inc(m.norm_steps, 1)
            dve.wait_ge(m.sqrt_steps, t * 2 + 1)
            dve.reciprocal(m.st[:, 10:11], m.st[:, 9:10]).then_inc(m.sqrt_steps, 1)
            dve.wait_ge(m.sqrt_steps, t * 2 + 2)
            dve.tensor_scalar(m.x1[:, :], m.y[:, :], m.st[:, 6:7], m.st[:, 10:11], ALU.subtract, ALU.mult).then_inc(m.x1_ready, 1)
            dve.wait_ge(m.x1_transposed, t + 1)
            dve.tensor_copy(m.x1T[:, :, :].rearrange("p c r -> p (c r)"), g.bank[2][:, 0:D]).then_inc(m.x1T_copied, 1)
            dve.wait_ge(m.qkv_ready, t + 1)
            dve.tensor_copy(m.qkT[:, :, :].rearrange("p c r -> p (c r)"), g.bank[3][:, :]).then_inc(m.qkv_copied, 1)
            dve.tensor_copy(m.v_sb[:, :], g.bank[4][:, 0:D]).then_inc(m.qkv_copied, 1)

    def tail_scalar(act):
        with act.Fori(0, TILES) as t:
            act.wait_ge(m.norm_steps, t * 4 + 4)
            act.activation(m.st[:, 9:10], m.st[:, 8:9], ACT.Sqrt).then_inc(m.sqrt_steps, 1)

    def att_sync(sp):
        with sp.Fori(0, HEADS) as h:
            sp.dma_start(m.kT_h[:, :], dr.kT[bass.ds(h * HD, HD), :]).then_inc(m.head_loaded, 16)
            with nc.allow_non_contiguous_dma("a head's 128-byte rows of V"):
                sp.dma_start(m.v_h[:, :, :], dr.v.rearrange("(t p) d -> p t d", p=P)[:, :, bass.ds(h * HD, HD)]).then_inc(m.head_loaded, 16)
            with sp.Fori(0, TILES) as t:
                n = h * TILES + t
                sp.dma_start(m.adjt[:, :], dr.adj[bass.ds(t * P, P), :]).then_inc(m.att_inputs_loaded, 16)
                sp.dma_start(m.qT_h[:, :], dr.qT[bass.ds(h * HD, HD), bass.ds(t * P, P)]).then_inc(m.att_inputs_loaded, 16)
                sp.wait_ge(m.att_ready, n + 1)
                g.hold(sp)
                with nc.allow_non_contiguous_dma("a head's 128-byte rows"):
                    sp.dma_start(dr.att[bass.ds(t * P, P), bass.ds(h * HD, HD)], m.o_sb[:, :]).then_inc(m.att_stored, 16)
                sp.wait_ge(m.att_stored, n * 16 + 16)
                g.hold(sp)

    def att_tensor(pe):
        with pe.Fori(0, HEADS) as h:
            pe.wait_ge(m.head_loaded, h * 32 + 32)
            g.hold(pe)
            with pe.Fori(0, TILES) as t:
                n = h * TILES + t
                pe.wait_ge(m.att_inputs_loaded, n * 32 + 32)
                pe.matmul(g.bank[4][:, 0:1], m.qT_h[:, :], g.we_col[:, :], start=True, stop=True).then_inc(m.energy_ready, 1)
                for c in range(8):
                    if c >= 4:
                        pe.wait_ge(m.score_chunk_copied, n * 8 + (c - 3))
                    pe.matmul(g.bank[c % 4][:, :], m.qT_h[:, :], m.kT_h[:, c * 512:(c + 1) * 512],
                              start=True, stop=True).then_inc(m.score_chunk_ready, 1)
                pe.wait_ge(m.hard_ready, n + 1)
                for b in range(4):
                    if b >= 2:
                        pe.wait_ge(m.hardT_copied, n * 4 + (b - 1))
                    for c in range(8):
                        last = pe.transpose(g.bank[5 + b % 2][:, :].bitcast(BF16)[:, c * P:(c + 1) * P],
                                            m.hard[:, (8 * b + c) * P:(8 * b + c + 1) * P], g.identb[:, :])
                    last.then_inc(m.hard_transposed, 1)
                pe.wait_ge(m.hardT_copied, n * 4 + 4)
                for c in range(TILES):
                    last = pe.matmul(g.bank[7][:, 0:HD], m.maskT[:, c, :], m.v_h[:, c, :],
                                     start=(c == 0), stop=(c == TILES - 1))
                last.then_inc(m.att_sums_ready, 1)

    def att_vector(dve):
        with dve.Fori(0, HEADS) as h:
            with dve.Fori(0, TILES) as t:
                n = h * TILES + t
                dve.wait_ge(m.att_inputs_loaded, n * 32 + 32)
                dve.tensor_scalar(m.mask[:, :], m.adjt[:, :], 0.0, None, ALU.is_gt).then_inc(m.att_mask_steps, 1)
                dve.wait_ge(m.att_mask_steps, n * 3 + 1)
                dve.tensor_scalar(m.madd[:, :], m.mask[:, :], 1.0, BIG, ALU.subtract, ALU.mult).then_inc(m.att_mask_steps, 1)
                dve.wait_ge(m.energy_ready, n + 1)
                dve.tensor_scalar(m.en[:, :], g.bank[4][:, 0:1], g.be_col[:, :], None, ALU.add).then_inc(m.att_mask_steps, 1)
                dve.wait_ge(m.att_mask_steps, n * 3 + 3)
                for c in range(8):
                    dve.wait_ge(m.score_chunk_ready, n * 8 + (c + 1))
                    dve.tensor_scalar(m.sc[:, c * 512:(c + 1) * 512], g.bank[c % 4][:, :], SCALING, m.en[:, :],
                                      ALU.mult, ALU.add).then_inc(m.score_chunk_copied, 1)
                dve.wait_ge(m.score_chunk_copied, n * 8 + 8)
                dve.tensor_tensor(m.sc[:, :], m.sc[:, :], m.madd[:, :], ALU.add).then_inc(m.softmax_steps, 1)
                dve.wait_ge(m.softmax_steps, n * 6 + 1)
                dve.tensor_reduce(m.sm[:, 0:1], m.sc[:, :], AX_X, ALU.max, negate=True).then_inc(m.softmax_steps, 1)
                dve.wait_ge(m.exp_ready, n + 1)
                dve.reciprocal(m.sm[:, 2:3], m.sm[:, 1:2]).then_inc(m.softmax_steps, 1)
                dve.wait_ge(m.softmax_steps, n * 6 + 3)
                dve.tensor_scalar(m.sc[:, :], m.sc[:, :], m.sm[:, 2:3], None, ALU.mult).then_inc(m.softmax_steps, 1)
                dve.wait_ge(m.softmax_steps, n * 6 + 4)
                dve.tensor_reduce(m.sm[:, 3:4], m.sc[:, :], AX_X, ALU.max).then_inc(m.softmax_steps, 1)
                dve.wait_ge(m.softmax_steps, n * 6 + 5)
                dve.scalar_tensor_tensor(m.hard[:, :], m.sc[:, :], m.sm[:, 3:4], m.mask[:, :], ALU.is_equal, ALU.mult).then_inc(m.hard_ready, 1)
                dve.tensor_scalar(m.sm[:, 4:5], m.sm[:, 3:4], 1.0, None, ALU.mult).then_inc(m.softmax_steps, 1)
                for b in range(4):
                    dve.wait_ge(m.hard_transposed, n * 4 + (b + 1))
                    dve.tensor_copy(m.maskT[:, 8 * b:8 * b + 8, :].rearrange("p c r -> p (c r)"),
                                    g.bank[5 + b % 2][:, :].bitcast(BF16)).then_inc(m.hardT_copied, 1)
                dve.wait_ge(m.att_sums_ready, n + 1)
                dve.tensor_scalar(m.o_sb[:, :], g.bank[7][:, 0:HD], 1.0 / HEADS, None, ALU.mult).then_inc(m.att_ready, 1)

    def att_scalar(act):
        with act.Fori(0, HEADS) as h:
            with act.Fori(0, TILES) as t:
                n = h * TILES + t
                act.wait_ge(m.softmax_steps, n * 6 + 2)
                act.activation(m.sc[:, :], m.sc[:, :], ACT.Exp, bias=m.sm[:, 0:1], accum_out=m.sm[:, 1:2]).then_inc(m.exp_ready, 1)

    def fin_sync(sp):
        with sp.Fori(0, TILES) as t:
            sp.dma_start(m.xa[:, 0, :], dr.x1[bass.ds(t * P, P), :]).then_inc(m.final_inputs_loaded, 16)
            sp.dma_start(m.xa[:, 1, :], dr.att[bass.ds(t * P, P), :]).then_inc(m.final_inputs_loaded, 16)
            sp.wait_ge(m.output_ready, t + 1)
            g.hold(sp)
            sp.dma_start(dr.out[bass.ds(t * P, P), :], m.x1[:, :]).then_inc(m.output_stored, 16)
            sp.wait_ge(m.output_stored, t * 16 + 16)
            g.hold(sp)

    def fin_vector(dve):
        with dve.Fori(0, TILES) as t:
            dve.wait_ge(m.final_inputs_loaded, t * 32 + 32)
            dve.tensor_tensor(m.y[:, :], m.xa[:, 0, :], m.xa[:, 1, :], ALU.add).then_inc(m.final_norm_steps, 1)
            dve.wait_ge(m.final_norm_steps, t * 4 + 1)
            dve.bn_stats(m.st[:, 0:6], m.y[:, :]).then_inc(m.final_norm_steps, 1)
            dve.wait_ge(m.final_norm_steps, t * 4 + 2)
            g.hold(dve)
            dve.bn_aggr(m.st[:, 6:8], m.st[:, 0:6]).then_inc(m.final_norm_steps, 1)
            dve.wait_ge(m.final_norm_steps, t * 4 + 3)
            dve.tensor_scalar(m.st[:, 8:9], m.st[:, 7:8], EPS, None, ALU.add).then_inc(m.final_norm_steps, 1)
            dve.wait_ge(m.final_sqrt_steps, t * 2 + 1)
            dve.reciprocal(m.st[:, 10:11], m.st[:, 9:10]).then_inc(m.final_sqrt_steps, 1)
            dve.wait_ge(m.final_sqrt_steps, t * 2 + 2)
            dve.tensor_scalar(m.x1[:, :], m.y[:, :], m.st[:, 6:7], m.st[:, 10:11], ALU.subtract, ALU.mult).then_inc(m.output_ready, 1)

    def fin_scalar(act):
        with act.Fori(0, TILES) as t:
            act.wait_ge(m.final_norm_steps, t * 4 + 4)
            act.activation(m.st[:, 9:10], m.st[:, 8:9], ACT.Sqrt).then_inc(m.final_sqrt_steps, 1)


    def sync(sp):
        agg_sync(sp)
        tail_sync(sp)
        att_sync(sp)
        fin_sync(sp)

    def tensor(pe):
        agg_tensor(pe)
        tail_tensor(pe)
        att_tensor(pe)

    def vector(dve):
        agg_vector(dve)
        tail_vector(dve)
        att_vector(dve)
        fin_vector(dve)

    def scalar(act):
        tail_scalar(act)
        att_scalar(act)
        fin_scalar(act)

    return dict(sync=sync, gpsimd=None, scalar=scalar, tensor=tensor, vector=vector)


class Names:
    pass


def gnn_kernel(nc, x, adj, W_self, b_self, W_nb, b_nb, W_comb, b_comb, WQ, WK, WV, we, be, out):
    ctx = ExitStack()
    with ctx:
        def dram(name, shape):
            return nc.dram_tensor(name, shape, F32, kind="Internal").ap()

        dr = Names()
        dr.x, dr.adj, dr.W_self, dr.b_self, dr.W_nb, dr.b_nb = x, adj, W_self, b_self, W_nb, b_nb
        dr.W_comb, dr.b_comb, dr.WQ, dr.WK, dr.WV, dr.we, dr.be, dr.out = W_comb, b_comb, WQ, WK, WV, we, be, out
        dr.x1, dr.q, dr.kv = dram("x1_d", [N, D]), dram("q_d", [N, QW]), dram("kv_d", [N, KVW])
        dr.agg, dr.qT, dr.kT, dr.v, dr.att = (dram("agg_d", [N, D]), dram("qT_d", [D, N]), dram("kT_d", [D, N]),
                                              dram("v_d", [N, D]), dram("att_d", [N, D]))

        def sb(stack, name, shape, dt=F32):
            return stack.enter_context(nc.sbuf_tensor(name, shape, dt))

        def sem(name):
            return ctx.enter_context(nc.semaphore(name))

        g = Names()
        g.ident = sb(ctx, "g_ident", [P, P])
        g.identb = sb(ctx, "g_identb", [P, P], BF16)
        g.identh = sb(ctx, "g_identh", [P, P], F16)
        g.adjt = sb(ctx, "g_adjt", [P, GT, N], I32)
        g.kv = (g.adjt[:, :, :].rearrange("p t n -> p (t n)")[:, 0:2 * PB * KVW].bitcast(F32)
                .rearrange("p (h b c) -> p h b c", h=2, b=PB))
        g.two_to = sb(ctx, "g_two_to", [P, SLOTS])
        g.ones = sb(ctx, "g_ones", [1, P])
        g.ones_col = sb(ctx, "g_ones_col", [P, 1])
        g.below = sb(ctx, "g_below", [P, P], F16)
        g.iota_e = sb(ctx, "g_iota_e", [P, EDGES], F16)
        g.iota_s = sb(ctx, "g_iota_s", [P, SLOTS])
        g.edge_no = sb(ctx, "g_edge_no", [P, GB])
        g.w_t = sb(ctx, "g_w_t", [P, 5, KC, D])
        g.w_fused = sb(ctx, "g_w_fused", [P, 2 * KC, D])
        g.w_en = sb(ctx, "g_w_en", [P, KC, HEADS])
        g.b_fused = sb(ctx, "g_b_fused", [1, D])
        g.b_col = sb(ctx, "g_b_col", [P, 2, KC])
        g.bc_row = sb(ctx, "g_bc_row", [1, D])
        g.we_col = sb(ctx, "g_we_col", [HD, 1])
        g.we_heads = sb(ctx, "g_we_heads", [P, KC, HEADS])
        g.be_col = sb(ctx, "g_be_col", [P, 1])
        g.be_row = sb(ctx, "g_be_row", [1, HEADS])
        g.deg_all = sb(ctx, "g_deg_all", [P, TILES])
        g.start_all = sb(ctx, "g_start_all", [P, TILES])
        g.end_all = sb(ctx, "g_end_all", [P, TILES])
        g.full_all = sb(ctx, "g_full_all", [P, TILES, CHUNKS])
        g.slot_all = sb(ctx, "g_slot_all", [P, TILES * EB, SLOTS], BF16)
        g.shift_all = sb(ctx, "g_shift_all", [P, TILES * EB], I32)
        g.colu_all = sb(ctx, "g_colu_all", [P, TILES * EB], U32)
        g.over = sb(ctx, "g_over", [P, 8])
        g.flag = sb(ctx, "g_flag", [1, 1], I32)
        g.bank = [ctx.enter_context(nc.psum_tensor(f"bank{i}", [P, 512], F32)) for i in range(8)]
        g.held = {}

        def hold(eng):
            name = str(eng.engine)
            if name not in g.held:
                g.held[name] = ctx.enter_context(nc.semaphore(f"held{len(g.held)}"))
            eng.sem_inc(g.held[name], 1)

        g.hold = hold
        g.N_CONST = 14 + SLOTS

        def constants(pool, const_ready):
            pool.memset(g.ident[:, :], 0.0).then_inc(const_ready, 1)
            pool.memset(g.identb[:, :], 0.0).then_inc(const_ready, 1)
            pool.memset(g.identh[:, :], 0.0).then_inc(const_ready, 1)
            for s in range(SLOTS):
                pool.memset(g.two_to[:, s:s + 1], float(1 << s)).then_inc(const_ready, 1)
            pool.memset(g.below[:, :], 1.0).then_inc(const_ready, 1)
            pool.memset(g.ones[:, :], 1.0).then_inc(const_ready, 1)
            pool.memset(g.ones_col[:, :], 1.0).then_inc(const_ready, 1)
            pool.memset(g.we_heads[:, :, :], 0.0).then_inc(const_ready, 1)
            pool.wait_ge(const_ready, 7 + SLOTS)
            for eye in (g.ident, g.identb, g.identh):
                pool.affine_select(out=eye[:, :], in_=eye[:, :], compare_op=ALU.not_equal, fill=1.0, base=0,
                                   pattern=[[-1, P]], channel_multiplier=1).then_inc(const_ready, 1)
            pool.affine_select(out=g.below[:, :], in_=g.below[:, :], compare_op=ALU.is_gt, fill=0.0, base=0,
                               pattern=[[1, P]], channel_multiplier=-1).then_inc(const_ready, 1)
            loose = dict(allow_small_or_imprecise_dtypes=True)
            pool.iota(g.iota_e[:, :], [[1, EDGES]], base=0, channel_multiplier=0, **loose).then_inc(const_ready, 1)
            pool.iota(g.iota_s[:, :], [[1, SLOTS]], base=0, channel_multiplier=0, **loose).then_inc(const_ready, 1)
            pool.iota(g.edge_no[:, :], [[0, GT], [P, EB]], base=0, channel_multiplier=1, **loose).then_inc(const_ready, 1)

        g.constants = constants
        sparse_layer1(nc, g, dr)

        m = Names()
        m.kv = g.kv
        with ExitStack() as stack:
            m.qt = sb(stack, "p2_qt", [P, 2, PT, QW])
            m.x1t = sb(stack, "p2_x1t", [P, 2, PT, D])
            m.colu = sb(stack, "p2_colu", [P, 2, PB], U32)
            m.vw = sb(stack, "p2_vw", [P, PB, D])
            m.sel = sb(stack, "p2_sel", [P, 2, PT, EDGES], F16)
            m.sel32 = sb(stack, "p2_sel32", [P, PT, EDGES])
            m.selT = sb(stack, "p2_selT", [P, 2, PB, P])
            m.prod = sb(stack, "p2_prod", [P, PB, D])
            m.se = sb(stack, "p2_se", [P, PB, HEADS])
            m.rhs = sb(stack, "p2_rhs", [P, PB, P])
            m.past = sb(stack, "p2_past", [P, TILES, SLOTS])
            m.em = sb(stack, "p2_em", [P, PT, P])
            m.att = sb(stack, "p2_att", [P, PT, P])
            m.mx = sb(stack, "p2_mx", [P, 4, PT, HEADS])
            m.top = sb(stack, "p2_top", [P, PT, P])
            m.hard = sb(stack, "p2_hard", [P, PT, 2 * HEADS], F16)
            m.bit_of = sb(stack, "p2_bit_of", [P, TILES * EB], I32)
            m.one = sb(stack, "p2_one", [P, 1], I32)
            m.code = sb(stack, "p2_code", [P, PB, HEADS], I32)
            m.w = sb(stack, "p2_w", [P, PB, HEADS])
            m.y = sb(stack, "p2_y", [P, PT, D])
            m.stats = sb(stack, "p2_stats", [P, PT, 6])
            m.mv = sb(stack, "p2_mv", [P, PT, 2])
            m.rs = sb(stack, "p2_rs", [P, 4, PT])
            m.o_sb = sb(stack, "p2_o_sb", [P, PT, D])
        m.energies_ready = sem("p2_energies_ready")
        m.residual_ready = sem("p2_residual_ready")
        m.output_ready = sem("p2_output_ready")
        m.output_stored = sem("p2_output_stored")
        m.indices_ready = sem("p2_indices_ready")
        m.products_ready = sem("p2_products_ready")
        m.weighed_by_pool = sem("p2_weighed_by_pool")
        m.weighed_by_vector = sem("p2_weighed_by_vector")
        m.weights_ready = sem("p2_weights_ready")
        m.sums_ready = sem("p2_sums_ready")
        m.sel_steps = sem("p2_sel_steps")
        m.sel32_ready = sem("p2_sel32_ready")
        m.selT_copied = sem("p2_selT_copied")
        m.queries_ready = sem("p2_queries_ready")
        m.softmax_steps = sem("p2_softmax_steps")
        m.exp_ready = sem("p2_exp_ready")
        m.norm_steps = sem("p2_norm_steps")
        m.sqrt_ready = sem("p2_sqrt_ready")
        m.spread_ready = sem("p2_spread_ready")
        m.scores_ready = sem("p2_scores_ready")
        m.bits_ready = sem("p2_bits_ready")
        m.edge_bits_ready = sem("p2_edge_bits_ready")
        m.edge_scores_ready = sem("p2_edge_scores_ready")
        m.start_steps = sem("p2_start_steps")
        m.top_steps = sem("p2_top_steps")
        m.decode_steps = sem("p2_decode_steps")
        m.sel_transposed = sem("p2_sel_transposed")
        m.rstd_steps = sem("p2_rstd_steps")
        m.q_loaded, m.x1_loaded, m.kv_gathered = ([ctx.enter_context(nc.semaphore(f"p2_{n}_{half}")) for half in range(2)]
                                     for n in ("q_loaded", "x1_loaded", "kv_gathered"))
        d = Names()
        d.adjt = g.adjt[:, 0, :]
        d.x_all = g.adjt[:, 1:3, :].rearrange("p t n -> p (t n)").bitcast(F32).rearrange("p (t d) -> p t d", d=D)
        with ExitStack() as stack:
            d.mask = sb(stack, "d_mask", [P, N], BF16)
            d.maskT = sb(stack, "d_maskT", [P, TILES, P])
            d.deg = sb(stack, "d_deg", [P, 4])
            d.agg_sb = sb(stack, "d_agg_sb", [P, D])
            d.xa = sb(stack, "d_xa", [P, 2, D])
            d.xaT = sb(stack, "d_xaT", [P, 2 * KC, P])
            d.y = sb(stack, "d_y", [P, D])
            d.st = sb(stack, "d_st", [P, 12])
            d.x1 = sb(stack, "d_x1", [P, D])
            d.x1T = sb(stack, "d_x1T", [P, KC, P])
            d.qkT = sb(stack, "d_qkT", [P, 4, P])
            d.v_sb = sb(stack, "d_v_sb", [P, D])
            d.kT_h = sb(stack, "d_kT_h", [HD, N])
            d.v_h = sb(stack, "d_v_h", [P, TILES, HD])
            d.qT_h = sb(stack, "d_qT_h", [HD, P])
            d.sc = sb(stack, "d_sc", [P, N])
            d.madd = sb(stack, "d_madd", [P, N], BF16)
            d.hard = sb(stack, "d_hard", [P, N], BF16)
            d.en = sb(stack, "d_en", [P, 1])
            d.sm = sb(stack, "d_sm", [P, 8])
            d.o_sb = sb(stack, "d_o_sb", [P, HD])
        d.adj_loaded = sem("d_adj_loaded")
        d.sums_ready = sem("d_sums_ready")
        d.means_ready = sem("d_means_ready")
        d.means_stored = sem("d_means_stored")
        d.att_inputs_loaded = sem("d_att_inputs_loaded")
        d.degree_steps = sem("d_degree_steps")
        d.energy_ready = sem("d_energy_ready")
        d.exp_ready = sem("d_exp_ready")
        d.final_inputs_loaded = sem("d_final_inputs_loaded")
        d.final_norm_steps = sem("d_final_norm_steps")
        d.final_sqrt_steps = sem("d_final_sqrt_steps")
        d.output_stored = sem("d_output_stored")
        d.output_ready = sem("d_output_ready")
        d.hard_transposed = sem("d_hard_transposed")
        d.hardT_copied = sem("d_hardT_copied")
        d.hard_ready = sem("d_hard_ready")
        d.head_loaded = sem("d_head_loaded")
        d.linear_ready = sem("d_linear_ready")
        d.norm_steps = sem("d_norm_steps")
        d.att_mask_steps = sem("d_att_mask_steps")
        d.mask_transposed = sem("d_mask_transposed")
        d.maskT_copied = sem("d_maskT_copied")
        d.mask_ready = sem("d_mask_ready")
        d.att_sums_ready = sem("d_att_sums_ready")
        d.att_ready = sem("d_att_ready")
        d.att_stored = sem("d_att_stored")
        d.qkv_ready = sem("d_qkv_ready")
        d.qkv_copied = sem("d_qkv_copied")
        d.score_chunk_ready = sem("d_score_chunk_ready")
        d.score_chunk_copied = sem("d_score_chunk_copied")
        d.softmax_steps = sem("d_softmax_steps")
        d.sqrt_steps = sem("d_sqrt_steps")
        d.tables_stored = sem("d_tables_stored")
        d.x1_ready = sem("d_x1_ready")
        d.x1_transposed = sem("d_x1_transposed")
        d.x1T_copied = sem("d_x1T_copied")
        d.inputs_loaded = sem("d_inputs_loaded")
        d.inputs_transposed = sem("d_inputs_transposed")
        d.inputsT_copied = sem("d_inputsT_copied")
        d.x_loaded = sem("d_x_loaded")
        fast, slow = sparse_layer2(nc, g, dr, m), dense_layers(nc, g, dr, d)

        with nc.Block() as block:
            def either(eng, part):
                over = eng.value_load(g.flag[0:1, 0:1], min_val=0, max_val=3)
                with eng.If(over > 0):
                    if slow[part] is not None:
                        slow[part](eng)
                with eng.Else():
                    fast[part](eng)

            @block.sync
            def _(sp):
                either(sp, "sync")

            @block.gpsimd
            def _(pool):
                either(pool, "gpsimd")

            @block.scalar
            def _(act):
                either(act, "scalar")

            @block.tensor
            def _(pe):
                either(pe, "tensor")

            @block.vector
            def _(dve):
                either(dve, "vector")


_INS = ['x', 'adj', 'L0_gnn_W_self', 'L0_gnn_b_self', 'L0_gnn_W_nb', 'L0_gnn_b_nb', 'L0_gnn_W_comb', 'L0_gnn_b_comb',
        'L1_gnn_WQ', 'L1_gnn_WK', 'L1_gnn_WV', 'L1_gnn_we', 'L1_gnn_be']


def kernel(**inputs):
    import numpy as _np
    import concourse.bacc as _bacc
    from concourse import mybir as _mybir
    from concourse.bass_utils import run_bass_kernel_spmd as _run

    nc = _bacc.Bacc("TRN2", target_bir_lowering=False, num_devices=1)
    arrays, args = {}, []
    for name in _INS:
        a = _np.ascontiguousarray(inputs[name])
        arrays[f"in_{name}"] = a
        args.append(nc.dram_tensor(f"in_{name}", a.shape, _mybir.dt.from_np(a.dtype), kind="ExternalInput").ap())
    args.append(nc.dram_tensor("out_0", (N, D), _mybir.dt.float32, kind="ExternalOutput").ap())
    gnn_kernel(nc, *args)
    return _run(nc, [arrays], core_ids=[0]).results[0]["out_0"]
```
